# Optimizing a Trainium2 kernel written in Bass

```python
import numpy as np
import jax
import jax.numpy as jnp

def _softmax(x, axis=-1):
    return jax.nn.softmax(x, axis=axis)

def _gelu(x):
    return jax.nn.gelu(x, approximate=True)

def _silu(x):
    return jax.nn.silu(x)

def _sigmoid(x):
    return jax.nn.sigmoid(x)

def _layernorm(x, axis=-1, eps=1e-05):
    m = jnp.mean(x, axis=axis, keepdims=True)
    v = jnp.var(x, axis=axis, keepdims=True)
    return (x - m) / jnp.sqrt(v + eps)

def _scatter_add(tgt, idx, src, axis=0):
    return tgt.at[idx].add(src)

def _segment_sum(src, seg, n):
    return jax.ops.segment_sum(src, seg, n)
kernel_name = 'mk_recurrent_d2_jaxref_r8_e7702d'

def setup_inputs(seed: int=0):
    np.random.seed(seed)
    _w = jnp.asarray

    def _L0_attn_setup():
        import jax, jax.numpy as jnp
        import numpy as np
        BH = 32
        BW = 32
        key = jax.random.key(seed)
        k1, k2, k3, k4 = jax.random.split(key, 4)
        B, S, K, N = (2, 256, 512, 512)
        data = jax.random.normal(k1, (B, S, K), dtype=jnp.float32)
        weight = jax.random.normal(k2, (N, K), dtype=jnp.float32) * 0.02
        bias = jax.random.normal(k3, (N,), dtype=jnp.float32) * 0.02
        Nb, Kb = (N // BH, K // BW)
        block_on = jax.random.uniform(k4, (Nb, Kb)) < 0.3
        mask = jnp.repeat(jnp.repeat(block_on, BH, axis=0), BW, axis=1).astype(jnp.int32)
        return {'data': data, 'mask': mask, 'weight': weight, 'bias': bias}
    _L0_attn_in = _L0_attn_setup()

    def _L0_ffn_setup():
        import jax, jax.numpy as jnp
        import numpy as np
        DIM = 512
        INTER = 1792
        SPARSITY = 32
        RANK = 16
        key = jax.random.key(seed)
        ks = jax.random.split(key, 5)
        B, T = (32, 1)
        x = jax.random.normal(ks[0], (B, T, DIM), dtype=jnp.float32)
        c1_w = jax.random.normal(ks[1], (RANK, DIM), dtype=jnp.float32) * (1.0 / np.sqrt(DIM))
        c2_w = jax.random.normal(ks[2], (INTER, RANK), dtype=jnp.float32) * (1.0 / np.sqrt(RANK))
        w1 = jax.random.normal(ks[3], (INTER, DIM), dtype=jnp.float32) * (1.0 / np.sqrt(DIM))
        w2t = jax.random.normal(ks[4], (INTER, DIM), dtype=jnp.float32) * (1.0 / np.sqrt(INTER))
        return {'x': x, 'c1_w': c1_w, 'c2_w': c2_w, 'w1': w1, 'w2t': w2t}
    _L0_ffn_in = _L0_ffn_setup()

    def _L1_attn_setup():
        import jax, jax.numpy as jnp
        import numpy as np
        H = 512
        D = H // 4
        key = jax.random.key(seed)
        k1, k2, k3, k4, k5 = jax.random.split(key, 5)
        x = jax.random.normal(k1, (4, 512, H), dtype=jnp.float32)
        s_in = 1.0 / np.sqrt(H)
        Wqkv = jax.random.normal(k2, (H, 3 * D), dtype=jnp.float32) * s_in
        bqkv = jax.random.normal(k3, (3 * D,), dtype=jnp.float32) * 0.01
        Wo = jax.random.normal(k4, (D, H), dtype=jnp.float32) * (1.0 / np.sqrt(D))
        bo = jax.random.normal(k5, (H,), dtype=jnp.float32) * 0.01
        return {'x': x, 'Wqkv': Wqkv, 'bqkv': bqkv, 'Wo': Wo, 'bo': bo}
    _L1_attn_in = _L1_attn_setup()

    def _L1_ffn_setup():
        import jax, jax.numpy as jnp
        import numpy as np
        TOP_K = 2
        SCALING = 32.0 / 64.0
        key = jax.random.key(seed)
        ks = jax.random.split(key, 6)
        Bsz, S, Din, Dout, R, E = (4, 256, 512, 512, 64, 16)
        x = jax.random.normal(ks[0], (Bsz, S, Din), dtype=jnp.float32)
        base_w = jax.random.normal(ks[1], (Dout, Din), dtype=jnp.float32) * 0.02
        base_b = jax.random.normal(ks[2], (Dout,), dtype=jnp.float32) * 0.02
        A = jax.random.normal(ks[3], (R, Din), dtype=jnp.float32) * (1.0 / np.sqrt(Din))
        B = jax.random.normal(ks[4], (E, Dout, R), dtype=jnp.float32) * 0.02
        router_w = jax.random.normal(ks[5], (E, Din), dtype=jnp.float32) * 0.02
        return {'x': x, 'base_w': base_w, 'base_b': base_b, 'A': A, 'B': B, 'router_w': router_w}
    _L1_ffn_in = _L1_ffn_setup()
    _d = {'L0_attn_data': _L0_attn_in['data'], 'L0_attn_mask': _L0_attn_in['mask'], 'L0_attn_weight': _L0_attn_in['weight'], 'L0_attn_bias': _L0_attn_in['bias'], 'L0_ffn_c1_w': _L0_ffn_in['c1_w'], 'L0_ffn_c2_w': _L0_ffn_in['c2_w'], 'L0_ffn_w1': _L0_ffn_in['w1'], 'L0_ffn_w2t': _L0_ffn_in['w2t'], 'L1_attn_Wqkv': _L1_attn_in['Wqkv'], 'L1_attn_bqkv': _L1_attn_in['bqkv'], 'L1_attn_Wo': _L1_attn_in['Wo'], 'L1_attn_bo': _L1_attn_in['bo'], 'L1_ffn_base_w': _L1_ffn_in['base_w'], 'L1_ffn_base_b': _L1_ffn_in['base_b'], 'L1_ffn_A': _L1_ffn_in['A'], 'L1_ffn_B': _L1_ffn_in['B'], 'L1_ffn_router_w': _L1_ffn_in['router_w']}
    _x0 = _d['L0_attn_data']
    _d['L0_attn_data'] = jax.random.normal(jax.random.fold_in(jax.random.key(seed), 1), (4, 512, 512), dtype=_x0.dtype)
    del _x0
    return _d

def reference(L0_attn_data, L0_attn_mask, L0_attn_weight, L0_attn_bias, L0_ffn_c1_w, L0_ffn_c2_w, L0_ffn_w1, L0_ffn_w2t, L1_attn_Wqkv, L1_attn_bqkv, L1_attn_Wo, L1_attn_bo, L1_ffn_base_w, L1_ffn_base_b, L1_ffn_A, L1_ffn_B, L1_ffn_router_w):

    def _L0_attn_ref(data, mask, weight, bias):
        import jax, jax.numpy as jnp
        import numpy as np
        BH = 32
        BW = 32
        N, K = weight.shape
        Nb, Kb = (N // BH, K // BW)
        bm = mask.reshape(Nb, BH, Kb, BW).sum(axis=(1, 3)) > 0
        wb = weight.reshape(Nb, BH, Kb, BW) * bm[:, None, :, None].astype(weight.dtype)
        w = wb.reshape(N, K)
        out = jnp.einsum('bsk,nk->bsn', data, w) + bias
        return out

    def _L0_ffn_ref(x, c1_w, c2_w, w1, w2t):
        import jax, jax.numpy as jnp
        import numpy as np
        DIM = 512
        INTER = 1792
        SPARSITY = 32
        RANK = 16
        B, T, M = x.shape
        xf = x.reshape(B * T, M)
        inter = xf @ c1_w.T @ c2_w.T
        n_blocks = INTER // SPARSITY
        blk = inter.reshape(B * T, n_blocks, SPARSITY)
        idx = jnp.argmax(blk, axis=-1) + jnp.arange(0, INTER, SPARSITY)
        w1_g = w1[idx]
        w2_g = w2t[idx]
        h = jax.nn.relu(jnp.einsum('bkm,bm->bk', w1_g, xf))
        out = jnp.einsum('bk,bkm->bm', h, w2_g)
        return out.reshape(B, T, M)

    def _L1_attn_ref(x, Wqkv, bqkv, Wo, bo):
        import jax, jax.numpy as jnp
        import numpy as np
        H = 512
        D = H // 4
        B, S, C = x.shape
        d = C // 4
        qkv = jnp.einsum('bsc,cf->bsf', x, Wqkv) + bqkv
        qkv = qkv.reshape(B, S, 3, d)
        q, k, v = (qkv[:, :, 0], qkv[:, :, 1], qkv[:, :, 2])
        scale = 1.0 / jnp.sqrt(jnp.float32(d)).astype(x.dtype)
        attn = jnp.einsum('bqd,bkd->bqk', q, k) * scale
        attn = jax.nn.softmax(attn, axis=-1)
        out = jnp.einsum('bqk,bkd->bqd', attn, v)
        return jnp.einsum('bqd,dc->bqc', out, Wo) + bo

    def _L1_ffn_ref(x, base_w, base_b, A, B, router_w):
        import jax, jax.numpy as jnp
        import numpy as np
        TOP_K = 2
        SCALING = 32.0 / 64.0
        base_out = jnp.einsum('bsi,oi->bso', x, base_w) + base_b
        res_hidden = jnp.einsum('bsi,ri->bsr', x, A)
        logits = jnp.einsum('bsi,ei->bse', x, router_w)
        probs = jax.nn.softmax(logits, axis=-1)
        topw, topi = jax.lax.top_k(probs, TOP_K)
        topw = topw / (jnp.sum(topw, axis=-1, keepdims=True) + 1e-06)
        num_experts = B.shape[0]
        combine = jnp.sum(jax.nn.one_hot(topi, num_experts, dtype=x.dtype) * topw[..., None], axis=-2)
        delta = jnp.einsum('bse,bsr,eor->bso', combine, res_hidden, B)
        return base_out + delta * SCALING
    x = L0_attn_data
    xn = _layernorm(x, axis=-1)
    s = _L0_attn_ref(xn, L0_attn_mask, L0_attn_weight, L0_attn_bias)
    g = _silu(_L0_ffn_ref(xn, L0_ffn_c1_w, L0_ffn_c2_w, L0_ffn_w1, L0_ffn_w2t))
    x = x + s * g
    xn = _layernorm(x, axis=-1)
    s = _L1_attn_ref(xn, L1_attn_Wqkv, L1_attn_bqkv, L1_attn_Wo, L1_attn_bo)
    g = _silu(_L1_ffn_ref(xn, L1_ffn_base_w, L1_ffn_base_b, L1_ffn_A, L1_ffn_B, L1_ffn_router_w))
    x = x + s * g
    return x

_drawn_inputs = setup_inputs


def setup_inputs(seed=0):
    import zlib

    import numpy as np

    out = dict(_drawn_inputs(seed))
    spreads = {}
    factors = {'L0_attn_weight': 3.598,
     'L0_attn_bias': 8.0,
     'L0_ffn_c1_w': 3.635,
     'L0_ffn_c2_w': 3.58,
     'L0_ffn_w1': 4.268,
     'L0_ffn_w2t': 3.537,
     'L1_attn_bqkv': 8.0,
     'L1_attn_bo': 8.0,
     'L1_ffn_base_b': 42.412,
     'L1_ffn_A': 8.0,
     'L1_ffn_B': 8.0,
     'L1_ffn_router_w': 8.0}
    for name, (base, spread) in spreads.items():
        noise = np.random.default_rng([zlib.crc32(name.encode()), seed]).standard_normal(out[name].shape)
        drawn = base * np.exp(spread * noise) if base else spread * noise
        out[name] = jnp.asarray(drawn.astype(out[name].dtype))
    for name, factor in factors.items():
        out[name] = (out[name] * factor).astype(out[name].dtype)
    return out
```

```python
from contextlib import ExitStack

import concourse.bass as bass
from concourse import mybir

P = 128
BANK = 512

ALU = mybir.AluOpType
ACT = mybir.ActivationFunctionType
AX = mybir.AxisListType
F32 = mybir.dt.float32
F32R = mybir.dt.float32r
BF16 = mybir.dt.bfloat16
I32 = mybir.dt.int32


def block_mask_ffn_then_attention_lora_kernel(
    nc: bass.Bass,
    x_in: bass.AP,
    mask: bass.AP,
    w_s0: bass.AP,
    b_s0: bass.AP,
    c1_w: bass.AP,
    c2_w: bass.AP,
    w1: bass.AP,
    w2: bass.AP,
    wqkv: bass.AP,
    bqkv: bass.AP,
    wo: bass.AP,
    bo: bass.AP,
    base_w: bass.AP,
    base_b: bass.AP,
    lora_a: bass.AP,
    lora_b: bass.AP,
    router_w: bass.AP,
    out: bass.AP,
):
    B, S, D = x_in.shape
    INTER = w1.shape[0]
    RANK = c1_w.shape[0]
    DH = wo.shape[0]
    E, _, R = lora_b.shape
    SEG = 32
    KD = D // P
    TT = S // P
    IT = INTER // P
    CH = B
    PIECES = -(-INTER // BANK)
    PW = [min(BANK, INTER - p * BANK) for p in range(PIECES)]
    KE = E * R // P
    EPT = P // R
    SCALING = 32.0 / 64.0
    EPS = 1e-5
    QK_SCALE = float(DH) ** -0.5
    Q = P // 4
    assert D == BANK and S == BANK and DH == P and RANK <= Q and E <= Q and R * 2 == P and IT % 2 == 0

    x_rows = x_in.rearrange("b (t p) d -> b p t d", p=P)
    out_rows = out.rearrange("b (t p) d -> b p t d", p=P)
    mid = nc.dram_tensor("mid_state", (B, S, D), F32, kind="Internal").ap()
    mid_rows = mid.rearrange("b (t p) d -> b p t d", p=P)

    ctx = ExitStack()
    with ctx:
        def sb(name, shape, dt=F32, into=ctx):
            return into.enter_context(nc.sbuf_tensor(name, shape, dt))

        def sem(name):
            return ctx.enter_context(nc.semaphore(name))

        ident = sb("ident", [P, P])
        ident_bf = sb("ident_bf", [P, P], BF16)
        restart = sb("restart", [P, BANK], BF16)
        restart_e = sb("restart_e", [P, TT * E])
        neg_half = sb("neg_half", [P, TT])
        x_tile = sb("x_tile", [P, TT, D])
        x_res = sb("x_res", [P, TT, D])
        s_tile = sb("s_tile", [P, TT, D])
        g_tile = sb("g_tile", [P, TT, D])
        xT_hi = sb("xT_hi", [P, KD, S], F32R)
        xT_lo = sb("xT_lo", [P, KD, S], F32R)
        bn = sb("bn", [P, TT, 6])
        mean_var = sb("mean_var", [P, TT, 2])
        rstd = sb("rstd", [P, TT])
        eps = sb("eps", [P, TT])
        bias_a = sb("bias_a", [P, D])
        bias_b = sb("bias_b", [P, D])

        banks = [ctx.enter_context(nc.psum_tensor(f"bank{i}", [P, BANK], F32)) for i in range(8)]

        consts_gp = sem("consts_gp")
        consts_dve = sem("consts_dve")
        ld_x = sem("ld_x")
        ld_res = sem("ld_res")
        st_rows = sem("st_rows")
        ld_small = sem("ld_small")
        ld_mask = sem("ld_mask")
        ld_ws0 = sem("ld_ws0")
        ld_w1 = [sem(f"ld_w1_{i}") for i in range(4)]
        ld_w2 = [sem(f"ld_w2_{i}") for i in range(2)]
        ld_l1 = sem("ld_l1")
        ld_l1_bias = sem("ld_l1_bias")
        w_tr = sem("w_tr")
        w_hi = sem("w_hi")
        w_lo = sem("w_lo")
        w2_hi = sem("w2_hi")
        w2_lo = sem("w2_lo")
        mask_sum = sem("mask_sum")
        mask_cnt = sem("mask_cnt")
        mask_on = sem("mask_on")
        ws0_masked = sem("ws0_masked")
        c2_wide = sem("c2_wide")
        half_bias = sem("half_bias")
        stats_in = sem("stats_in")
        stats = sem("stats")
        rstd_step = sem("rstd_step")
        xn_ready = sem("xn_ready")
        xT_tr = sem("xT_tr")
        xT_hi_done = sem("xT_hi_done")
        xT_done = sem("xT_done")
        t_done = sem("t_done")
        t_hi = sem("t_hi")
        t_split = sem("t_split")
        s0_done = sem("s0_done")
        s0_read = sem("s0_read")
        s_biased = sem("s_biased")
        sel_done = sem("sel_done")
        seg_max = sem("seg_max")
        sel_eq = sem("sel_eq")
        sel_count = sem("sel_count")
        first_tr = sem("first_tr")
        up_done = sem("up_done")
        relu_done = sem("relu_done")
        h_masked = sem("h_masked")
        h_hi_done = sem("h_hi_done")
        h_split = sem("h_split")
        down_done = sem("down_done")
        tanh_done = sem("tanh_done")
        silu_done = sem("silu_done")
        rows_done = sem("rows_done")

        s_free = sem("s_free")
        g_free = sem("g_free")
        w_direct_hi = sem("w_direct_hi")
        w_direct_lo = sem("w_direct_lo")
        pick_ready = sem("pick_ready")
        route_in = sem("route_in")
        route_step = sem("route_step")
        route_exp = sem("route_exp")
        comb_ready = sem("comb_ready")
        comb_tr = sem("comb_tr")
        comb_hi = sem("comb_hi")
        comb_split = sem("comb_split")
        proj_done = sem("proj_done")
        proj_read = sem("proj_read")
        qk_hi_done = sem("qk_hi_done")
        qk_split = sem("qk_split")
        v_tr = sem("v_tr")
        v_hi_done = sem("v_hi_done")
        v_split = sem("v_split")
        score_done = sem("score_done")
        score_max = sem("score_max")
        neg_max = sem("neg_max")
        exp_done = sem("exp_done")
        inv_step = sem("inv_step")
        p_tr = sem("p_tr")
        p_hi_done = sem("p_hi_done")
        p_split = sem("p_split")
        pv_done = sem("pv_done")
        a_hi_done = sem("a_hi_done")
        a_split = sem("a_split")
        spread_done = sem("spread_done")
        prod_done = sem("prod_done")
        prod_hi_done = sem("prod_hi_done")
        prod_split = sem("prod_split")
        y_done = sem("y_done")
        y_read = sem("y_read")
        o_done = sem("o_done")
        o_read = sem("o_read")
        st_out = sem("st_out")

        def transpose_rows(pe, g, tt):
            pe.wait_ge(xn_ready, g * TT + tt + 1)
            for k in range(KD):
                last = nc.tensor.transpose(banks[tt % 2][:, k * P:(k + 1) * P],
                                           x_tile[:, tt, k * P:(k + 1) * P], ident[:])
            last.then_inc(xT_tr, 1)

        def rows_hi(act, g, tt):
            act.wait_ge(xT_tr, g * TT + tt + 1)
            nc.scalar.activation(xT_hi[:, :, tt * P:(tt + 1) * P],
                                 banks[tt % 2][:].rearrange("p (k t) -> p k t", k=KD), ACT.Copy).then_inc(xT_hi_done, 1)

        def rows_lo(dve, g, tt):
            dve.wait_ge(xT_hi_done, g * TT + tt + 1)
            cols = slice(tt * P, (tt + 1) * P)
            nc.vector.tensor_tensor(xT_lo[:, :, cols], banks[tt % 2][:].rearrange("p (k t) -> p k t", k=KD),
                                    xT_hi[:, :, cols].bitcast(F32), ALU.subtract).then_inc(xT_done, 1)

        def rows_stats(dve, g, tt):
            if tt == 0:
                dve.wait_ge(ld_x, g * 16 + 16)
            nc.vector.bn_stats(bn[:, tt, :], x_tile[:, tt, :]).then_inc(stats_in, 1)

        def rows_moments():
            for tt in range(TT):
                last = nc.vector.bn_aggr(mean_var[:, tt, :], bn[:, tt, :])
            last.then_inc(stats, 1)

        def rows_rstd(gp, g):
            gp.wait_ge(stats, g + 1)
            nc.gpsimd.tensor_tensor(rstd[:], mean_var[:, :, 1], eps[:], ALU.add).then_inc(rstd_step, 1)
            gp.wait_ge(rstd_step, g * 2 + 1)
            nc.gpsimd.tensor_tensor(rstd[:], rstd[:], neg_half[:], ALU.pow).then_inc(rstd_step, 1)

        def rows_norm(dve, g):
            dve.wait_ge(rstd_step, g * 2 + 2)
            for tt in range(TT):
                nc.vector.tensor_scalar(x_tile[:, tt, :], x_tile[:, tt, :], mean_var[:, tt, 0:1],
                                        rstd[:, tt:tt + 1], ALU.subtract, ALU.mult).then_inc(xn_ready, 1)

        def gate(gp, g, tt):
            gp.wait_ge(silu_done, g * TT + tt + 1)
            nc.gpsimd.tensor_tensor(g_tile[:, tt, :], g_tile[:, tt, :], s_tile[:, tt, :], ALU.mult).then_inc(s_free, 1)
            if tt == 0:
                gp.wait_ge(ld_res, g * 16 + 16)
            gp.wait_ge(s_free, g * TT + tt + 1 + TT)
            nc.gpsimd.tensor_tensor(g_tile[:, tt, :], g_tile[:, tt, :], x_res[:, tt, :], ALU.add).then_inc(rows_done, 1)

        with ExitStack() as l0:
            w1T_hi = sb("w1T_hi", [P, KD, INTER], F32R, l0)
            w1T_lo = sb("w1T_lo", [P, KD, INTER], F32R, l0)
            w2_hi_t = sb("w2_hi_t", [P, IT, D], F32R, l0)
            w2_lo_t = sb("w2_lo_t", [P, IT, D], F32R, l0)
            ws_hi = sb("ws_hi", [P, KD, D], F32R, l0)
            ws_lo = sb("ws_lo", [P, KD, D], F32R, l0)
            c1_hi = sb("c1_hi", [P, KD, P], F32R, l0)
            c1_lo = sb("c1_lo", [P, KD, P], F32R, l0)
            c2_stack = sb("c2_stack", [P, INTER], F32R, l0)
            t_stack = sb("t_stack", [P, S], F32R, l0)
            eq = sb("eq", [P, BANK], BF16, l0)
            counts = sb("counts", [P, 2, TT, BANK], BF16, l0)
            seg_top = sb("seg_top", [P, BANK // SEG], F32, l0)
            h = sb("h", [P, S], F32, l0)
            h_hi = sb("h_hi", [P, 2, S], F32R, l0)
            h_lo = sb("h_lo", [P, 2, S], F32R, l0)
            c1_nat = sb("c1_nat", [RANK, D], F32, l0)
            seg_ones = h[:, 0:P]
            row_cnt = h[:, P:2 * P]
            on = h[:, 2 * P:3 * P]

            ws_nat = s_tile
            mask_nat = g_tile[:].bitcast(I32)
            c2_nat = x_res[:, 0, 0:IT * RANK].rearrange("p (i r) -> p i r", r=RANK)
            c2_rep = counts[:].bitcast(F32).rearrange("p a t n -> p (a t n)")[:, 0:IT * P]
            c2_rep_q = c2_rep.rearrange("p (i q r) -> p i q r", q=4, r=Q)

            up = [banks[0], banks[1]]
            acc = [banks[2 + tt] for tt in range(TT)]
            sel = banks[6]
            first = banks[7][:].bitcast(BF16)[:, 0:S]

            ring = [banks[i] for i in range(2, 7)]
            items = [("c1", 0)] + [("c2", i) for i in range(0, IT, 4)] + [("ws", k) for k in range(KD)]
            items += [("w1", i) for i in range(IT)]
            W1_AT = items.index(("w1", 0))
            NW = len(items)

            block = l0.enter_context(nc.Block())

            @block.sync
            def _(sp):
                sp.dma_start(x_tile[:], x_rows[0]).then_inc(ld_x, 16)
                sp.dma_start(c1_nat[:], c1_w).then_inc(ld_small, 16)
                sp.dma_start(c2_nat, c2_w.rearrange("(i p) r -> p i r", p=P)).then_inc(ld_small, 16)
                sp.dma_start(bias_a[:], b_s0.rearrange("(a n) -> a n", a=1).to_broadcast([P, D])).then_inc(ld_small, 16)
                sp.dma_start(mask_nat, mask.rearrange("(t p) k -> p t k", p=P)).then_inc(ld_mask, 16)
                sp.dma_start(ws_nat[:], w_s0.rearrange("(t p) k -> p t k", p=P)).then_inc(ld_ws0, 16)
                sp.wait_ge(mask_sum, 1)
                sp.wait_ge(c2_wide, 1)
                for i in range(IT):
                    if i >= 4:
                        sp.wait_ge(w_tr, W1_AT + i - 4 + 1)
                    sp.dma_start(g_tile[:, i % 4, :], w1[i * P:(i + 1) * P, :]).then_inc(ld_w1[i % 4], 16)
                    if i >= 2:
                        sp.wait_ge(w2_lo, i - 2 + 1)
                    sp.dma_start(x_res[:, 2 + i % 2, :], w2[i * P:(i + 1) * P, :]).then_inc(ld_w2[i % 2], 16)
                sp.wait_ge(w2_lo, IT)
                sp.sem_inc(g_free, 1)

                def chunk(c, source):
                    sp.dma_start(x_res[:], x_rows[c]).then_inc(ld_res, 16)
                    sp.wait_ge(xT_tr, c * TT + TT)
                    sp.dma_start(x_tile[:], source).then_inc(ld_x, 16)
                    for tt in range(TT):
                        sp.wait_ge(rows_done, c * TT + tt + 1)
                        sp.dma_start(mid_rows[c][:, tt, :], g_tile[:, tt, :]).then_inc(st_rows, 16)
                    sp.wait_ge(st_rows, c * TT * 16 + TT * 16)
                    sp.sem_inc(g_free, 1)

                with sp.Fori(0, CH - 1) as c:
                    chunk(c, x_rows[c + 1])
                chunk(CH - 1, mid_rows[0])

            @block.gpsimd
            def _(gp):
                gp.memset(ident[:], 0.0).then_inc(consts_gp, 1)
                gp.memset(ident_bf[:], 0.0).then_inc(consts_gp, 1)
                gp.memset(neg_half[:], -0.5).then_inc(consts_gp, 1)
                gp.memset(eps[:], EPS).then_inc(consts_gp, 1)
                gp.wait_ge(consts_gp, 4)
                for m in (ident, ident_bf):
                    gp.affine_select(out=m[:], in_=m[:], compare_op=ALU.not_equal, fill=1.0, base=0,
                                     pattern=[[-1, P]], channel_multiplier=1).then_inc(consts_gp, 1)
                gp.sem_inc(s_free, TT)
                rows_rstd(gp, 0)
                gp.wait_ge(ld_small, 48)
                nc.gpsimd.tensor_scalar(bias_a[:], bias_a[:], 0.5, 1.0, ALU.mult, ALU.mult).then_inc(half_bias, 1)
                for i in range(IT):
                    gp.wait_ge(ld_w2[i % 2], 16 * (i // 2 + 1))
                    nc.gpsimd.tensor_copy(w2_hi_t[:, i, :], x_res[:, 2 + i % 2, :]).then_inc(w2_hi, 1)
                    gp.wait_ge(w2_hi, i + 1)
                    nc.gpsimd.tensor_tensor(w2_lo_t[:, i, :], x_res[:, 2 + i % 2, :], w2_hi_t[:, i, :].bitcast(F32),
                                            ALU.subtract).then_inc(w2_lo, 1)
                gp.wait_ge(half_bias, 1)

                def chunk(c):
                    for tt in range(TT):
                        gp.wait_ge(s0_read, c * TT + tt + 1)
                        nc.gpsimd.tensor_tensor(s_tile[:, tt, :], s_tile[:, tt, :], bias_a[:], ALU.add).then_inc(s_biased, 1)
                    rows_rstd(gp, c + 1)
                    gp.wait_ge(s_biased, c * TT + TT)
                    for tt in range(TT):
                        gate(gp, c, tt)

                with gp.Fori(0, CH - 1) as c:
                    chunk(c)
                chunk(CH - 1)

            @block.scalar
            def _(act):
                for n, (kind, i) in enumerate(items):
                    act.wait_ge(w_tr, n + 1)
                    src = ring[n % 5]
                    if kind == "c1":
                        act.wait_ge(consts_dve, 4)
                        for q in range(4):
                            last = nc.scalar.activation(c1_hi[:, :, q * Q:q * Q + RANK],
                                                        src[:, 0:KD * RANK].rearrange("p (k r) -> p k r", k=KD), ACT.Copy)
                    elif kind == "c2":
                        w = min(4, IT - i) * P
                        last = nc.scalar.activation(c2_stack[:, i * P:i * P + w], src[:, 0:w], ACT.Copy)
                    elif kind == "ws":
                        last = nc.scalar.activation(ws_hi[:, i, :], src[:], ACT.Copy)
                    else:
                        last = nc.scalar.activation(w1T_hi[:, :, i * P:(i + 1) * P],
                                                    src[:].rearrange("p (k n) -> p k n", k=KD), ACT.Copy)
                    last.then_inc(w_hi, 1)
                    if kind == "c2" and i + 4 >= IT:
                        for tt in range(TT):
                            rows_hi(act, 0, tt)

                def chunk(c):
                    act.wait_ge(t_done, c + 1)
                    nc.scalar.activation(t_stack[:], sel[:], ACT.Copy).then_inc(t_hi, 1)
                    for tt in range(TT):
                        act.wait_ge(s0_done, c * TT + tt + 1)
                        act.wait_ge(s_free, c * TT + tt + 1)
                        nc.scalar.activation(s_tile[:, tt, :], up[tt % 2][:], ACT.Copy, scale=0.5).then_inc(s0_read, 1)
                    for it in range(IT):
                        act.wait_ge(up_done, c * IT + it + 1)
                        if it:
                            act.wait_ge(h_split, c * IT + it)
                        nc.scalar.activation(h[:], up[it % 2][:], ACT.Relu).then_inc(relu_done, 1)
                        act.wait_ge(h_masked, c * IT + it + 1)
                        if it >= 2:
                            act.wait_ge(down_done, c * IT + it - 1)
                        nc.scalar.activation(h_hi[:, it % 2, :], h[:], ACT.Copy).then_inc(h_hi_done, 1)
                    for tt in range(TT):
                        rows_hi(act, c + 1, tt)
                    act.wait_ge(down_done, c * IT + IT)
                    act.wait_ge(g_free, c + 1)
                    for tt in range(TT):
                        nc.scalar.activation(g_tile[:, tt, :], acc[tt][:], ACT.Tanh, scale=0.5).then_inc(tanh_done, 1)

                with act.Fori(0, CH - 1) as c:
                    chunk(c)
                chunk(CH - 1)

            @block.vector
            def _(dve):
                nc.vector.memset(restart[:], 2.0).then_inc(consts_dve, 1)
                nc.vector.memset(restart_e[:], 2.0).then_inc(consts_dve, 1)
                nc.vector.memset(c1_hi[:].bitcast(F32), 0.0).then_inc(consts_dve, 1)
                nc.vector.memset(c1_lo[:].bitcast(F32), 0.0).then_inc(consts_dve, 1)
                nc.vector.memset(c2_rep, 0.0).then_inc(consts_dve, 1)
                nc.vector.memset(seg_ones, 0.0).then_inc(consts_dve, 1)
                dve.wait_ge(consts_dve, 6)
                nc.vector.memset(restart[:].rearrange("p (s n) -> p s n", n=SEG)[:, :, 0:1], 0.0).then_inc(consts_dve, 1)
                nc.vector.memset(restart_e[:].rearrange("p (s n) -> p s n", n=E)[:, :, 0:1], 0.0).then_inc(consts_dve, 1)
                for q in range(4):
                    nc.vector.memset(h[q * Q:(q + 1) * Q, q * Q:(q + 1) * Q], 1.0).then_inc(consts_dve, 1)
                dve.wait_ge(ld_small, 48)
                for q in range(4):
                    last = nc.vector.tensor_copy(c2_rep_q[:, :, q, 0:RANK], c2_nat)
                last.then_inc(c2_wide, 1)
                dve.wait_ge(ld_mask, 16)
                with nc.allow_low_precision(reason="counts of ones"):
                    nc.vector.reduce_sum(row_cnt[:, 0:TT * D // SEG].rearrange("p (t n) -> p t n", t=TT),
                                         mask_nat.rearrange("p t (n s) -> p t n s", s=SEG), AX.X).then_inc(mask_sum, 1)
                for tt in range(TT):
                    rows_stats(dve, 0, tt)
                dve.wait_ge(stats_in, TT)
                rows_moments()
                dve.wait_ge(mask_cnt, 1)
                nc.vector.tensor_scalar(on[:, 0:TT * D // SEG], banks[0][:, 0:TT * D // SEG], 0.0, None,
                                        ALU.is_gt).then_inc(mask_on, 1)
                dve.wait_ge(mask_on, 1)
                dve.wait_ge(ld_ws0, 16)
                for t in range(TT):
                    nc.vector.tensor_tensor(ws_nat[:, t, :].rearrange("p (n s) -> p n s", s=SEG),
                                            ws_nat[:, t, :].rearrange("p (n s) -> p n s", s=SEG),
                                            on[:, t * D // SEG:(t + 1) * D // SEG][:, :, None].to_broadcast([P, D // SEG, SEG]),
                                            ALU.mult).then_inc(ws0_masked, 1)
                rows_norm(dve, 0)
                for n, (kind, i) in enumerate(items):
                    dve.wait_ge(w_hi, n + 1)
                    src = ring[n % 5]
                    if kind == "c1":
                        for q in range(4):
                            last = nc.vector.tensor_tensor(c1_lo[:, :, q * Q:q * Q + RANK],
                                                           src[:, 0:KD * RANK].rearrange("p (k r) -> p k r", k=KD),
                                                           c1_hi[:, :, q * Q:q * Q + RANK].bitcast(F32), ALU.subtract)
                    elif kind == "c2":
                        w = min(4, IT - i) * P
                        for q in (1, 3):
                            part = c2_stack[q * Q:(q + 1) * Q, i * P:i * P + w]
                            last = nc.vector.tensor_tensor(part, src[q * Q:(q + 1) * Q, 0:w], part.bitcast(F32), ALU.subtract)
                    elif kind == "ws":
                        last = nc.vector.tensor_tensor(ws_lo[:, i, :], src[:], ws_hi[:, i, :].bitcast(F32), ALU.subtract)
                    else:
                        cols = slice(i * P, (i + 1) * P)
                        last = nc.vector.tensor_tensor(w1T_lo[:, :, cols], src[:].rearrange("p (k n) -> p k n", k=KD),
                                                       w1T_hi[:, :, cols].bitcast(F32), ALU.subtract)
                    last.then_inc(w_lo, 1)
                    if kind == "c2" and i + 4 >= IT:
                        for tt in range(TT):
                            rows_lo(dve, 0, tt)

                def select(c, p, tt):
                    n = p * TT + tt
                    segs = PW[p] // SEG
                    got = sel[:, 0:PW[p]].rearrange("p (s n) -> p s n", n=SEG)
                    dve.wait_ge(sel_done, c * PIECES * TT + n + 1)
                    nc.vector.reduce_max(seg_top[:, 0:segs], got, AX.X).then_inc(seg_max, 1)
                    dve.wait_ge(seg_max, c * PIECES * TT + n + 1)
                    nc.vector.tensor_tensor(eq[:, 0:PW[p]].rearrange("p (s n) -> p s n", n=SEG), got,
                                            seg_top[:, 0:segs, None].to_broadcast([P, segs, SEG]),
                                            ALU.is_equal).then_inc(sel_eq, 1)
                    dve.wait_ge(sel_eq, c * PIECES * TT + n + 1)
                    if tt == 0 and p >= 2:
                        dve.wait_ge(first_tr, c * IT + 4 * (p - 1))
                    nc.vector.tensor_tensor_scan(counts[:, p % 2, tt, 0:PW[p]], restart[:, 0:PW[p]], eq[:, 0:PW[p]], 0.0,
                                                 ALU.mult, ALU.add).then_inc(sel_count, 1)

                def chunk(c):
                    dve.wait_ge(t_hi, c + 1)
                    nc.vector.tensor_tensor(t_stack[2 * Q:P, :], sel[2 * Q:P, :], t_stack[2 * Q:P, :].bitcast(F32),
                                            ALU.subtract).then_inc(t_split, 1)
                    for tt in range(TT):
                        select(c, 0, tt)
                    for it in range(IT):
                        if it // 4 + 1 < PIECES:
                            select(c, it // 4 + 1, it % 4)
                        dve.wait_ge(relu_done, c * IT + it + 1)
                        dve.wait_ge(first_tr, c * IT + it + 1)
                        nc.vector.scalar_tensor_tensor(h[:], first, 1.0, h[:], ALU.is_equal, ALU.mult).then_inc(h_masked, 1)
                        if IT - 8 <= it < IT - 4:
                            rows_stats(dve, c + 1, it - (IT - 8))
                        if it == IT - 4:
                            dve.wait_ge(stats_in, (c + 1) * TT + TT)
                        dve.wait_ge(h_hi_done, c * IT + it + 1)
                        nc.vector.tensor_tensor(h_lo[:, it % 2, :], h[:], h_hi[:, it % 2, :].bitcast(F32),
                                                ALU.subtract).then_inc(h_split, 1)
                        if it == IT - 4:
                            rows_moments()
                        if it == IT - 2:
                            rows_norm(dve, c + 1)
                    for tt in range(TT):
                        rows_lo(dve, c + 1, tt)
                    for tt in range(TT):
                        dve.wait_ge(tanh_done, c * TT + tt + 1)
                        nc.vector.scalar_tensor_tensor(g_tile[:, tt, :], g_tile[:, tt, :], 1.0, acc[tt][:],
                                                       ALU.add, ALU.mult).then_inc(silu_done, 1)

                dve.wait_ge(consts_dve, 12)
                with dve.Fori(0, CH - 1) as c:
                    chunk(c)
                chunk(CH - 1)

            @block.tensor
            def _(pe):
                pe.wait_ge(consts_gp, 6)
                pe.wait_ge(ld_small, 48)
                pe.wait_ge(mask_sum, 1)
                pe.wait_ge(consts_dve, 12)
                nc.tensor.matmul(banks[0][:, 0:TT * D // SEG], seg_ones, row_cnt[:, 0:TT * D // SEG],
                                 start=True, stop=True).then_inc(mask_cnt, 1)
                for n, (kind, i) in enumerate(items):
                    dst = ring[n % 5]
                    if n >= 5:
                        pe.wait_ge(w_lo, n - 5 + 1)
                    if kind == "c1":
                        for k in range(KD):
                            last = nc.tensor.transpose(dst[:, k * RANK:(k + 1) * RANK], c1_nat[:, k * P:(k + 1) * P],
                                                       ident[0:RANK, 0:RANK])
                    elif kind == "c2":
                        pe.wait_ge(c2_wide, 1)
                        for j in range(i, min(i + 4, IT)):
                            last = nc.tensor.transpose(dst[:, (j - i) * P:(j - i + 1) * P], c2_rep[:, j * P:(j + 1) * P], ident[:])
                    elif kind == "ws":
                        pe.wait_ge(ws0_masked, TT)
                        for t in range(TT):
                            last = nc.tensor.transpose(dst[:, t * P:(t + 1) * P], ws_nat[:, t, i * P:(i + 1) * P], ident[:])
                    else:
                        pe.wait_ge(ld_w1[i % 4], 16 * (i // 4 + 1))
                        for k in range(KD):
                            last = nc.tensor.transpose(dst[:, k * P:(k + 1) * P], g_tile[:, i % 4, k * P:(k + 1) * P], ident[:])
                    last.then_inc(w_tr, 1)
                    if kind == "c2" and i + 4 >= IT:
                        pe.wait_ge(mask_on, 1)
                        for tt in range(TT):
                            if tt >= 2:
                                pe.wait_ge(xT_done, tt - 1)
                            transpose_rows(pe, 0, tt)
                pe.wait_ge(w_lo, NW)
                pe.wait_ge(w2_lo, IT)

                def rank_product():
                    n = 0
                    for k in range(KD):
                        for a, b in ((c1_hi, xT_hi), (c1_lo, xT_hi), (c1_hi, xT_lo)):
                            last = nc.tensor.matmul(sel[:], a[:, k, :], b[:, k, :], start=(n == 0), stop=(n == 3 * KD - 1))
                            n += 1
                    last.then_inc(t_done, 1)

                def s_product(c, tt):
                    if tt >= 2:
                        pe.wait_ge(s0_read, c * TT + tt - 1)
                    n = 0
                    for k in range(KD):
                        cols = slice(tt * P, (tt + 1) * P)
                        for a, b in ((xT_hi, ws_hi), (xT_hi, ws_lo), (xT_lo, ws_hi)):
                            last = nc.tensor.matmul(up[tt % 2][:], a[:, k, cols], b[:, k, :], start=(n == 0), stop=(n == 3 * KD - 1))
                            n += 1
                    last.then_inc(s0_done, 1)

                def select(c, p, tt):
                    if p == 0 and tt == 0:
                        pe.wait_ge(t_split, c + 1)
                    else:
                        pe.wait_ge(sel_eq, c * PIECES * TT + p * TT + tt)
                    nc.tensor.matmul(sel[:, 0:PW[p]], t_stack[:, tt * P:(tt + 1) * P],
                                     c2_stack[:, p * BANK:p * BANK + PW[p]], start=True, stop=True).then_inc(sel_done, 1)

                def up_product(c, it):
                    if it < 2:
                        pe.wait_ge(s0_read, c * TT + TT - 1 + it)
                    else:
                        pe.wait_ge(relu_done, c * IT + it - 1)
                    n = 0
                    rows = slice(it * P, (it + 1) * P)
                    for k in range(KD):
                        for a, b in ((w1T_hi, xT_hi), (w1T_lo, xT_hi), (w1T_hi, xT_lo)):
                            last = nc.tensor.matmul(up[it % 2][:], a[:, k, rows], b[:, k, :], start=(n == 0), stop=(n == 3 * KD - 1))
                            n += 1
                    last.then_inc(up_done, 1)

                def transpose_counts(c, it):
                    pe.wait_ge(sel_count, c * PIECES * TT + (it // 4 + 1) * TT)
                    if it:
                        pe.wait_ge(h_masked, c * IT + it)
                    for tt in range(TT):
                        last = nc.tensor.transpose(first[:, tt * P:(tt + 1) * P],
                                                   counts[:, it // 4 % 2, tt, it % 4 * P:(it % 4 + 1) * P], ident_bf[:])
                    last.then_inc(first_tr, 1)

                def down_product(it, tts):
                    for tt in tts:
                        cols = slice(tt * P, (tt + 1) * P)
                        for n, (a, b) in enumerate(((h_hi, w2_hi_t), (h_hi, w2_lo_t), (h_lo, w2_hi_t))):
                            last = nc.tensor.matmul(acc[tt][:], a[:, it % 2, cols], b[:, it, :],
                                                    start=(it == 0 and n == 0), stop=(it == IT - 1 and n == 2))
                    return last

                def chunk(c):
                    pe.wait_ge(xT_done, c * TT + TT)
                    rank_product()
                    s_product(c, 0)
                    s_product(c, 1)
                    for tt in range(2):
                        select(c, 0, tt)
                        s_product(c, 2 + tt)
                    select(c, 0, 2)
                    up_product(c, 0)
                    select(c, 0, 3)
                    for it in range(1, IT + 1):
                        if it < IT:
                            up_product(c, it)
                            if (it - 1) // 4 + 1 < PIECES:
                                select(c, (it - 1) // 4 + 1, (it - 1) % 4)
                        else:
                            pe.wait_ge(relu_done, c * IT + IT - 1)
                            transpose_rows(pe, c + 1, 0)
                        transpose_counts(c, it - 1)
                        if it >= 2:
                            pe.wait_ge(h_split, c * IT + it - 1)
                            down_product(it - 2, range(TT)).then_inc(down_done, 1)
                    pe.wait_ge(relu_done, c * IT + IT)
                    transpose_rows(pe, c + 1, 1)
                    pe.wait_ge(xT_done, (c + 1) * TT + 1)
                    transpose_rows(pe, c + 1, 2)
                    pe.wait_ge(h_split, c * IT + IT)
                    down_product(IT - 1, range(0, 2))
                    pe.wait_ge(xT_done, (c + 1) * TT + 2)
                    transpose_rows(pe, c + 1, 3)
                    down_product(IT - 1, range(2, TT)).then_inc(down_done, 1)

                with pe.Fori(0, CH - 1) as c:
                    chunk(c)
                chunk(CH - 1)

        with ExitStack() as l1:
            wqkv_hi = sb("wqkv_hi", [P, KD, 3 * DH], F32R, l1)
            wqkv_lo = sb("wqkv_lo", [P, KD, 3 * DH], F32R, l1)
            wo_hi = sb("wo_hi", [P, D], F32R, l1)
            wo_lo = sb("wo_lo", [P, D], F32R, l1)
            base_hi = sb("base_hi", [P, KD, D], F32R, l1)
            base_lo = sb("base_lo", [P, KD, D], F32R, l1)
            b_hi = sb("b_hi", [P, KE, D], F32R, l1)
            b_lo = sb("b_lo", [P, KE, D], F32R, l1)
            a_hi = sb("a_hi", [P, KD, EPT * R], F32R, l1)
            a_lo = sb("a_lo", [P, KD, EPT * R], F32R, l1)
            router = sb("router", [P, KD, 2 * E], F32R, l1)
            pick = sb("pick", [2 * Q, KE, P], F32R, l1)
            bqkv_col = sb("bqkv_col", [P, 3], F32, l1)
            qkv = sb("qkv", [P, 3, S], F32, l1)
            qk_hi = sb("qk_hi", [P, 2, S], F32R, l1)
            qk_lo = sb("qk_lo", [P, 2, S], F32R, l1)
            v_hi = sb("v_hi", [P, TT, DH], F32R, l1)
            v_lo = sb("v_lo", [P, TT, DH], F32R, l1)
            probs = sb("probs", [P, TT, S], F32, l1)
            pT_hi = sb("pT_hi", [P, TT, S], F32R, l1)
            pT_lo = sb("pT_lo", [P, TT, S], F32R, l1)
            at_hi = sb("at_hi", [P, S], F32R, l1)
            at_lo = sb("at_lo", [P, S], F32R, l1)
            res = sb("res", [P, S], F32, l1)
            prod = sb("prod", [P, 2, S], F32, l1)
            comb = sb("comb", [P, TT, 2 * Q], F32, l1)
            combT = sb("combT", [2 * Q, S], F32R, l1)
            lo_part = sb("lo_part", [P, TT, E], F32, l1)
            gate_p = sb("gate_p", [P, TT, E], F32, l1)
            is_top = sb("is_top", [P, TT, E], F32, l1)
            top_cnt = sb("top_cnt", [P, TT, E], F32, l1)
            top_w = sb("top_w", [P, 2, TT, E], F32, l1)
            row_a = sb("row_a", [P, TT], F32, l1)
            top_p = sb("top_p", [P, 2, TT], F32, l1)
            s_max = sb("s_max", [P, TT], F32, l1)
            s_neg = sb("s_neg", [P, TT], F32, l1)
            p_sum = sb("p_sum", [P, TT], F32, l1)
            p_inv = sb("p_inv", [P, TT], F32, l1)
            stage = ExitStack()
            b_nat = sb("b_nat", [P, TT, E, R], F32, stage)
            wqkv_nat = sb("wqkv_nat", [P, KD, 3 * DH], F32, stage)
            wo_nat = sb("wo_nat", [P, D], F32, stage)
            pick_f = sb("pick_f", [2 * Q, KE, P], F32, stage)
            stage.close()
            prod_hi = sb("prod_hi", [P, KE, S], F32R, l1)
            prod_lo = sb("prod_lo", [P, KE, S], F32R, l1)

            base_nat = x_res
            a_nat = s_tile[0:R, 0, :]
            router_nat = s_tile[0:E, 1, :]
            pj = [banks[0], banks[1]]
            y = [banks[2], banks[3]]
            sc = [banks[4], banks[5]]
            tr = [banks[6], banks[7]]
            ring = [banks[i] for i in range(2, 7)]
            items = [("router", 0), ("a", 0)] + [("base", k) for k in range(KD)] + [("b", k) for k in range(KE)]
            N0, N1 = NW, NW + len(items)
            NROUTE = 21

            block = l1.enter_context(nc.Block())

            @block.sync
            def _(sp):
                sp.dma_start(router_nat, router_w).then_inc(ld_l1, 16)
                sp.dma_start(a_nat, lora_a).then_inc(ld_l1, 16)
                sp.dma_start(base_nat[:], base_w.rearrange("(t p) k -> p t k", p=P)).then_inc(ld_l1, 16)
                sp.dma_start(wqkv_nat[:], wqkv.rearrange("(k p) n -> p k n", p=P)).then_inc(ld_l1, 16)
                sp.dma_start(wo_nat[:], wo).then_inc(ld_l1, 16)
                for t in range(TT):
                    sp.dma_start(b_nat[:, t], lora_b[:, t * P:(t + 1) * P, :].rearrange("e p r -> p e r")).then_inc(ld_l1, 16)
                sp.dma_start(bias_a[:], bo.rearrange("(a n) -> a n", a=1).to_broadcast([P, D])).then_inc(ld_l1_bias, 16)
                sp.dma_start(bias_b[:], base_b.rearrange("(a n) -> a n", a=1).to_broadcast([P, D])).then_inc(ld_l1_bias, 16)
                with nc.allow_non_contiguous_dma(reason="three short columns"):
                    sp.dma_start(bqkv_col[:], bqkv.rearrange("(j p) -> p j", p=P)).then_inc(ld_l1_bias, 16)
                sp.wait_ge(w_tr, N0 + 2 + KD)

                def chunk(c, source):
                    g = c + CH
                    sp.dma_start(x_res[:], mid_rows[c]).then_inc(ld_res, 16)
                    if source is not None:
                        sp.wait_ge(xT_tr, g * TT + TT)
                        sp.dma_start(x_tile[:], source).then_inc(ld_x, 16)
                    for tt in range(TT):
                        sp.wait_ge(rows_done, g * TT + tt + 1)
                        sp.dma_start(out_rows[c][:, tt, :], g_tile[:, tt, :]).then_inc(st_out, 16)
                    sp.wait_ge(st_out, c * TT * 16 + TT * 16)
                    sp.sem_inc(g_free, 1)

                with sp.Fori(0, CH - 1) as c:
                    chunk(c, mid_rows[c + 1])
                chunk(CH - 1, None)

            @block.gpsimd
            def _(gp):
                gp.memset(pick_f[:], 0.0).then_inc(pick_ready, 1)
                for q in range(2):
                    gp.wait_ge(pick_ready, q + 1)
                    sq = pick_f[:].rearrange("e k (h r) -> e k h r", r=R)
                    gp.affine_select(out=sq, in_=sq, compare_op=ALU.not_equal, fill=1.0, base=-q * Q,
                                     pattern=[[-EPT, KE], [-1, EPT], [0, R]], channel_multiplier=1).then_inc(pick_ready, 1)

                def chunk(c, last):
                    if not last:
                        rows_rstd(gp, c + CH + 1)
                    for tt in range(TT):
                        gate(gp, c + CH, tt)

                with gp.Fori(0, CH - 1) as c:
                    chunk(c, False)
                chunk(CH - 1, True)

            @block.scalar
            def _(act):
                act.wait_ge(ld_l1, 9 * 16)
                nc.scalar.activation(wqkv_hi[:], wqkv_nat[:], ACT.Copy).then_inc(w_direct_hi, 1)
                nc.scalar.activation(wo_hi[:], wo_nat[:], ACT.Copy).then_inc(w_direct_hi, 1)
                for n, (kind, i) in enumerate(items):
                    act.wait_ge(w_tr, N0 + n + 1)
                    src = ring[n % 5]
                    if kind == "router":
                        last = nc.scalar.activation(router[:, :, 0:E], src[:, 0:KD * E].rearrange("p (k e) -> p k e", k=KD), ACT.Copy)
                    elif kind == "a":
                        for j in range(EPT):
                            last = nc.scalar.activation(a_hi[:, :, j * R:(j + 1) * R],
                                                        src[:, 0:KD * R].rearrange("p (k r) -> p k r", k=KD), ACT.Copy)
                    elif kind == "base":
                        last = nc.scalar.activation(base_hi[:, i, :], src[:], ACT.Copy)
                    else:
                        last = nc.scalar.activation(b_hi[:, i, :], src[:], ACT.Copy)
                    last.then_inc(w_hi, 1)
                act.wait_ge(ld_l1_bias, 3 * 16)

                def probs_exp(c, tt):
                    act.wait_ge(neg_max, c * TT + tt + 1)
                    act.wait_ge(silu_done, (c + CH - 1) * TT + tt + 1)
                    nc.scalar.activation(probs[:, tt, :], sc[tt % 2][:], ACT.Exp, bias=s_neg[:, tt:tt + 1], scale=QK_SCALE,
                                         accum_out=p_sum[:, tt:tt + 1]).then_inc(exp_done, 1)

                def prods_hi(c, kt):
                    act.wait_ge(prod_done, c * KE + kt + 1)
                    nc.scalar.activation(prod_hi[:, kt, :], prod[:, kt % 2, :], ACT.Copy).then_inc(prod_hi_done, 1)

                def probs_hi(c, kt):
                    act.wait_ge(p_tr, c * TT + kt + 1)
                    nc.scalar.activation(pT_hi[:, kt, :], tr[kt % 2][:], ACT.Copy).then_inc(p_hi_done, 1)

                def gate_tanh(c, tt):
                    act.wait_ge(y_read, (c + 1) * TT + tt + 1)
                    nc.scalar.activation(probs[:, tt, :], g_tile[:, tt, :], ACT.Tanh, scale=0.5).then_inc(tanh_done, 1)

                def chunk(c, last):
                    act.wait_ge(route_step, c * NROUTE + 4)
                    nc.scalar.activation(gate_p[:], gate_p[:], ACT.Exp).then_inc(route_exp, 1)
                    act.wait_ge(proj_done, c * 4 + 1)
                    nc.scalar.activation(res[:], pj[0][:], ACT.Copy).then_inc(proj_read, 1)
                    for j, src in enumerate((pj[1], sc[0], sc[1])):
                        act.wait_ge(proj_done, c * 4 + j + 2)
                        nc.scalar.activation(qkv[:, j, :], src[:], ACT.Identity, bias=bqkv_col[:, j:j + 1]).then_inc(proj_read, 1)
                        if j < 2:
                            act.wait_ge(proj_read, c * 4 + j + 2)
                            nc.scalar.activation(qk_hi[:, j, :], qkv[:, j, :], ACT.Copy).then_inc(qk_hi_done, 1)
                    act.wait_ge(comb_tr, c + 1)
                    nc.scalar.activation(combT[:], tr[0][0:2 * Q, :], ACT.Copy).then_inc(comb_hi, 1)
                    probs_exp(c, 0)
                    act.wait_ge(v_tr, c + 1)
                    nc.scalar.activation(v_hi[:], tr[1][:].rearrange("p (t d) -> p t d", t=TT), ACT.Copy).then_inc(v_hi_done, 1)
                    probs_exp(c, 1)
                    prods_hi(c, 0)
                    prods_hi(c, 1)
                    probs_exp(c, 2)
                    prods_hi(c, 2)
                    prods_hi(c, 3)
                    probs_exp(c, 3)
                    prods_hi(c, 4)
                    prods_hi(c, 5)
                    probs_hi(c, 0)
                    probs_hi(c, 1)
                    prods_hi(c, 6)
                    prods_hi(c, 7)
                    probs_hi(c, 2)
                    probs_hi(c, 3)
                    act.wait_ge(pv_done, c + 1)
                    nc.scalar.activation(at_hi[:], sc[0][:], ACT.Copy).then_inc(a_hi_done, 1)
                    for tt in range(3):
                        gate_tanh(c, tt)
                    if not last:
                        for tt in range(TT):
                            rows_hi(act, c + CH + 1, tt)
                    gate_tanh(c, 3)

                with act.Fori(0, CH - 1) as c:
                    chunk(c, False)
                chunk(CH - 1, True)

            @block.vector
            def _(dve):
                nc.vector.memset(comb[:], 0.0)
                dve.sem_inc(y_read, TT)
                dve.sem_inc(o_read, TT)
                dve.wait_ge(pick_ready, 3)
                nc.vector.tensor_copy(pick[:], pick_f[:])
                dve.wait_ge(w_direct_hi, 1)
                nc.vector.tensor_tensor(wqkv_lo[:], wqkv_nat[:], wqkv_hi[:].bitcast(F32), ALU.subtract).then_inc(w_direct_lo, 1)
                dve.wait_ge(w_direct_hi, 2)
                nc.vector.tensor_tensor(wo_lo[:], wo_nat[:], wo_hi[:].bitcast(F32), ALU.subtract).then_inc(w_direct_lo, 1)
                dve.wait_ge(ld_l1_bias, 3 * 16)
                nc.vector.tensor_scalar(bias_a[:], bias_a[:], 0.5, None, ALU.mult).then_inc(w_direct_lo, 1)
                for n, (kind, i) in enumerate(items):
                    dve.wait_ge(w_hi, N0 + n + 1)
                    src = ring[n % 5]
                    if kind == "router":
                        last = nc.vector.tensor_tensor(router[:, :, E:2 * E], src[:, 0:KD * E].rearrange("p (k e) -> p k e", k=KD),
                                                       router[:, :, 0:E].bitcast(F32), ALU.subtract)
                    elif kind == "a":
                        for j in range(EPT):
                            cols = slice(j * R, (j + 1) * R)
                            last = nc.vector.tensor_tensor(a_lo[:, :, cols], src[:, 0:KD * R].rearrange("p (k r) -> p k r", k=KD),
                                                           a_hi[:, :, cols].bitcast(F32), ALU.subtract)
                    elif kind == "base":
                        last = nc.vector.tensor_tensor(base_lo[:, i, :], src[:], base_hi[:, i, :].bitcast(F32), ALU.subtract)
                    else:
                        last = nc.vector.tensor_tensor(b_lo[:, i, :], src[:], b_hi[:, i, :].bitcast(F32), ALU.subtract)
                    last.then_inc(w_lo, 1)
                dve.wait_ge(w_direct_lo, 3)

                def wide(a):
                    return a[:, :, None].to_broadcast([P, TT, E])

                def route(c):
                    steps = [0]

                    def step(ins):
                        steps[0] += 1
                        ins.then_inc(route_step, 1)
                        dve.wait_ge(route_step, c * NROUTE + steps[0])

                    v = nc.vector
                    got = tr[0][:, 0:TT * 2 * E].rearrange("p (t h e) -> p t h e", t=TT, h=2)
                    dve.wait_ge(route_in, c + 1)
                    step(v.tensor_copy(lo_part[:], got[:, :, 1, :]))
                    step(v.tensor_tensor(gate_p[:], got[:, :, 0, :], lo_part[:], ALU.add))
                    step(v.reduce_max(row_a[:], gate_p[:], AX.X))
                    step(v.tensor_tensor(gate_p[:], gate_p[:], wide(row_a), ALU.subtract))
                    dve.wait_ge(route_exp, c + 1)
                    step(v.reduce_sum(row_a[:], gate_p[:], AX.X))
                    step(v.reciprocal(row_a[:], row_a[:]))
                    step(v.tensor_tensor(gate_p[:], gate_p[:], wide(row_a), ALU.mult))
                    for j in range(2):
                        step(v.reduce_max(top_p[:, j, :], gate_p[:], AX.X))
                        step(v.tensor_tensor(is_top[:], gate_p[:], wide(top_p[:, j, :]), ALU.is_equal))
                        step(v.tensor_tensor_scan(top_cnt[:].rearrange("p t e -> p (t e)"), restart_e[:],
                                                  is_top[:].rearrange("p t e -> p (t e)"), 0.0, ALU.mult, ALU.add))
                        step(v.scalar_tensor_tensor(top_w[:, j], top_cnt[:], 1.0, gate_p[:], ALU.is_equal, ALU.mult))
                        if j == 0:
                            step(v.tensor_tensor(gate_p[:], gate_p[:], top_w[:, 0], ALU.subtract))
                    step(v.scalar_tensor_tensor(row_a[:], top_p[:, 0, :], 1e-6, top_p[:, 1, :], ALU.add, ALU.add))
                    step(v.reciprocal(row_a[:], row_a[:]))
                    step(v.tensor_tensor(top_w[:, 0], top_w[:, 0], top_w[:, 1], ALU.add))
                    step(v.scalar_tensor_tensor(comb[:, :, 0:E], top_w[:, 0], SCALING, wide(row_a), ALU.mult, ALU.mult))
                    step(v.tensor_copy(comb[:, :, Q:Q + E], comb[:, :, 0:E]))
                    assert steps[0] == NROUTE

                def score_peak(c, tt):
                    dve.wait_ge(score_done, c * TT + tt + 1)
                    nc.vector.reduce_max(s_max[:, tt:tt + 1], sc[tt % 2][:], AX.X).then_inc(score_max, 1)
                    dve.wait_ge(score_max, c * TT + tt + 1)
                    nc.vector.tensor_scalar(s_neg[:, tt:tt + 1], s_max[:, tt:tt + 1], -QK_SCALE, None, ALU.mult).then_inc(neg_max, 1)

                def prods(c, kt):
                    dve.wait_ge(spread_done, c * KE + kt + 1)
                    if kt >= 2:
                        dve.wait_ge(prod_split, c * KE + kt - 1)
                    nc.vector.tensor_tensor(prod[:, kt % 2, :], pj[kt % 2][:], res[:], ALU.mult).then_inc(prod_done, 1)

                def prods_lo(c, kt):
                    dve.wait_ge(prod_hi_done, c * KE + kt + 1)
                    nc.vector.tensor_tensor(prod_lo[:, kt, :], prod[:, kt % 2, :], prod_hi[:, kt, :].bitcast(F32),
                                            ALU.subtract).then_inc(prod_split, 1)

                def probs_lo(c, kt):
                    dve.wait_ge(p_hi_done, c * TT + kt + 1)
                    nc.vector.tensor_tensor(pT_lo[:, kt, :], tr[kt % 2][:], pT_hi[:, kt, :].bitcast(F32),
                                            ALU.subtract).then_inc(p_split, 1)

                def four_prods(c, kt):
                    prods(c, kt)
                    prods(c, kt + 1)
                    prods_lo(c, kt)
                    prods_lo(c, kt + 1)

                def y_out(c, tt):
                    dve.wait_ge(y_done, c * TT + tt + 1)
                    if tt == 0:
                        dve.wait_ge(g_free, c + CH + 1)
                    nc.vector.tensor_tensor(g_tile[:, tt, :], y[tt % 2][:], bias_b[:], ALU.add).then_inc(y_read, 1)

                def s_out(c, tt):
                    dve.wait_ge(o_done, c * TT + tt + 1)
                    dve.wait_ge(s_free, (c + CH) * TT + tt + 1)
                    nc.vector.scalar_tensor_tensor(s_tile[:, tt, :], sc[(tt + 1) % 2][:], p_inv[:, tt:tt + 1], bias_a[:],
                                                   ALU.mult, ALU.add).then_inc(o_read, 1)

                def silu(c, tt):
                    dve.wait_ge(tanh_done, (c + CH) * TT + tt + 1)
                    nc.vector.scalar_tensor_tensor(g_tile[:, tt, :], probs[:, tt, :], 1.0, g_tile[:, tt, :],
                                                   ALU.add, ALU.mult).then_inc(silu_done, 1)

                def chunk(c, last):
                    route(c)
                    for j in range(2):
                        dve.wait_ge(qk_hi_done, c * 2 + j + 1)
                        nc.vector.tensor_tensor(qk_lo[:, j, :], qkv[:, j, :], qk_hi[:, j, :].bitcast(F32),
                                                ALU.subtract).then_inc(qk_split, 1)
                    dve.wait_ge(comb_hi, c + 1)
                    nc.vector.tensor_tensor(combT[Q:2 * Q, :], tr[0][Q:2 * Q, :], combT[Q:2 * Q, :].bitcast(F32),
                                            ALU.subtract).then_inc(comb_split, 1)
                    score_peak(c, 0)
                    dve.wait_ge(v_hi_done, c + 1)
                    nc.vector.tensor_tensor(v_lo[:], tr[1][:].rearrange("p (t d) -> p t d", t=TT), v_hi[:].bitcast(F32),
                                            ALU.subtract).then_inc(v_split, 1)
                    score_peak(c, 1)
                    four_prods(c, 0)
                    score_peak(c, 2)
                    four_prods(c, 2)
                    score_peak(c, 3)
                    four_prods(c, 4)
                    probs_lo(c, 0)
                    probs_lo(c, 1)
                    four_prods(c, 6)
                    probs_lo(c, 2)
                    probs_lo(c, 3)
                    dve.wait_ge(exp_done, c * TT + TT)
                    nc.vector.reciprocal(p_inv[:], p_sum[:]).then_inc(inv_step, 1)
                    dve.wait_ge(inv_step, c * 2 + 1)
                    nc.vector.tensor_scalar(p_inv[:], p_inv[:], 0.5, None, ALU.mult).then_inc(inv_step, 1)
                    dve.wait_ge(a_hi_done, c + 1)
                    nc.vector.tensor_tensor(at_lo[:], sc[0][:], at_hi[:].bitcast(F32), ALU.subtract).then_inc(a_split, 1)
                    dve.wait_ge(inv_step, c * 2 + 2)
                    for tt in range(TT):
                        if tt == TT - 1 and not last:
                            for t in range(TT):
                                rows_lo(dve, c + CH + 1, t)
                        y_out(c, tt)
                        s_out(c, tt)
                        silu(c, tt)
                        if tt == 0 and not last:
                            for t in range(TT):
                                rows_stats(dve, c + CH + 1, t)
                            dve.wait_ge(stats_in, (c + CH + 1) * TT + TT)
                        if tt == 1 and not last:
                            rows_moments()
                            rows_norm(dve, c + CH + 1)

                with dve.Fori(0, CH - 1) as c:
                    chunk(c, False)
                chunk(CH - 1, True)

            @block.tensor
            def _(pe):
                pe.wait_ge(ld_l1, 9 * 16)
                for n, (kind, i) in enumerate(items):
                    dst = ring[n % 5]
                    if n >= 5:
                        pe.wait_ge(w_lo, N0 + n - 5 + 1)
                    if kind == "router":
                        for k in range(KD):
                            last = nc.tensor.transpose(dst[:, k * E:(k + 1) * E], router_nat[:, k * P:(k + 1) * P], ident[0:E, 0:E])
                    elif kind == "a":
                        for k in range(KD):
                            last = nc.tensor.transpose(dst[:, k * R:(k + 1) * R], a_nat[:, k * P:(k + 1) * P], ident[0:R, 0:R])
                    elif kind == "base":
                        for t in range(TT):
                            last = nc.tensor.transpose(dst[:, t * P:(t + 1) * P], base_nat[:, t, i * P:(i + 1) * P], ident[:])
                    else:
                        for t in range(TT):
                            last = nc.tensor.transpose(dst[:, t * P:(t + 1) * P],
                                                       b_nat[:, t, EPT * i:EPT * (i + 1), :].rearrange("p e r -> p (e r)"), ident[:])
                    last.then_inc(w_tr, 1)
                pe.wait_ge(w_lo, N1)
                pe.wait_ge(w_direct_lo, 3)

                def three(dst, pairs, start=True, stop=True):
                    mms = [(a, b) for ah, al, bh, bl in pairs for a, b in ((ah, bh), (ah, bl), (al, bh))]
                    for n, (a, b) in enumerate(mms):
                        last = nc.tensor.matmul(dst, a, b, start=(start and n == 0), stop=(stop and n == len(mms) - 1))
                    return last

                def rows(tt):
                    return slice(tt * P, (tt + 1) * P)

                def scores(c, tt):
                    if tt >= 2:
                        pe.wait_ge(exp_done, c * TT + tt - 1)
                    three(sc[tt % 2][:], [(qk_hi[:, 0, rows(tt)], qk_lo[:, 0, rows(tt)], qk_hi[:, 1, :], qk_lo[:, 1, :])])\
                        .then_inc(score_done, 1)

                def spread(c, kt):
                    if kt < 2:
                        pe.wait_ge(proj_read, c * 4 + kt + 1)
                    else:
                        pe.wait_ge(prod_done, c * KE + kt - 1)
                    nc.tensor.matmul(pj[kt % 2][:], pick[:, kt, :], combT[:], start=True, stop=True).then_inc(spread_done, 1)

                def base(c, tt):
                    pe.wait_ge(y_read, c * TT + TT + tt - 1)
                    three(y[tt % 2][:], [(xT_hi[:, k, rows(tt)], xT_lo[:, k, rows(tt)], base_hi[:, k, :], base_lo[:, k, :])
                                         for k in range(KD)], stop=False)

                def lora(c, tt, k0, k1):
                    pe.wait_ge(prod_split, c * KE + k1)
                    last = three(y[tt % 2][:], [(prod_hi[:, k, rows(tt)], prod_lo[:, k, rows(tt)], b_hi[:, k, :], b_lo[:, k, :])
                                                for k in range(k0, k1)], start=False, stop=(k1 == KE))
                    if k1 == KE:
                        last.then_inc(y_done, 1)

                def probs_transpose(c, kt):
                    if kt == 0:
                        pe.wait_ge(exp_done, c * TT + TT)
                    elif kt == 1:
                        pe.wait_ge(v_split, c + 1)
                    else:
                        pe.wait_ge(p_split, c * TT + kt - 1)
                    for tt in range(TT):
                        last = nc.tensor.transpose(tr[kt % 2][:, rows(tt)], probs[:, tt, rows(kt)], ident[:])
                    last.then_inc(p_tr, 1)

                def project(c, tt):
                    if tt >= 2:
                        pe.wait_ge(o_read, c * TT + TT + tt - 1)
                    three(sc[(tt + 1) % 2][:], [(at_hi[:, rows(tt)], at_lo[:, rows(tt)], wo_hi[:], wo_lo[:])]).then_inc(o_done, 1)

                def chunk(c, last_chunk):
                    g = c + CH
                    pe.wait_ge(xT_done, g * TT + TT)
                    for tt in range(TT):
                        n = 0
                        for k in range(KD):
                            for a in (xT_hi, xT_lo):
                                last = nc.tensor.matmul(tr[0][:, tt * 2 * E:(tt + 1) * 2 * E], a[:, k, rows(tt)], router[:, k, :],
                                                        start=(n == 0), stop=(n == 2 * KD - 1))
                                n += 1
                    last.then_inc(route_in, 1)
                    three(pj[0][:], [(a_hi[:, k, :], a_lo[:, k, :], xT_hi[:, k, :], xT_lo[:, k, :]) for k in range(KD)]).then_inc(proj_done, 1)
                    for j, dst in enumerate((pj[1], sc[0], sc[1])):
                        if j == 1:
                            pe.wait_ge(o_read, c * TT + TT)
                        d = slice(j * DH, (j + 1) * DH)
                        three(dst[:], [(wqkv_hi[:, k, d], wqkv_lo[:, k, d], xT_hi[:, k, :], xT_lo[:, k, :])
                                       for k in range(KD)]).then_inc(proj_done, 1)
                    pe.wait_ge(route_step, c * NROUTE + NROUTE)
                    pe.wait_ge(qk_split, c * 2 + 2)
                    scores(c, 0)
                    for tt in range(TT):
                        last = nc.tensor.transpose(tr[0][0:2 * Q, rows(tt)], comb[:, tt, :], ident[:])
                    last.then_inc(comb_tr, 1)
                    pe.wait_ge(proj_read, c * 4 + 4)
                    for tt in range(TT):
                        last = nc.tensor.transpose(tr[1][:, rows(tt)], qkv[:, 2, rows(tt)], ident[:])
                    last.then_inc(v_tr, 1)
                    scores(c, 1)
                    pe.wait_ge(comb_split, c + 1)
                    spread(c, 0)
                    spread(c, 1)
                    base(c, 0)
                    scores(c, 2)
                    spread(c, 2)
                    spread(c, 3)
                    scores(c, 3)
                    base(c, 1)
                    spread(c, 4)
                    spread(c, 5)
                    probs_transpose(c, 0)
                    probs_transpose(c, 1)
                    lora(c, 0, 0, 4)
                    spread(c, 6)
                    spread(c, 7)
                    probs_transpose(c, 2)
                    probs_transpose(c, 3)
                    lora(c, 1, 0, 4)
                    pe.wait_ge(p_split, c * TT + TT)
                    three(sc[0][:], [(v_hi[:, k, :], v_lo[:, k, :], pT_hi[:, k, :], pT_lo[:, k, :]) for k in range(TT)]).then_inc(pv_done, 1)
                    lora(c, 0, 4, 8)
                    pe.wait_ge(a_split, c + 1)
                    project(c, 0)
                    lora(c, 1, 4, 8)
                    project(c, 1)
                    base(c, 2)
                    lora(c, 2, 0, 8)
                    project(c, 2)
                    base(c, 3)
                    if not last_chunk:
                        transpose_rows(pe, g + 1, 0)
                        transpose_rows(pe, g + 1, 1)
                    lora(c, 3, 0, 4)
                    if not last_chunk:
                        for tt in (2, 3):
                            pe.wait_ge(xT_done, (g + 1) * TT + tt - 1)
                            transpose_rows(pe, g + 1, tt)
                    lora(c, 3, 4, 8)
                    project(c, 3)

                with pe.Fori(0, CH - 1) as c:
                    chunk(c, False)
                chunk(CH - 1, True)



_INS = ["L0_attn_data", "L0_attn_mask", "L0_attn_weight", "L0_attn_bias", "L0_ffn_c1_w", "L0_ffn_c2_w", "L0_ffn_w1",
        "L0_ffn_w2t", "L1_attn_Wqkv", "L1_attn_bqkv", "L1_attn_Wo", "L1_attn_bo", "L1_ffn_base_w", "L1_ffn_base_b",
        "L1_ffn_A", "L1_ffn_B", "L1_ffn_router_w"]


def kernel(**inputs):
    import numpy as np
    import concourse.bacc as bacc
    from concourse.bass_utils import run_bass_kernel_spmd

    nc = bacc.Bacc("TRN2", target_bir_lowering=False, num_devices=1, dynamic_dma_scratch_size=1024)
    arrays, args = {}, []
    for name in _INS:
        a = np.ascontiguousarray(inputs[name])
        arrays[f"in_{name}"] = a
        args.append(nc.dram_tensor(f"in_{name}", a.shape, mybir.dt.from_np(a.dtype), kind="ExternalInput").ap())
    shape = arrays["in_L0_attn_data"].shape
    args.append(nc.dram_tensor("out", shape, F32, kind="ExternalOutput").ap())
    block_mask_ffn_then_attention_lora_kernel(nc, *args)
    r = run_bass_kernel_spmd(nc, [arrays], core_ids=[0])
    return r.results[0]["out"]
```

```python
from contextlib import ExitStack

import concourse.bass as bass
import numpy as np
from concourse import mybir

P = 128
BANK = 512

ALU = mybir.AluOpType
ACT = mybir.ActivationFunctionType
AX = mybir.AxisListType
F32 = mybir.dt.float32
F32R = mybir.dt.float32r
BF16 = mybir.dt.bfloat16
I32 = mybir.dt.int32


def block_mask_ffn_then_attention_lora_kernel(
    nc: bass.Bass,
    x_in: bass.AP,
    mask: bass.AP,
    w_s0: bass.AP,
    b_s0: bass.AP,
    c1_w: bass.AP,
    c2_w: bass.AP,
    w1: bass.AP,
    w2: bass.AP,
    wqkv: bass.AP,
    bqkv: bass.AP,
    wo: bass.AP,
    bo: bass.AP,
    base_w: bass.AP,
    base_b: bass.AP,
    lora_a: bass.AP,
    lora_b: bass.AP,
    router_w: bass.AP,
    out: bass.AP,
):
    B, S, D = x_in.shape
    INTER = w1.shape[0]
    RANK = c1_w.shape[0]
    DH = wo.shape[0]
    E, _, R = lora_b.shape
    SEG = 32
    KD = D // P
    TT = S // P
    IT = INTER // P
    CH = B
    PIECES = -(-INTER // BANK)
    PW = [min(BANK, INTER - p * BANK) for p in range(PIECES)]
    KE = E * R // P
    EPT = P // R
    SCALING = 32.0 / 64.0
    EPS = 1e-5
    QK_SCALE = float(DH) ** -0.5
    Q = P // 4
    assert D == BANK and S == BANK and DH == P and RANK <= Q and E <= Q and R * 2 == P and IT % 2 == 0

    x_rows = x_in.rearrange("b (t p) d -> b p t d", p=P)
    out_rows = out.rearrange("b (t p) d -> b p t d", p=P)
    mid = nc.dram_tensor("mid_state", (B, S, D), F32, kind="Internal").ap()
    mid_rows = mid.rearrange("b (t p) d -> b p t d", p=P)

    ctx = ExitStack()
    with ctx:
        def sem(name):
            return ctx.enter_context(nc.semaphore(name))

        class Span:

            def __init__(self, start):
                self.start = self.end = start

            def take(self, name, shape, dt=F32):
                t = nc.alloc_sbuf_tensor_at(name, shape, dt, offset=self.end)
                size = int(np.prod(shape[1:])) * mybir.dt.size(dt)
                self.end += -(-size // 32) * 32
                return t

        both = Span(-(-nc.sbuf_base // 64) * 64)
        ident = both.take("ident", [P, P])
        ident_bf = both.take("ident_bf", [P, P], BF16)
        restart = both.take("restart", [P, BANK], BF16)
        restart_e = both.take("restart_e", [P, TT * E])
        neg_half = both.take("neg_half", [P, TT])
        eps = both.take("eps", [P, TT])
        x_tile = both.take("x_tile", [P, TT, D])
        x_res = both.take("x_res", [P, TT, D])
        s_tile = both.take("s_tile", [P, TT, D])
        g_tile = both.take("g_tile", [P, TT, D])
        xT_hi = both.take("xT_hi", [P, KD, S], F32R)
        xT_lo = both.take("xT_lo", [P, KD, S], F32R)
        bn = both.take("bn", [P, TT, 6])
        mean_var = both.take("mean_var", [P, TT, 2])
        rstd = both.take("rstd", [P, TT])
        bias_a = both.take("bias_a", [P, D])
        bias_b = both.take("bias_b", [P, D])
        a_nat = both.take("a_nat", [P, D])
        bqkv_col = both.take("bqkv_col", [P, 3])
        comb = both.take("comb", [P, TT, 2 * Q])
        gate_p = both.take("gate_p", [P, TT, E])
        is_top = both.take("is_top", [P, TT, E])
        top_cnt = both.take("top_cnt", [P, TT, E])
        top_w = both.take("top_w", [P, 2, TT, E])
        row_a = both.take("row_a", [P, TT])
        top_p = both.take("top_p", [P, 2, TT])
        s_max = both.take("s_max", [P, TT])
        s_neg = both.take("s_neg", [P, TT])
        p_sum = both.take("p_sum", [P, TT])
        p_inv = both.take("p_inv", [P, TT])

        span_c = Span(both.end)
        c1_hi = span_c.take("c1_hi", [P, KD, P], F32R)
        c1_lo = span_c.take("c1_lo", [P, KD, P], F32R)
        c1_nat = span_c.take("c1_nat", [RANK, D])
        next_c = Span(span_c.start)
        wqkv_nat = next_c.take("wqkv_nat", [P, KD, 3 * DH])
        next_c2 = Span(span_c.start)
        res = next_c2.take("res", [P, S])
        prod = next_c2.take("prod", [P, 2, S])

        span_s = Span(max(span_c.end, next_c.end, next_c2.end))
        ws_hi = span_s.take("ws_hi", [P, KD, D], F32R)
        ws_lo = span_s.take("ws_lo", [P, KD, D], F32R)
        next_s = Span(span_s.start)
        wqkv_hi = next_s.take("wqkv_hi", [P, KD, 3 * DH], F32R)
        wqkv_lo = next_s.take("wqkv_lo", [P, KD, 3 * DH], F32R)
        a_hi = next_s.take("a_hi", [P, KD, R + E], F32R)
        a_lo = next_s.take("a_lo", [P, KD, R + E], F32R)

        span_1 = Span(max(span_s.end, next_s.end))
        w1T_hi = span_1.take("w1T_hi", [P, KD, INTER], F32R)
        w1T_lo = span_1.take("w1T_lo", [P, KD, INTER], F32R)
        next_1 = Span(span_1.start)
        base_hi = next_1.take("base_hi", [P, KD, D], F32R)
        base_lo = next_1.take("base_lo", [P, KD, D], F32R)
        wo_hi = next_1.take("wo_hi", [P, D], F32R)
        wo_lo = next_1.take("wo_lo", [P, D], F32R)
        pick = next_1.take("pick", [2 * Q, KE, P], F32R)
        next_1b = Span(next_1.end)
        base_nat = next_1.take("base_nat", [P, TT, D])
        wo_nat = next_1.take("wo_nat", [P, D])
        pick_f = next_1.take("pick_f", [2 * Q, KE, P])
        prod_hi = next_1b.take("prod_hi", [P, KE, S], F32R)
        prod_lo = next_1b.take("prod_lo", [P, KE, S], F32R)

        span_2 = Span(max(span_1.end, next_1.end, next_1b.end))
        w2_hi_t = span_2.take("w2_hi_t", [P, IT, D], F32R)
        w2_lo_t = span_2.take("w2_lo_t", [P, IT, D], F32R)
        c2_stack = span_2.take("c2_stack", [P, INTER], F32R)
        t_stack = span_2.take("t_stack", [P, S], F32R)
        eq = span_2.take("eq", [P, BANK], BF16)
        counts = span_2.take("counts", [P, 2, TT, BANK], BF16)
        seg_top = span_2.take("seg_top", [P, BANK // SEG])
        h = span_2.take("h", [P, S])
        before_h = Span(span_2.end)
        h_hi = span_2.take("h_hi", [P, 2, S], F32R)
        h_lo = span_2.take("h_lo", [P, 2, S], F32R)
        mask_nat = before_h.take("mask_nat", [P, TT, D], I32)
        next_2 = Span(span_2.start)
        b_nat = next_2.take("b_nat", [P, TT, E, R])
        next_2b = Span(span_2.start)
        pT_hi = next_2b.take("pT_hi", [P, TT, S], F32R)
        pT_lo = next_2b.take("pT_lo", [P, TT, S], F32R)
        rest_2 = Span(max(next_2.end, next_2b.end))
        b_hi = rest_2.take("b_hi", [P, KE, D], F32R)
        b_lo = rest_2.take("b_lo", [P, KE, D], F32R)
        probs = rest_2.take("probs", [P, TT, S])
        qkv = rest_2.take("qkv", [P, 3, S])
        qk_hi = rest_2.take("qk_hi", [P, 2, S], F32R)
        qk_lo = rest_2.take("qk_lo", [P, 2, S], F32R)
        v_hi = rest_2.take("v_hi", [P, TT, DH], F32R)
        v_lo = rest_2.take("v_lo", [P, TT, DH], F32R)
        at_hi = rest_2.take("at_hi", [P, S], F32R)
        at_lo = rest_2.take("at_lo", [P, S], F32R)
        combT = rest_2.take("combT", [2 * Q, S], F32R)
        assert max(span_2.end, rest_2.end, before_h.end) <= nc.sbuf_usable_end

        banks = [ctx.enter_context(nc.psum_tensor(f"bank{i}", [P, BANK], F32)) for i in range(8)]

        consts_gp = sem("consts_gp")
        consts_dve = sem("consts_dve")
        ld_x = sem("ld_x")
        ld_res = sem("ld_res")
        st_rows = sem("st_rows")
        ld_c1 = sem("ld_c1")
        ld_c2 = sem("ld_c2")
        ld_mask = sem("ld_mask")
        ld_ws0 = sem("ld_ws0")
        ld_w = [sem(f"ld_w_{i}") for i in range(7)]
        ld_bias = sem("ld_bias")
        ld_l1_small = sem("ld_l1_small")
        ld_wqkv = sem("ld_wqkv")
        ld_bo = sem("ld_bo")
        ld_base = sem("ld_base")
        ld_b = sem("ld_b")
        w_tr = sem("w_tr")
        w_hi = sem("w_hi")
        w_lo = sem("w_lo")
        w2_hi = sem("w2_hi")
        w2_lo = sem("w2_lo")
        mask_sum = sem("mask_sum")
        mask_cnt = sem("mask_cnt")
        mask_on = sem("mask_on")
        ws0_masked = sem("ws0_masked")
        c2_wide = sem("c2_wide")
        half_bias = sem("half_bias")
        stats_in = sem("stats_in")
        stats = sem("stats")
        rstd_step = sem("rstd_step")
        xn_ready = sem("xn_ready")
        xT_tr = sem("xT_tr")
        xT_hi_done = sem("xT_hi_done")
        xT_done = sem("xT_done")
        t_done = sem("t_done")
        t_hi = sem("t_hi")
        t_split = sem("t_split")
        s0_done = sem("s0_done")
        s0_read = sem("s0_read")
        s_biased = sem("s_biased")
        sel_done = sem("sel_done")
        seg_max = sem("seg_max")
        sel_eq = sem("sel_eq")
        sel_count = sem("sel_count")
        first_tr = sem("first_tr")
        up_done = sem("up_done")
        relu_done = sem("relu_done")
        h_masked = sem("h_masked")
        h_hi_done = sem("h_hi_done")
        h_split = sem("h_split")
        down_done = sem("down_done")
        tanh_done = sem("tanh_done")
        silu_done = sem("silu_done")
        rows_done = sem("rows_done")

        s_free = sem("s_free")
        g_free = sem("g_free")
        w_direct_hi = sem("w_direct_hi")
        w_direct_lo = sem("w_direct_lo")
        pick_ready = sem("pick_ready")
        logits_out = sem("logits_out")
        route_in = sem("route_in")
        route_step = sem("route_step")
        route_exp = sem("route_exp")
        comb_ready = sem("comb_ready")
        comb_tr = sem("comb_tr")
        comb_hi = sem("comb_hi")
        comb_split = sem("comb_split")
        proj_done = sem("proj_done")
        proj_read = sem("proj_read")
        qk_hi_done = sem("qk_hi_done")
        qk_split = sem("qk_split")
        v_tr = sem("v_tr")
        v_hi_done = sem("v_hi_done")
        v_split = sem("v_split")
        score_done = sem("score_done")
        score_max = sem("score_max")
        neg_max = sem("neg_max")
        exp_done = sem("exp_done")
        inv_step = sem("inv_step")
        p_tr = sem("p_tr")
        p_hi_done = sem("p_hi_done")
        p_split = sem("p_split")
        pv_done = sem("pv_done")
        a_hi_done = sem("a_hi_done")
        a_split = sem("a_split")
        spread_done = sem("spread_done")
        prod_done = sem("prod_done")
        prod_hi_done = sem("prod_hi_done")
        prod_split = sem("prod_split")
        y_done = sem("y_done")
        y_read = sem("y_read")
        o_done = sem("o_done")
        o_read = sem("o_read")
        st_out = sem("st_out")

        def transpose_rows(pe, g, tt):
            pe.wait_ge(xn_ready, g * TT + tt + 1)
            for k in range(KD):
                last = nc.tensor.transpose(banks[tt % 2][:, k * P:(k + 1) * P],
                                           x_tile[:, tt, k * P:(k + 1) * P], ident[:])
            last.then_inc(xT_tr, 1)

        def rows_hi(act, g, tt):
            act.wait_ge(xT_tr, g * TT + tt + 1)
            nc.scalar.activation(xT_hi[:, :, tt * P:(tt + 1) * P],
                                 banks[tt % 2][:].rearrange("p (k t) -> p k t", k=KD), ACT.Copy).then_inc(xT_hi_done, 1)

        def rows_lo(dve, g, tt):
            dve.wait_ge(xT_hi_done, g * TT + tt + 1)
            cols = slice(tt * P, (tt + 1) * P)
            nc.vector.tensor_tensor(xT_lo[:, :, cols], banks[tt % 2][:].rearrange("p (k t) -> p k t", k=KD),
                                    xT_hi[:, :, cols].bitcast(F32), ALU.subtract).then_inc(xT_done, 1)

        def rows_stats(dve, g, tt):
            if tt == 0:
                dve.wait_ge(ld_x, g * 16 + 16)
            nc.vector.bn_stats(bn[:, tt, :], x_tile[:, tt, :]).then_inc(stats_in, 1)

        def rows_moments():
            for tt in range(TT):
                last = nc.vector.bn_aggr(mean_var[:, tt, :], bn[:, tt, :])
            last.then_inc(stats, 1)

        def rows_rstd(gp, g):
            gp.wait_ge(stats, g + 1)
            nc.gpsimd.tensor_tensor(rstd[:], mean_var[:, :, 1], eps[:], ALU.add).then_inc(rstd_step, 1)
            gp.wait_ge(rstd_step, g * 2 + 1)
            nc.gpsimd.tensor_tensor(rstd[:], rstd[:], neg_half[:], ALU.pow).then_inc(rstd_step, 1)

        def rows_norm(dve, g):
            dve.wait_ge(rstd_step, g * 2 + 2)
            for tt in range(TT):
                nc.vector.tensor_scalar(x_tile[:, tt, :], x_tile[:, tt, :], mean_var[:, tt, 0:1],
                                        rstd[:, tt:tt + 1], ALU.subtract, ALU.mult).then_inc(xn_ready, 1)

        def gate(gp, g, tt):
            gp.wait_ge(silu_done, g * TT + tt + 1)
            nc.gpsimd.tensor_tensor(g_tile[:, tt, :], g_tile[:, tt, :], s_tile[:, tt, :], ALU.mult).then_inc(s_free, 1)
            if tt == 0:
                gp.wait_ge(ld_res, g * 16 + 16)
            gp.wait_ge(s_free, g * TT + tt + 1 + TT)
            nc.gpsimd.tensor_tensor(g_tile[:, tt, :], g_tile[:, tt, :], x_res[:, tt, :], ALU.add).then_inc(rows_done, 1)

        def rows(tt):
            return slice(tt * P, (tt + 1) * P)

        def three(dst, pairs, start=True, stop=True):
            mms = [(a, b) for ah, al, bh, bl in pairs for a, b in ((ah, bh), (ah, bl), (al, bh))]
            for n, (a, b) in enumerate(mms):
                last = nc.tensor.matmul(dst, a, b, start=(start and n == 0), stop=(stop and n == len(mms) - 1))
            return last

        seg_ones = h[:, 0:P]
        row_cnt = h[:, P:2 * P]
        on = h[:, 2 * P:3 * P]
        ws_nat = s_tile
        c2_nat = x_res[:, 0, 0:IT * RANK].rearrange("p (i r) -> p i r", r=RANK)
        c2_rep = counts[:].bitcast(F32).rearrange("p a t n -> p (a t n)")[:, 0:IT * P]
        c2_rep_q = c2_rep.rearrange("p (i q r) -> p i q r", q=4, r=Q)
        up = [banks[0], banks[1]]
        acc = [banks[2 + tt] for tt in range(TT)]
        sel = banks[6]
        first = banks[7][:].bitcast(BF16)[:, 0:S]
        NSEL = PIECES * TT
        MB = D // SEG

        logits = qkv[R:R + E, 2, :]
        pj = [banks[0], banks[1]]
        y = [banks[2], banks[3]]
        sc = [banks[4], banks[5]]
        tr = [banks[6], banks[7]]
        NROUTE = 19

        EARLY = [banks[i] for i in (2, 3, 4, 5, 7)]
        LATE = [banks[i] for i in (2, 3, 7)]
        W1 = [("w1", i) for i in range(IT)]
        C2 = [("c2", i) for i in range(0, IT, 4)]
        WS = [("ws", k) for k in range(KD)]
        items = W1[:4] + [("c1", 0)] + W1[4:6]
        BEFORE_ROWS = len(items)
        items += W1[6:8]
        BEFORE_MASK = len(items)
        items += W1[8:9] + C2[:1] + W1[9:10] + WS
        BEFORE_S = len(items)
        items += W1[10:11] + C2[1:2] + W1[11:12] + C2[2:3] + W1[12:13] + C2[3:] + W1[13:14]
        bank_of = [EARLY[n % 5] for n in range(len(items))]
        frees = [n - 5 for n in range(len(items))]
        NW = len(items)
        w_at = {item: n for n, item in enumerate(items)}
        AFTER_S = [range(BEFORE_S + 2 * tt, min(BEFORE_S + 2 * tt + 2, NW)) for tt in range(TT)]
        places = [g_tile[:, i, :] for i in range(4)] + [x_res[:, i, :] for i in range(1, 4)]
        NP = len(places)
        items += [("a", 0)]
        bank_of += [banks[6]]
        frees += [-1]
        L1_AT = len(items)
        items += [("base", k) for k in range(KD)] + [("b", k) for k in range(KE)]
        bank_of += [LATE[n % 3] for n in range(len(items) - L1_AT)]
        frees += [n - 3 if n >= 3 else -1 for n in range(len(items) - L1_AT)]
        for n, m in enumerate(frees):
            if n >= L1_AT and m >= 0:
                frees[n] = L1_AT + m

        def item_in(pe, n):
            kind, i = items[n]
            dst = bank_of[n]
            if frees[n] >= 0:
                pe.wait_ge(w_lo, frees[n] + 1)
            if kind == "c1":
                pe.wait_ge(ld_c1, 16)
                for k in range(KD):
                    last = nc.tensor.transpose(dst[:, k * RANK:(k + 1) * RANK], c1_nat[:, rows(k)], ident[0:RANK, 0:RANK])
            elif kind == "c2":
                pe.wait_ge(c2_wide, 1)
                for j in range(i, min(i + 4, IT)):
                    last = nc.tensor.transpose(dst[:, rows(j - i)], c2_rep[:, rows(j)], ident[:])
            elif kind == "ws":
                pe.wait_ge(ws0_masked, TT)
                for t in range(TT):
                    last = nc.tensor.transpose(dst[:, rows(t)], ws_nat[:, t, rows(i)], ident[:])
            elif kind == "w1":
                pe.wait_ge(ld_w[i % NP], 16 * (i // NP + 1))
                for k in range(KD):
                    last = nc.tensor.transpose(dst[:, rows(k)], places[i % NP][:, rows(k)], ident[:])
            elif kind == "a":
                pe.wait_ge(ld_l1_small, 16 * 4)
                for k in range(KD):
                    last = nc.tensor.transpose(dst[:, k * (R + E):(k + 1) * (R + E)], a_nat[0:R + E, rows(k)],
                                               ident[0:R + E, 0:R + E])
            elif kind == "base":
                pe.wait_ge(ld_base, 2 * 16)
                for t in range(TT):
                    last = nc.tensor.transpose(dst[:, rows(t)], base_nat[:, t, rows(i)], ident[:])
            else:
                pe.wait_ge(ld_b, TT * 16)
                for t in range(TT):
                    last = nc.tensor.transpose(dst[:, rows(t)],
                                               b_nat[:, t, EPT * i:EPT * (i + 1), :].rearrange("p e r -> p (e r)"), ident[:])
            last.then_inc(w_tr, 1)

        def item_parts(n):
            kind, i = items[n]
            src = bank_of[n]
            by_k = src[:].rearrange("p (k n) -> p k n", k=KD)
            if kind == "c1":
                got = src[:, 0:KD * RANK].rearrange("p (k r) -> p k r", k=KD)
                return [(got, c1_hi[:, :, q * Q:q * Q + RANK], c1_lo[:, :, q * Q:q * Q + RANK]) for q in range(4)]
            if kind == "ws":
                return [(src[:], ws_hi[:, i, :], ws_lo[:, i, :])]
            if kind == "w1":
                return [(by_k, w1T_hi[:, :, rows(i)], w1T_lo[:, :, rows(i)])]
            if kind == "a":
                return [(src[:, 0:KD * (R + E)].rearrange("p (k r) -> p k r", k=KD), a_hi[:], a_lo[:])]
            if kind == "base":
                return [(src[:], base_hi[:, i, :], base_lo[:, i, :])]
            return [(src[:], b_hi[:, i, :], b_lo[:, i, :])]

        def item_hi(act, n):
            kind, i = items[n]
            act.wait_ge(w_tr, n + 1)
            if kind == "c1":
                act.wait_ge(consts_dve, 13)
            if kind == "c2":
                cols = slice(i * P, min(i + 4, IT) * P)
                last = nc.scalar.activation(c2_stack[:, cols], bank_of[n][:, 0:cols.stop - cols.start], ACT.Copy)
            else:
                for got, hi, _ in item_parts(n):
                    last = nc.scalar.activation(hi, got, ACT.Copy)
            last.then_inc(w_hi, 1)

        def item_lo(dve, n):
            kind, i = items[n]
            dve.wait_ge(w_hi, n + 1)
            if kind == "c2":
                cols = slice(i * P, min(i + 4, IT) * P)
                for q in (1, 3):
                    part = c2_stack[q * Q:(q + 1) * Q, cols]
                    last = nc.vector.tensor_tensor(part, bank_of[n][q * Q:(q + 1) * Q, 0:cols.stop - cols.start],
                                                   part.bitcast(F32), ALU.subtract)
            else:
                for got, hi, lo in item_parts(n):
                    last = nc.vector.tensor_tensor(lo, got, hi.bitcast(F32), ALU.subtract)
            last.then_inc(w_lo, 1)

        LATE_GROUPS = [range(L1_AT + 4 * j, L1_AT + 4 * j + 4) for j in range(3)]

        block = ctx.enter_context(nc.Block())

        @block.sync
        def _(sp):
            def stage(n):
                m = n - NP
                if 0 <= m < IT:
                    sp.wait_ge(w_tr, w_at["w1", m] + 1)
                elif m >= IT:
                    sp.wait_ge(w2_lo, m - IT + 1)
                w, i = (w1, n) if n < IT else (w2, n - IT)
                sp.dma_start(places[n % NP], w[i * P:(i + 1) * P, :]).then_inc(ld_w[n % NP], 16)

            for n in range(4):
                stage(n)
            sp.dma_start(c1_nat[:], c1_w).then_inc(ld_c1, 16)
            sp.dma_start(x_tile[:], x_rows[0]).then_inc(ld_x, 16)
            for n in range(4, 6):
                stage(n)
            sp.dma_start(mask_nat[:], mask.rearrange("(t p) k -> p t k", p=P)).then_inc(ld_mask, 16)
            stage(6)
            sp.dma_start(ws_nat[:], w_s0.rearrange("(t p) k -> p t k", p=P)).then_inc(ld_ws0, 16)
            for n in range(7, 9):
                stage(n)
            sp.dma_start(c2_nat, c2_w.rearrange("(i p) r -> p i r", p=P)).then_inc(ld_c2, 16)
            for n in range(9, IT):
                stage(n)
            sp.dma_start(bias_a[:], b_s0.rearrange("(a n) -> a n", a=1).to_broadcast([P, D])).then_inc(ld_bias, 16)
            for n in range(IT, 2 * IT):
                stage(n)
            sp.dma_start(a_nat[R:R + E, :], router_w).then_inc(ld_l1_small, 16)
            sp.dma_start(a_nat[0:R, :], lora_a).then_inc(ld_l1_small, 16)
            sp.dma_start(bias_b[:], base_b.rearrange("(a n) -> a n", a=1).to_broadcast([P, D])).then_inc(ld_l1_small, 16)
            with nc.allow_non_contiguous_dma(reason="three short columns"):
                sp.dma_start(bqkv_col[:], bqkv.rearrange("(j p) -> p j", p=P)).then_inc(ld_l1_small, 16)

            def chunk(c, source, last):
                sp.wait_ge(xT_tr, c * TT + TT)
                sp.dma_start(x_tile[:], source).then_inc(ld_x, 16)
                sp.wait_ge(w2_lo, IT)
                sp.wait_ge(c2_wide, 1)
                sp.dma_start(x_res[:], x_rows[c]).then_inc(ld_res, 16)
                if last:
                    sp.wait_ge(t_done, CH)
                    sp.dma_start(wqkv_nat[:], wqkv.rearrange("(k p) n -> p k n", p=P)).then_inc(ld_wqkv, 16)
                if last:
                    sp.wait_ge(s_biased, CH * TT)
                    sp.dma_start(bias_a[:], bo.rearrange("(a n) -> a n", a=1).to_broadcast([P, D])).then_inc(ld_bo, 16)
                    sp.wait_ge(up_done, CH * IT)
                    sp.dma_start(base_nat[:], base_w.rearrange("(t p) k -> p t k", p=P)).then_inc(ld_base, 16)
                    sp.dma_start(wo_nat[:], wo).then_inc(ld_base, 16)
                    sp.wait_ge(down_done, CH * IT)
                    for t in range(TT):
                        sp.dma_start(b_nat[:, t], lora_b[:, rows(t), :].rearrange("e p r -> p e r")).then_inc(ld_b, 16)
                for tt in range(TT):
                    sp.wait_ge(rows_done, c * TT + tt + 1)
                    sp.dma_start(mid_rows[c][:, tt, :], g_tile[:, tt, :]).then_inc(st_rows, 16)
                sp.wait_ge(st_rows, c * TT * 16 + TT * 16)
                sp.sem_inc(g_free, 1)

            sp.sem_inc(g_free, 1)
            with sp.Fori(0, CH - 1) as c:
                chunk(c, x_rows[c + 1], False)
            chunk(CH - 1, mid_rows[0], True)

            def chunk(c, source):
                g = c + CH
                sp.dma_start(x_res[:], mid_rows[c]).then_inc(ld_res, 16)
                if source is not None:
                    sp.wait_ge(xT_tr, g * TT + TT)
                    sp.dma_start(x_tile[:], source).then_inc(ld_x, 16)
                for tt in range(TT):
                    sp.wait_ge(rows_done, g * TT + tt + 1)
                    sp.dma_start(out_rows[c][:, tt, :], g_tile[:, tt, :]).then_inc(st_out, 16)
                sp.wait_ge(st_out, c * TT * 16 + TT * 16)
                sp.sem_inc(g_free, 1)

            with sp.Fori(0, CH - 1) as c:
                chunk(c, mid_rows[c + 1])
            chunk(CH - 1, None)

        @block.gpsimd
        def _(gp):
            gp.memset(ident[:], 0.0).then_inc(consts_gp, 1)
            gp.memset(ident_bf[:], 0.0).then_inc(consts_gp, 1)
            gp.memset(neg_half[:], -0.5).then_inc(consts_gp, 1)
            gp.memset(eps[:], EPS).then_inc(consts_gp, 1)
            gp.wait_ge(consts_gp, 4)
            for m in (ident, ident_bf):
                gp.affine_select(out=m[:], in_=m[:], compare_op=ALU.not_equal, fill=1.0, base=0,
                                 pattern=[[-1, P]], channel_multiplier=1).then_inc(consts_gp, 1)
            gp.sem_inc(s_free, TT)
            rows_rstd(gp, 0)
            gp.wait_ge(mask_on, 1)
            gp.wait_ge(ld_ws0, 16)
            for t in range(TT):
                part = ws_nat[:, t, :].rearrange("p (n s) -> p n s", s=SEG)
                nc.gpsimd.tensor_tensor(part, part, on[:, t * MB:(t + 1) * MB][:, :, None].to_broadcast([P, MB, SEG]),
                                        ALU.mult).then_inc(ws0_masked, 1)
            gp.wait_ge(ld_bias, 16)
            nc.gpsimd.tensor_scalar(bias_a[:], bias_a[:], 0.5, 1.0, ALU.mult, ALU.mult).then_inc(half_bias, 1)
            for i in range(IT):
                n = IT + i
                gp.wait_ge(ld_w[n % NP], 16 * (n // NP + 1))
                nc.gpsimd.tensor_copy(w2_hi_t[:, i, :], places[n % NP]).then_inc(w2_hi, 1)
                gp.wait_ge(w2_hi, i + 1)
                nc.gpsimd.tensor_tensor(w2_lo_t[:, i, :], places[n % NP], w2_hi_t[:, i, :].bitcast(F32),
                                        ALU.subtract).then_inc(w2_lo, 1)
            gp.wait_ge(half_bias, 1)

            def head(c):
                for tt in range(TT):
                    gp.wait_ge(s0_read, c * TT + tt + 1)
                    nc.gpsimd.tensor_tensor(s_tile[:, tt, :], s_tile[:, tt, :], bias_a[:], ALU.add).then_inc(s_biased, 1)

            def body(c, last):
                rows_rstd(gp, c + 1)
                if last:
                    gp.wait_ge(up_done, CH * IT)
                    gp.memset(pick_f[:], 0.0).then_inc(pick_ready, 1)
                    for q in range(2):
                        gp.wait_ge(pick_ready, q + 1)
                        sq = pick_f[:].rearrange("e k (h r) -> e k h r", r=R)
                        gp.affine_select(out=sq, in_=sq, compare_op=ALU.not_equal, fill=1.0, base=-q * Q,
                                         pattern=[[-EPT, KE], [-1, EPT], [0, R]], channel_multiplier=1).then_inc(pick_ready, 1)
                    gp.wait_ge(pick_ready, 3)
                    nc.gpsimd.tensor_copy(pick[:], pick_f[:]).then_inc(pick_ready, 1)
                gp.wait_ge(s_biased, c * TT + TT)
                for tt in range(TT):
                    gate(gp, c, tt)

            head(0)
            with gp.Fori(0, CH - 1) as c:
                body(c, False)
                head(c + 1)
            body(CH - 1, True)

            def chunk(c, last):
                for kt in range(KE):
                    gp.wait_ge(prod_hi_done, c * KE + kt + 1)
                    nc.gpsimd.tensor_tensor(prod_lo[:, kt, :], prod[:, kt % 2, :], prod_hi[:, kt, :].bitcast(F32),
                                            ALU.subtract).then_inc(prod_split, 1)
                if not last:
                    rows_rstd(gp, c + CH + 1)
                for tt in range(TT):
                    gate(gp, c + CH, tt)

            with gp.Fori(0, CH - 1) as c:
                chunk(c, False)
            chunk(CH - 1, True)

        @block.scalar
        def _(act):
            def t_round(c):
                act.wait_ge(t_done, c + 1)
                nc.scalar.activation(t_stack[:], sel[:], ACT.Copy).then_inc(t_hi, 1)

            def s_read(c, tt):
                act.wait_ge(s0_done, c * TT + tt + 1)
                act.wait_ge(s_free, c * TT + tt + 1)
                nc.scalar.activation(s_tile[:, tt, :], up[tt % 2][:], ACT.Copy, scale=0.5).then_inc(s0_read, 1)

            def head(c):
                t_round(c)
                for tt in range(TT):
                    s_read(c, tt)

            def body(c, last):
                for it in range(IT):
                    act.wait_ge(up_done, c * IT + it + 1)
                    if it:
                        act.wait_ge(h_split, c * IT + it)
                    nc.scalar.activation(h[:], up[it % 2][:], ACT.Relu).then_inc(relu_done, 1)
                    if last and it == IT - 4:
                        act.wait_ge(ld_wqkv, 16)
                        nc.scalar.activation(wqkv_hi[:], wqkv_nat[:], ACT.Copy).then_inc(w_direct_hi, 1)
                    if last and it == IT - 1:
                        item_hi(act, NW)
                    act.wait_ge(h_masked, c * IT + it + 1)
                    if it >= 2:
                        act.wait_ge(down_done, c * IT + it - 1)
                    nc.scalar.activation(h_hi[:, it % 2, :], h[:], ACT.Copy).then_inc(h_hi_done, 1)
                for tt in range(TT):
                    rows_hi(act, c + 1, tt)
                act.wait_ge(down_done, c * IT + IT)
                act.wait_ge(w2_lo, IT)
                act.wait_ge(g_free, c + 1)
                for tt in range(TT):
                    nc.scalar.activation(g_tile[:, tt, :], acc[tt][:], ACT.Tanh, scale=0.5).then_inc(tanh_done, 1)

            for n in range(BEFORE_ROWS):
                item_hi(act, n)
            for tt in range(TT):
                rows_hi(act, 0, tt)
            for n in range(BEFORE_ROWS, BEFORE_MASK):
                item_hi(act, n)
            act.wait_ge(consts_dve, 13)
            act.wait_ge(ld_c2, 16)
            for q in range(4):
                last = nc.scalar.activation(c2_rep_q[:, :, q, 0:RANK], c2_nat, ACT.Copy)
            last.then_inc(c2_wide, 1)
            for n in range(BEFORE_MASK, BEFORE_S):
                item_hi(act, n)
            t_round(0)
            for tt in range(TT):
                s_read(0, tt)
                for n in AFTER_S[tt]:
                    item_hi(act, n)
            with act.Fori(0, CH - 1) as c:
                body(c, False)
                head(c + 1)
            body(CH - 1, True)

            def probs_exp(c, tt):
                act.wait_ge(neg_max, c * TT + tt + 1)
                act.wait_ge(silu_done, (c + CH - 1) * TT + tt + 1)
                nc.scalar.activation(probs[:, tt, :], sc[tt % 2][:], ACT.Exp, bias=s_neg[:, tt:tt + 1], scale=QK_SCALE,
                                     accum_out=p_sum[:, tt:tt + 1]).then_inc(exp_done, 1)

            def prods_hi(c, kt):
                act.wait_ge(prod_done, c * KE + kt + 1)
                nc.scalar.activation(prod_hi[:, kt, :], prod[:, kt % 2, :], ACT.Copy).then_inc(prod_hi_done, 1)

            def probs_hi(c, kt):
                act.wait_ge(p_tr, c * TT + kt + 1)
                nc.scalar.activation(pT_hi[:, kt, :], tr[kt % 2][:], ACT.Copy).then_inc(p_hi_done, 1)

            def gate_tanh(c, tt):
                act.wait_ge(y_read, (c + 1) * TT + tt + 1)
                nc.scalar.activation(probs[:, tt, :], g_tile[:, tt, :], ACT.Tanh, scale=0.5).then_inc(tanh_done, 1)

            def chunk(c, is_first, last):
                act.wait_ge(proj_done, c * 4 + 1)
                nc.scalar.activation(logits, pj[0][R:R + E, :], ACT.Copy).then_inc(logits_out, 1)
                for j in range(EPT):
                    last_read = nc.scalar.activation(res[j * R:(j + 1) * R, :], pj[0][0:R, :], ACT.Copy)
                last_read.then_inc(proj_read, 1)
                act.wait_ge(route_step, c * NROUTE + 2)
                nc.scalar.activation(gate_p[:], gate_p[:], ACT.Exp).then_inc(route_exp, 1)
                for j, src in enumerate((pj[1], sc[0], sc[1])):
                    if j == 2:
                        act.wait_ge(comb_tr, c + 1)
                        nc.scalar.activation(combT[:], tr[0][0:2 * Q, :], ACT.Copy).then_inc(comb_hi, 1)
                    act.wait_ge(proj_done, c * 4 + j + 2)
                    nc.scalar.activation(qkv[:, j, :], src[:], ACT.Identity, bias=bqkv_col[:, j:j + 1]).then_inc(proj_read, 1)
                    if j < 2:
                        act.wait_ge(proj_read, c * 4 + j + 2)
                        nc.scalar.activation(qk_hi[:, j, :], qkv[:, j, :], ACT.Copy).then_inc(qk_hi_done, 1)
                    if is_first:
                        for n in LATE_GROUPS[j]:
                            item_hi(act, n)
                if is_first:
                    nc.scalar.activation(wo_hi[:], wo_nat[:], ACT.Copy).then_inc(w_direct_hi, 1)
                probs_exp(c, 0)
                act.wait_ge(v_tr, c + 1)
                nc.scalar.activation(v_hi[:], tr[1][:].rearrange("p (t d) -> p t d", t=TT), ACT.Copy).then_inc(v_hi_done, 1)
                probs_exp(c, 1)
                prods_hi(c, 0)
                prods_hi(c, 1)
                probs_exp(c, 2)
                probs_exp(c, 3)
                prods_hi(c, 2)
                prods_hi(c, 3)
                prods_hi(c, 4)
                prods_hi(c, 5)
                probs_hi(c, 0)
                probs_hi(c, 1)
                prods_hi(c, 6)
                prods_hi(c, 7)
                probs_hi(c, 2)
                probs_hi(c, 3)
                act.wait_ge(pv_done, c + 1)
                nc.scalar.activation(at_hi[:], sc[0][:], ACT.Copy).then_inc(a_hi_done, 1)
                for tt in range(3):
                    gate_tanh(c, tt)
                if not last:
                    for tt in range(TT):
                        rows_hi(act, c + CH + 1, tt)
                gate_tanh(c, 3)

            chunk(0, True, False)
            with act.Fori(1, CH - 1) as c:
                chunk(c, False, False)
            chunk(CH - 1, False, True)

        @block.vector
        def _(dve):
            nc.vector.memset(restart[:], 2.0).then_inc(consts_dve, 1)
            nc.vector.memset(restart_e[:], 2.0).then_inc(consts_dve, 1)
            nc.vector.memset(c1_hi[:].bitcast(F32), 0.0).then_inc(consts_dve, 1)
            nc.vector.memset(c1_lo[:].bitcast(F32), 0.0).then_inc(consts_dve, 1)
            nc.vector.memset(c2_rep, 0.0).then_inc(consts_dve, 1)
            nc.vector.memset(seg_ones, 0.0).then_inc(consts_dve, 1)
            nc.vector.memset(comb[:], 0.0).then_inc(consts_dve, 1)
            dve.wait_ge(consts_dve, 7)
            nc.vector.memset(restart[:].rearrange("p (s n) -> p s n", n=SEG)[:, :, 0:1], 0.0).then_inc(consts_dve, 1)
            nc.vector.memset(restart_e[:].rearrange("p (s n) -> p s n", n=E)[:, :, 0:1], 0.0).then_inc(consts_dve, 1)
            for q in range(4):
                nc.vector.memset(h[q * Q:(q + 1) * Q, q * Q:(q + 1) * Q], 1.0).then_inc(consts_dve, 1)
            dve.sem_inc(y_read, TT)
            dve.sem_inc(o_read, TT)
            for n in range(5):
                item_lo(dve, n)
            for tt in range(TT):
                rows_stats(dve, 0, tt)
            dve.wait_ge(stats_in, TT)
            rows_moments()
            for n in range(5, BEFORE_ROWS):
                item_lo(dve, n)
            rows_norm(dve, 0)
            for tt in range(2):
                rows_lo(dve, 0, tt)
            dve.wait_ge(ld_mask, 16)
            with nc.allow_low_precision(reason="counts of ones"):
                nc.vector.reduce_sum(row_cnt[:, 0:TT * MB].rearrange("p (t n) -> p t n", t=TT),
                                     mask_nat[:].rearrange("p t (n s) -> p t n s", s=SEG), AX.X).then_inc(mask_sum, 1)
            for tt in range(2, TT):
                rows_lo(dve, 0, tt)
            for n in range(BEFORE_ROWS, BEFORE_MASK):
                item_lo(dve, n)

            def t_rest(c):
                dve.wait_ge(t_hi, c + 1)
                nc.vector.tensor_tensor(t_stack[2 * Q:P, :], sel[2 * Q:P, :], t_stack[2 * Q:P, :].bitcast(F32),
                                        ALU.subtract).then_inc(t_split, 1)

            def select(c, p, tt):
                n = p * TT + tt
                segs = PW[p] // SEG
                got = sel[:, 0:PW[p]].rearrange("p (s n) -> p s n", n=SEG)
                dve.wait_ge(sel_done, c * NSEL + n + 1)
                nc.vector.reduce_max(seg_top[:, 0:segs], got, AX.X).then_inc(seg_max, 1)
                dve.wait_ge(seg_max, c * NSEL + n + 1)
                nc.vector.tensor_tensor(eq[:, 0:PW[p]].rearrange("p (s n) -> p s n", n=SEG), got,
                                        seg_top[:, 0:segs, None].to_broadcast([P, segs, SEG]),
                                        ALU.is_equal).then_inc(sel_eq, 1)
                dve.wait_ge(sel_eq, c * NSEL + n + 1)
                if tt == 0 and p >= 2:
                    dve.wait_ge(first_tr, c * IT + 4 * (p - 1))
                nc.vector.tensor_tensor_scan(counts[:, p % 2, tt, 0:PW[p]], restart[:, 0:PW[p]], eq[:, 0:PW[p]], 0.0,
                                             ALU.mult, ALU.add).then_inc(sel_count, 1)

            def head(c):
                t_rest(c)
                for tt in range(TT - 1):
                    select(c, 0, tt)

            def body(c, last):
                select(c, 0, TT - 1)
                for it in range(IT):
                    if it // 4 + 1 < PIECES:
                        select(c, it // 4 + 1, it % 4)
                    if last and it == IT - 1:
                        item_lo(dve, NW)
                    dve.wait_ge(relu_done, c * IT + it + 1)
                    dve.wait_ge(first_tr, c * IT + it + 1)
                    nc.vector.scalar_tensor_tensor(h[:], first, 1.0, h[:], ALU.is_equal, ALU.mult).then_inc(h_masked, 1)
                    if IT - 8 <= it < IT - 4:
                        rows_stats(dve, c + 1, it - (IT - 8))
                    if it == IT - 4:
                        dve.wait_ge(stats_in, (c + 1) * TT + TT)
                    dve.wait_ge(h_hi_done, c * IT + it + 1)
                    nc.vector.tensor_tensor(h_lo[:, it % 2, :], h[:], h_hi[:, it % 2, :].bitcast(F32),
                                            ALU.subtract).then_inc(h_split, 1)
                    if it == IT - 4:
                        rows_moments()
                    if last and it == IT - 3:
                        dve.wait_ge(w_direct_hi, 1)
                        nc.vector.tensor_tensor(wqkv_lo[:], wqkv_nat[:], wqkv_hi[:].bitcast(F32), ALU.subtract).then_inc(w_direct_lo, 1)
                    if it == IT - 2:
                        rows_norm(dve, c + 1)
                for tt in range(TT):
                    rows_lo(dve, c + 1, tt)
                for tt in range(TT):
                    dve.wait_ge(tanh_done, c * TT + tt + 1)
                    nc.vector.scalar_tensor_tensor(g_tile[:, tt, :], g_tile[:, tt, :], 1.0, acc[tt][:],
                                                   ALU.add, ALU.mult).then_inc(silu_done, 1)

            dve.wait_ge(mask_cnt, 1)
            nc.vector.tensor_scalar(on[:, 0:TT * MB], banks[0][:, 0:TT * MB], 0.0, None, ALU.is_gt).then_inc(mask_on, 1)
            for n in range(BEFORE_MASK, BEFORE_S):
                item_lo(dve, n)
            t_rest(0)
            for tt in range(TT):
                if tt:
                    select(0, 0, tt - 1)
                for n in AFTER_S[tt]:
                    item_lo(dve, n)
            with dve.Fori(0, CH - 1) as c:
                body(c, False)
                head(c + 1)
            body(CH - 1, True)

            def wide(a):
                return a[:, :, None].to_broadcast([P, TT, E])

            def route(c, is_first):
                steps = [0]

                def step(ins):
                    steps[0] += 1
                    ins.then_inc(route_step, 1)
                    if is_first and steps[0] in (3, 7, 11, 15):
                        item_lo(dve, LATE_GROUPS[0][(steps[0] - 3) // 4])
                    dve.wait_ge(route_step, c * NROUTE + steps[0])

                v = nc.vector
                got = tr[0][:, 0:TT * E].rearrange("p (t e) -> p t e", t=TT)
                dve.wait_ge(route_in, c + 1)
                step(v.reduce_max(row_a[:], got, AX.X))
                step(v.tensor_tensor(gate_p[:], got, wide(row_a), ALU.subtract))
                dve.wait_ge(route_exp, c + 1)
                step(v.reduce_sum(row_a[:], gate_p[:], AX.X))
                step(v.reciprocal(row_a[:], row_a[:]))
                step(v.tensor_tensor(gate_p[:], gate_p[:], wide(row_a), ALU.mult))
                for j in range(2):
                    step(v.reduce_max(top_p[:, j, :], gate_p[:], AX.X))
                    step(v.tensor_tensor(is_top[:], gate_p[:], wide(top_p[:, j, :]), ALU.is_equal))
                    step(v.tensor_tensor_scan(top_cnt[:].rearrange("p t e -> p (t e)"), restart_e[:],
                                              is_top[:].rearrange("p t e -> p (t e)"), 0.0, ALU.mult, ALU.add))
                    step(v.scalar_tensor_tensor(top_w[:, j], top_cnt[:], 1.0, gate_p[:], ALU.is_equal, ALU.mult))
                    if j == 0:
                        step(v.tensor_tensor(gate_p[:], gate_p[:], top_w[:, 0], ALU.subtract))
                step(v.scalar_tensor_tensor(row_a[:], top_p[:, 0, :], 1e-6, top_p[:, 1, :], ALU.add, ALU.add))
                step(v.reciprocal(row_a[:], row_a[:]))
                step(v.tensor_tensor(top_w[:, 0], top_w[:, 0], top_w[:, 1], ALU.add))
                step(v.scalar_tensor_tensor(comb[:, :, 0:E], top_w[:, 0], SCALING, wide(row_a), ALU.mult, ALU.mult))
                step(v.tensor_copy(comb[:, :, Q:Q + E], comb[:, :, 0:E]))
                assert steps[0] == NROUTE

            def score_peak(c, tt):
                dve.wait_ge(score_done, c * TT + tt + 1)
                nc.vector.reduce_max(s_max[:, tt:tt + 1], sc[tt % 2][:], AX.X).then_inc(score_max, 1)
                dve.wait_ge(score_max, c * TT + tt + 1)
                nc.vector.tensor_scalar(s_neg[:, tt:tt + 1], s_max[:, tt:tt + 1], -QK_SCALE, None, ALU.mult).then_inc(neg_max, 1)

            def prods(c, kt):
                dve.wait_ge(spread_done, c * KE + kt + 1)
                if kt >= 2:
                    dve.wait_ge(prod_split, c * KE + kt - 1)
                nc.vector.tensor_tensor(prod[:, kt % 2, :], pj[kt % 2][:], res[:], ALU.mult).then_inc(prod_done, 1)

            def probs_lo(c, kt):
                dve.wait_ge(p_hi_done, c * TT + kt + 1)
                nc.vector.tensor_tensor(pT_lo[:, kt, :], tr[kt % 2][:], pT_hi[:, kt, :].bitcast(F32),
                                        ALU.subtract).then_inc(p_split, 1)

            def two_prods(c, kt):
                prods(c, kt)
                prods(c, kt + 1)

            def y_out(c, tt):
                dve.wait_ge(y_done, c * TT + tt + 1)
                if tt == 0:
                    dve.wait_ge(g_free, c + CH + 1)
                nc.vector.tensor_tensor(g_tile[:, tt, :], y[tt % 2][:], bias_b[:], ALU.add).then_inc(y_read, 1)

            def s_out(c, tt):
                dve.wait_ge(o_done, c * TT + tt + 1)
                dve.wait_ge(s_free, (c + CH) * TT + tt + 1)
                nc.vector.scalar_tensor_tensor(s_tile[:, tt, :], sc[(tt + 1) % 2][:], p_inv[:, tt:tt + 1], bias_a[:],
                                               ALU.mult, ALU.add).then_inc(o_read, 1)

            def silu(c, tt):
                dve.wait_ge(tanh_done, (c + CH) * TT + tt + 1)
                nc.vector.scalar_tensor_tensor(g_tile[:, tt, :], probs[:, tt, :], 1.0, g_tile[:, tt, :],
                                               ALU.add, ALU.mult).then_inc(silu_done, 1)

            def chunk(c, is_first, last):
                route(c, is_first)
                for j in range(2):
                    dve.wait_ge(qk_hi_done, c * 2 + j + 1)
                    nc.vector.tensor_tensor(qk_lo[:, j, :], qkv[:, j, :], qk_hi[:, j, :].bitcast(F32),
                                            ALU.subtract).then_inc(qk_split, 1)
                    if is_first:
                        for n in LATE_GROUPS[1 + j]:
                            item_lo(dve, n)
                if is_first:
                    dve.wait_ge(w_direct_hi, 2)
                    nc.vector.tensor_tensor(wo_lo[:], wo_nat[:], wo_hi[:].bitcast(F32), ALU.subtract).then_inc(w_direct_lo, 1)
                    dve.wait_ge(ld_bo, 16)
                    nc.vector.tensor_scalar(bias_a[:], bias_a[:], 0.5, None, ALU.mult).then_inc(w_direct_lo, 1)
                    dve.wait_ge(w_direct_lo, 3)
                dve.wait_ge(comb_hi, c + 1)
                nc.vector.tensor_tensor(combT[Q:2 * Q, :], tr[0][Q:2 * Q, :], combT[Q:2 * Q, :].bitcast(F32),
                                        ALU.subtract).then_inc(comb_split, 1)
                score_peak(c, 0)
                dve.wait_ge(v_hi_done, c + 1)
                nc.vector.tensor_tensor(v_lo[:], tr[1][:].rearrange("p (t d) -> p t d", t=TT), v_hi[:].bitcast(F32),
                                        ALU.subtract).then_inc(v_split, 1)
                score_peak(c, 1)
                two_prods(c, 0)
                score_peak(c, 2)
                score_peak(c, 3)
                two_prods(c, 2)
                two_prods(c, 4)
                probs_lo(c, 0)
                probs_lo(c, 1)
                two_prods(c, 6)
                probs_lo(c, 2)
                probs_lo(c, 3)
                dve.wait_ge(exp_done, c * TT + TT)
                nc.vector.reciprocal(p_inv[:], p_sum[:]).then_inc(inv_step, 1)
                dve.wait_ge(inv_step, c * 2 + 1)
                nc.vector.tensor_scalar(p_inv[:], p_inv[:], 0.5, None, ALU.mult).then_inc(inv_step, 1)
                dve.wait_ge(a_hi_done, c + 1)
                nc.vector.tensor_tensor(at_lo[:], sc[0][:], at_hi[:].bitcast(F32), ALU.subtract).then_inc(a_split, 1)
                dve.wait_ge(inv_step, c * 2 + 2)
                for tt in range(TT):
                    if tt == TT - 1 and not last:
                        for t in range(TT):
                            rows_lo(dve, c + CH + 1, t)
                    y_out(c, tt)
                    s_out(c, tt)
                    silu(c, tt)
                    if tt == 0 and not last:
                        for t in range(TT):
                            rows_stats(dve, c + CH + 1, t)
                        dve.wait_ge(stats_in, (c + CH + 1) * TT + TT)
                    if tt == 1 and not last:
                        rows_moments()
                        rows_norm(dve, c + CH + 1)

            chunk(0, True, False)
            with dve.Fori(1, CH - 1) as c:
                chunk(c, False, False)
            chunk(CH - 1, False, True)

        @block.tensor
        def _(pe):
            def rank_product():
                three(sel[:], [(c1_hi[:, k, :], c1_lo[:, k, :], xT_hi[:, k, :], xT_lo[:, k, :])
                               for k in range(KD)]).then_inc(t_done, 1)

            def s_product(c, tt):
                if tt >= 2:
                    pe.wait_ge(s0_read, c * TT + tt - 1)
                three(up[tt % 2][:], [(xT_hi[:, k, rows(tt)], xT_lo[:, k, rows(tt)], ws_hi[:, k, :], ws_lo[:, k, :])
                                      for k in range(KD)]).then_inc(s0_done, 1)

            def select(c, p, tt):
                if p == 0 and tt == 0:
                    pe.wait_ge(t_split, c + 1)
                else:
                    pe.wait_ge(sel_eq, c * NSEL + p * TT + tt)
                if tt == 0:
                    pe.wait_ge(w_lo, w_at["c2", TT * p] + 1)
                nc.tensor.matmul(sel[:, 0:PW[p]], t_stack[:, rows(tt)],
                                 c2_stack[:, p * BANK:p * BANK + PW[p]], start=True, stop=True).then_inc(sel_done, 1)

            def up_product(c, it):
                if it < 2:
                    pe.wait_ge(s0_read, c * TT + TT - 1 + it)
                else:
                    pe.wait_ge(relu_done, c * IT + it - 1)
                pe.wait_ge(w_lo, w_at["w1", it] + 1)
                three(up[it % 2][:], [(w1T_hi[:, k, rows(it)], w1T_lo[:, k, rows(it)], xT_hi[:, k, :], xT_lo[:, k, :])
                                      for k in range(KD)]).then_inc(up_done, 1)

            def transpose_counts(c, it):
                pe.wait_ge(sel_count, c * NSEL + (it // 4 + 1) * TT)
                if it:
                    pe.wait_ge(h_masked, c * IT + it)
                for tt in range(TT):
                    last = nc.tensor.transpose(first[:, rows(tt)], counts[:, it // 4 % 2, tt, rows(it % 4)], ident_bf[:])
                last.then_inc(first_tr, 1)

            def down_product(it, tts):
                pe.wait_ge(w2_lo, it + 1)
                for tt in tts:
                    last = three(acc[tt][:], [(h_hi[:, it % 2, rows(tt)], h_lo[:, it % 2, rows(tt)],
                                               w2_hi_t[:, it, :], w2_lo_t[:, it, :])], start=(it == 0), stop=(it == IT - 1))
                return last

            def head(c):
                pe.wait_ge(xT_done, c * TT + TT)
                rank_product()
                s_product(c, 0)
                s_product(c, 1)
                select(c, 0, 0)
                s_product(c, 2)
                select(c, 0, 1)
                s_product(c, 3)
                select(c, 0, 2)

            def body(c, last):
                up_product(c, 0)
                select(c, 0, 3)
                for it in range(1, IT + 1):
                    if it < IT:
                        up_product(c, it)
                        if (it - 1) // 4 + 1 < PIECES:
                            select(c, (it - 1) // 4 + 1, (it - 1) % 4)
                        elif last and it == IT - 1:
                            pe.wait_ge(sel_eq, c * NSEL + NSEL)
                            item_in(pe, NW)
                    else:
                        pe.wait_ge(relu_done, c * IT + IT - 1)
                        transpose_rows(pe, c + 1, 0)
                    transpose_counts(c, it - 1)
                    if it >= 2:
                        pe.wait_ge(h_split, c * IT + it - 1)
                        down_product(it - 2, range(TT)).then_inc(down_done, 1)
                pe.wait_ge(relu_done, c * IT + IT)
                transpose_rows(pe, c + 1, 1)
                pe.wait_ge(xT_done, (c + 1) * TT + 1)
                transpose_rows(pe, c + 1, 2)
                pe.wait_ge(h_split, c * IT + IT)
                down_product(IT - 1, range(0, 2))
                pe.wait_ge(xT_done, (c + 1) * TT + 2)
                transpose_rows(pe, c + 1, 3)
                down_product(IT - 1, range(2, TT)).then_inc(down_done, 1)

            pe.wait_ge(consts_gp, 6)
            for n in range(BEFORE_ROWS):
                item_in(pe, n)
            for tt in range(TT):
                if tt >= 2:
                    pe.wait_ge(xT_done, tt - 1)
                transpose_rows(pe, 0, tt)
            for n in range(BEFORE_ROWS, BEFORE_MASK):
                item_in(pe, n)
            pe.wait_ge(xT_done, TT)
            pe.wait_ge(mask_sum, 1)
            nc.tensor.matmul(banks[0][:, 0:TT * D // SEG], seg_ones, row_cnt[:, 0:TT * D // SEG],
                             start=True, stop=True).then_inc(mask_cnt, 1)
            rank_product()
            for n in range(BEFORE_MASK, BEFORE_S):
                item_in(pe, n)
            pe.wait_ge(w_lo, BEFORE_S)
            for tt in range(TT):
                s_product(0, tt)
                if tt:
                    select(0, 0, tt - 1)
                for n in AFTER_S[tt]:
                    item_in(pe, n)
            with pe.Fori(0, CH - 1) as c:
                body(c, False)
                head(c + 1)
            body(CH - 1, True)

            def scores(c, tt):
                if tt >= 2:
                    pe.wait_ge(exp_done, c * TT + tt - 1)
                three(sc[tt % 2][:], [(qk_hi[:, 0, rows(tt)], qk_lo[:, 0, rows(tt)], qk_hi[:, 1, :], qk_lo[:, 1, :])])\
                    .then_inc(score_done, 1)

            def spread(c, kt):
                if kt < 2:
                    pe.wait_ge(proj_read, c * 4 + kt + 1)
                else:
                    pe.wait_ge(prod_done, c * KE + kt - 1)
                nc.tensor.matmul(pj[kt % 2][:], pick[:, kt, :], combT[:], start=True, stop=True).then_inc(spread_done, 1)

            def base(c, tt):
                pe.wait_ge(y_read, c * TT + TT + tt - 1)
                three(y[tt % 2][:], [(xT_hi[:, k, rows(tt)], xT_lo[:, k, rows(tt)], base_hi[:, k, :], base_lo[:, k, :])
                                     for k in range(KD)], stop=False)

            def lora(c, tt, k0, k1):
                pe.wait_ge(prod_split, c * KE + k1)
                last = three(y[tt % 2][:], [(prod_hi[:, k, rows(tt)], prod_lo[:, k, rows(tt)], b_hi[:, k, :], b_lo[:, k, :])
                                            for k in range(k0, k1)], start=False, stop=(k1 == KE))
                if k1 == KE:
                    last.then_inc(y_done, 1)

            def probs_transpose(c, kt):
                if kt == 0:
                    pe.wait_ge(exp_done, c * TT + TT)
                elif kt == 1:
                    pe.wait_ge(v_split, c + 1)
                else:
                    pe.wait_ge(p_split, c * TT + kt - 1)
                for tt in range(TT):
                    last = nc.tensor.transpose(tr[kt % 2][:, rows(tt)], probs[:, tt, rows(kt)], ident[:])
                last.then_inc(p_tr, 1)

            def project(c, tt):
                if tt >= 2:
                    pe.wait_ge(o_read, c * TT + TT + tt - 1)
                three(sc[(tt + 1) % 2][:], [(at_hi[:, rows(tt)], at_lo[:, rows(tt)], wo_hi[:], wo_lo[:])]).then_inc(o_done, 1)

            def chunk(c, is_first, last_chunk):
                g = c + CH
                pe.wait_ge(xT_done, g * TT + TT)
                three(pj[0][0:R + E, :], [(a_hi[:, k, :], a_lo[:, k, :], xT_hi[:, k, :], xT_lo[:, k, :]) for k in range(KD)]).then_inc(proj_done, 1)
                if is_first:
                    pe.wait_ge(w_direct_lo, 1)
                for j, dst in enumerate((pj[1], sc[0], sc[1])):
                    if j == 1:
                        pe.wait_ge(o_read, c * TT + TT)
                    d = slice(j * DH, (j + 1) * DH)
                    parts = [(wqkv_hi[:, k, d], wqkv_lo[:, k, d], xT_hi[:, k, :], xT_lo[:, k, :]) for k in range(KD)]
                    if j == 0:
                        three(dst[:], parts[0:1], stop=False)
                        pe.wait_ge(logits_out, c + 1)
                        three(dst[:], parts[1:2], start=False, stop=False)
                        for tt in range(TT):
                            routed = nc.tensor.transpose(tr[0][:, tt * E:(tt + 1) * E], logits[:, rows(tt)],
                                                         ident[R:R + E, R:R + E])
                        routed.then_inc(route_in, 1)
                        three(dst[:], parts[2:], start=False).then_inc(proj_done, 1)
                    elif j == 1:
                        three(dst[:], parts).then_inc(proj_done, 1)
                    else:
                        three(dst[:], parts[0:2], stop=False)
                        pe.wait_ge(route_step, c * NROUTE + NROUTE)
                        three(dst[:], parts[2:3], start=False, stop=False)
                        for tt in range(TT):
                            combined = nc.tensor.transpose(tr[0][0:2 * Q, rows(tt)], comb[:, tt, :], ident[:])
                        combined.then_inc(comb_tr, 1)
                        three(dst[:], parts[3:], start=False).then_inc(proj_done, 1)
                    if is_first:
                        if j == 0:
                            pe.wait_ge(silu_done, CH * TT)
                            pe.wait_ge(pick_ready, 4)
                        for n in LATE_GROUPS[j]:
                            item_in(pe, n)
                pe.wait_ge(qk_split, c * 2 + 2)
                scores(c, 0)
                pe.wait_ge(proj_read, c * 4 + 4)
                if is_first:
                    pe.wait_ge(w_lo, len(items))
                for tt in range(TT):
                    last = nc.tensor.transpose(tr[1][:, rows(tt)], qkv[:, 2, rows(tt)], ident[:])
                last.then_inc(v_tr, 1)
                pe.wait_ge(comb_split, c + 1)
                spread(c, 0)
                spread(c, 1)
                scores(c, 1)
                base(c, 0)
                scores(c, 2)
                scores(c, 3)
                spread(c, 2)
                spread(c, 3)
                base(c, 1)
                spread(c, 4)
                spread(c, 5)
                probs_transpose(c, 0)
                probs_transpose(c, 1)
                lora(c, 0, 0, 4)
                spread(c, 6)
                spread(c, 7)
                probs_transpose(c, 2)
                probs_transpose(c, 3)
                lora(c, 1, 0, 4)
                pe.wait_ge(p_split, c * TT + TT)
                three(sc[0][:], [(v_hi[:, k, :], v_lo[:, k, :], pT_hi[:, k, :], pT_lo[:, k, :]) for k in range(TT)]).then_inc(pv_done, 1)
                lora(c, 0, 4, 8)
                pe.wait_ge(a_split, c + 1)
                project(c, 0)
                lora(c, 1, 4, 8)
                project(c, 1)
                base(c, 2)
                lora(c, 2, 0, 8)
                project(c, 2)
                base(c, 3)
                if not last_chunk:
                    transpose_rows(pe, g + 1, 0)
                    transpose_rows(pe, g + 1, 1)
                lora(c, 3, 0, 4)
                if not last_chunk:
                    for tt in (2, 3):
                        pe.wait_ge(xT_done, (g + 1) * TT + tt - 1)
                        transpose_rows(pe, g + 1, tt)
                lora(c, 3, 4, 8)
                project(c, 3)

            chunk(0, True, False)
            with pe.Fori(1, CH - 1) as c:
                chunk(c, False, False)
            chunk(CH - 1, False, True)


_INS = ["L0_attn_data", "L0_attn_mask", "L0_attn_weight", "L0_attn_bias", "L0_ffn_c1_w", "L0_ffn_c2_w", "L0_ffn_w1",
        "L0_ffn_w2t", "L1_attn_Wqkv", "L1_attn_bqkv", "L1_attn_Wo", "L1_attn_bo", "L1_ffn_base_w", "L1_ffn_base_b",
        "L1_ffn_A", "L1_ffn_B", "L1_ffn_router_w"]


def kernel(**inputs):
    import concourse.bacc as bacc
    from concourse.bass_utils import run_bass_kernel_spmd

    nc = bacc.Bacc("TRN2", target_bir_lowering=False, num_devices=1, dynamic_dma_scratch_size=1024)
    arrays, args = {}, []
    for name in _INS:
        a = np.ascontiguousarray(inputs[name])
        arrays[f"in_{name}"] = a
        args.append(nc.dram_tensor(f"in_{name}", a.shape, mybir.dt.from_np(a.dtype), kind="ExternalInput").ap())
    shape = arrays["in_L0_attn_data"].shape
    args.append(nc.dram_tensor("out", shape, F32, kind="ExternalOutput").ap())
    block_mask_ffn_then_attention_lora_kernel(nc, *args)
    r = run_bass_kernel_spmd(nc, [arrays], core_ids=[0])
    return r.results[0]["out"]
```

```python
from contextlib import ExitStack

import concourse.bass as bass
import numpy as np
from concourse import mybir

P = 128
BANK = 512

ALU = mybir.AluOpType
ACT = mybir.ActivationFunctionType
AX = mybir.AxisListType
F32 = mybir.dt.float32
F32R = mybir.dt.float32r
BF16 = mybir.dt.bfloat16
I32 = mybir.dt.int32


def block_mask_ffn_then_attention_lora_kernel(
    nc: bass.Bass,
    x_in: bass.AP,
    mask: bass.AP,
    w_s0: bass.AP,
    b_s0: bass.AP,
    c1_w: bass.AP,
    c2_w: bass.AP,
    w1: bass.AP,
    w2: bass.AP,
    wqkv: bass.AP,
    bqkv: bass.AP,
    wo: bass.AP,
    bo: bass.AP,
    base_w: bass.AP,
    base_b: bass.AP,
    lora_a: bass.AP,
    lora_b: bass.AP,
    router_w: bass.AP,
    out: bass.AP,
):
    B, S, D = x_in.shape
    INTER = w1.shape[0]
    RANK = c1_w.shape[0]
    DH = wo.shape[0]
    E, _, R = lora_b.shape
    SEG = 32
    KD = D // P
    TT = S // P
    IT = INTER // P
    CH = B
    PIECES = -(-INTER // BANK)
    PW = [min(BANK, INTER - p * BANK) for p in range(PIECES)]
    KE = E * R // P
    EPT = P // R
    SCALING = 32.0 / 64.0
    EPS = 1e-5
    QK_SCALE = float(DH) ** -0.5
    Q = P // 4
    assert D == BANK and S == BANK and DH == P and RANK <= Q and E <= Q and R * 2 == P and IT % 2 == 0

    x_rows = x_in.rearrange("b (t p) d -> b p t d", p=P)
    out_rows = out.rearrange("b (t p) d -> b p t d", p=P)
    mid = nc.dram_tensor("mid_state", (B, S, D), F32, kind="Internal").ap()
    mid_rows = mid.rearrange("b (t p) d -> b p t d", p=P)

    ctx = ExitStack()
    with ctx:
        def sem(name):
            return ctx.enter_context(nc.semaphore(name))

        class Span:

            def __init__(self, start):
                self.start = self.end = start

            def take(self, name, shape, dt=F32):
                t = nc.alloc_sbuf_tensor_at(name, shape, dt, offset=self.end)
                size = int(np.prod(shape[1:])) * mybir.dt.size(dt)
                self.end += -(-size // 32) * 32
                return t

        both = Span(-(-nc.sbuf_base // 64) * 64)
        ident = both.take("ident", [P, P])
        ident_bf = both.take("ident_bf", [P, P], BF16)
        restart = both.take("restart", [P, BANK], BF16)
        restart_e = both.take("restart_e", [P, TT * E])
        neg_half = both.take("neg_half", [P, TT])
        eps = both.take("eps", [P, TT])
        x_tile = both.take("x_tile", [P, TT, D])
        x_res = both.take("x_res", [P, TT, D])
        s_tile = both.take("s_tile", [P, TT, D])
        g_tile = both.take("g_tile", [P, TT, D])
        xT_hi = both.take("xT_hi", [P, KD, S], F32R)
        xT_lo = both.take("xT_lo", [P, KD, S], F32R)
        bn = both.take("bn", [P, TT, 6])
        mean_var = both.take("mean_var", [P, TT, 2])
        rstd = both.take("rstd", [P, TT])
        bias_a = both.take("bias_a", [P, D])
        bias_b = both.take("bias_b", [P, D])
        a_nat = both.take("a_nat", [P, D])
        bqkv_col = both.take("bqkv_col", [P, 3])
        comb = both.take("comb", [P, TT, 2 * Q])
        gate_p = both.take("gate_p", [P, TT, E])
        is_top = both.take("is_top", [P, TT, E])
        top_cnt = both.take("top_cnt", [P, TT, E])
        top_w = both.take("top_w", [P, 2, TT, E])
        row_a = both.take("row_a", [P, TT])
        top_p = both.take("top_p", [P, 2, TT])
        s_max = both.take("s_max", [P, TT])
        s_neg = both.take("s_neg", [P, TT])
        p_sum = both.take("p_sum", [P, TT])
        p_inv = both.take("p_inv", [P, TT])

        span_c = Span(both.end)
        c1_stack = span_c.take("c1_stack", [P, KD, P], F32R)
        c1_nat = span_c.take("c1_nat", [RANK, D])
        next_c = Span(span_c.start)
        wqkv_nat = next_c.take("wqkv_nat", [P, KD, 3 * DH])
        next_c2 = Span(span_c.start)
        res = next_c2.take("res", [P, S])
        prod = next_c2.take("prod", [P, 3, S])

        span_s = Span(max(span_c.end, next_c.end, next_c2.end))
        ws_hi = span_s.take("ws_hi", [P, KD, D], F32R)
        ws_lo = span_s.take("ws_lo", [P, KD, D], F32R)
        next_s = Span(span_s.start)
        wqkv_hi = next_s.take("wqkv_hi", [P, KD, 3 * DH], F32R)
        wqkv_lo = next_s.take("wqkv_lo", [P, KD, 3 * DH], F32R)
        a_hi = next_s.take("a_hi", [P, KD, R + E], F32R)
        a_lo = next_s.take("a_lo", [P, KD, R + E], F32R)

        span_1 = Span(max(span_s.end, next_s.end))
        w1T_hi = span_1.take("w1T_hi", [P, KD, INTER], F32R)
        w1T_lo = span_1.take("w1T_lo", [P, KD, INTER], F32R)
        next_1 = Span(span_1.start)
        base_hi = next_1.take("base_hi", [P, KD, D], F32R)
        base_lo = next_1.take("base_lo", [P, KD, D], F32R)
        wo_hi = next_1.take("wo_hi", [P, D], F32R)
        wo_lo = next_1.take("wo_lo", [P, D], F32R)
        pick = next_1.take("pick", [2 * Q, KE, P], F32R)
        next_1b = Span(next_1.end)
        base_nat = next_1.take("base_nat", [P, TT, D])
        wo_nat = next_1.take("wo_nat", [P, D])
        pick_f = next_1.take("pick_f", [2 * Q, KE, P])
        b_nat = next_1.take("b_nat", [P, TT, E, R])
        prod_hi = next_1b.take("prod_hi", [P, KE, S], F32R)
        prod_lo = next_1b.take("prod_lo", [P, KE, S], F32R)

        span_2 = Span(max(span_1.end, next_1.end, next_1b.end))
        w2_hi_t = span_2.take("w2_hi_t", [P, IT, D], F32R)
        w2_lo_t = span_2.take("w2_lo_t", [P, IT, D], F32R)
        c2_stack = span_2.take("c2_stack", [P, INTER], F32R)
        t_stack = span_2.take("t_stack", [P, S], F32R)
        eq = span_2.take("eq", [P, BANK], BF16)
        counts = span_2.take("counts", [P, 2, TT, BANK], BF16)
        seg_top = span_2.take("seg_top", [P, BANK // SEG])
        h = span_2.take("h", [P, S])
        before_h = Span(span_2.end)
        h_hi = span_2.take("h_hi", [P, 2, S], F32R)
        h_lo = span_2.take("h_lo", [P, 2, S], F32R)
        mask_nat = before_h.take("mask_nat", [P, TT, D], I32)
        rest_2 = Span(span_2.start)
        pT_hi = rest_2.take("pT_hi", [P, TT, S], F32R)
        pT_lo = rest_2.take("pT_lo", [P, TT, S], F32R)
        b_hi = rest_2.take("b_hi", [P, KE, D], F32R)
        b_lo = rest_2.take("b_lo", [P, KE, D], F32R)
        probs = rest_2.take("probs", [P, TT, S])
        qkv = rest_2.take("qkv", [P, 3, S])
        qk_hi = rest_2.take("qk_hi", [P, 2, S], F32R)
        qk_lo = rest_2.take("qk_lo", [P, 2, S], F32R)
        v_hi = rest_2.take("v_hi", [P, TT, DH], F32R)
        v_lo = rest_2.take("v_lo", [P, TT, DH], F32R)
        at_hi = rest_2.take("at_hi", [P, S], F32R)
        at_lo = rest_2.take("at_lo", [P, S], F32R)
        combT = rest_2.take("combT", [2 * Q, S], F32R)
        assert max(span_2.end, rest_2.end, before_h.end) <= nc.sbuf_usable_end

        banks = [ctx.enter_context(nc.psum_tensor(f"bank{i}", [P, BANK], F32)) for i in range(8)]

        consts_gp = sem("consts_gp")
        consts_dve = sem("consts_dve")
        ld_x_first = sem("ld_x_first")
        ld_x = sem("ld_x")
        ld_res = sem("ld_res")
        st_rows = sem("st_rows")
        ld_c1 = sem("ld_c1")
        ld_c2 = sem("ld_c2")
        ld_mask = sem("ld_mask")
        ld_ws0 = sem("ld_ws0")
        ld_w = [sem(f"ld_w_{i}") for i in range(7)]
        ld_bias = sem("ld_bias")
        ld_l1_small = sem("ld_l1_small")
        ld_wqkv = sem("ld_wqkv")
        ld_bo = sem("ld_bo")
        ld_base = sem("ld_base")
        ld_b = sem("ld_b")
        w_tr = sem("w_tr")
        w_hi = sem("w_hi")
        w_lo = sem("w_lo")
        w2_hi = sem("w2_hi")
        w2_lo = sem("w2_lo")
        mask_sum = sem("mask_sum")
        mask_cnt = sem("mask_cnt")
        mask_on = sem("mask_on")
        ws0_masked = sem("ws0_masked")
        c2_wide = sem("c2_wide")
        half_bias = sem("half_bias")
        stats_in = sem("stats_in")
        stats = sem("stats")
        rstd_step = sem("rstd_step")
        xn_ready = sem("xn_ready")
        xT_tr = sem("xT_tr")
        xT_hi_done = sem("xT_hi_done")
        xT_done = sem("xT_done")
        t_done = sem("t_done")
        t_hi = sem("t_hi")
        t_split = sem("t_split")
        s0_done = sem("s0_done")
        s0_read = sem("s0_read")
        s_biased = sem("s_biased")
        sel_done = sem("sel_done")
        seg_max = sem("seg_max")
        sel_eq = sem("sel_eq")
        sel_count = sem("sel_count")
        first_tr = sem("first_tr")
        up_done = sem("up_done")
        relu_done = sem("relu_done")
        h_masked = sem("h_masked")
        h_hi_done = sem("h_hi_done")
        h_split = sem("h_split")
        down_done = sem("down_done")
        tanh_done = sem("tanh_done")
        silu_done = sem("silu_done")
        rows_done = sem("rows_done")

        s_free = sem("s_free")
        g_free = sem("g_free")
        w_direct_hi = sem("w_direct_hi")
        w_direct_lo = sem("w_direct_lo")
        wo_split = sem("wo_split")
        pick_ready = sem("pick_ready")
        logits_out = sem("logits_out")
        route_in = sem("route_in")
        route_step = sem("route_step")
        route_exp = sem("route_exp")
        comb_tr = sem("comb_tr")
        comb_hi = sem("comb_hi")
        comb_split = sem("comb_split")
        proj_done = sem("proj_done")
        proj_read = sem("proj_read")
        qk_hi_done = sem("qk_hi_done")
        qk_split = sem("qk_split")
        v_tr = sem("v_tr")
        v_hi_done = sem("v_hi_done")
        v_split = sem("v_split")
        score_done = sem("score_done")
        score_max = sem("score_max")
        neg_max = sem("neg_max")
        exp_done = sem("exp_done")
        inv_step = sem("inv_step")
        p_tr = sem("p_tr")
        p_hi_done = sem("p_hi_done")
        p_split = sem("p_split")
        pv_done = sem("pv_done")
        a_hi_done = sem("a_hi_done")
        a_split = sem("a_split")
        spread_done = sem("spread_done")
        prod_done = sem("prod_done")
        prod_hi_done = sem("prod_hi_done")
        prod_split = sem("prod_split")
        y_done = sem("y_done")
        y_read = sem("y_read")
        o_done = sem("o_done")
        o_read = sem("o_read")
        end_y_done = sem("end_y_done")
        end_g = sem("end_g")
        end_tanh = sem("end_tanh")
        end_gs = sem("end_gs")
        end_silu = sem("end_silu")
        end_done = sem("end_done")
        st_out = sem("st_out")

        def rows_bank(g, tt):
            return banks[(0, 1, 6, 0)[tt]] if isinstance(g, int) and g == 0 else banks[tt % 2]

        def transpose_rows(pe, g, tt):
            pe.wait_ge(xn_ready, g * TT + tt + 1)
            for k in range(KD):
                last = nc.tensor.transpose(rows_bank(g, tt)[:, k * P:(k + 1) * P],
                                           x_tile[:, tt, k * P:(k + 1) * P], ident[:])
            last.then_inc(xT_tr, 1)

        def rows_hi(act, g, tt):
            act.wait_ge(xT_tr, g * TT + tt + 1)
            nc.scalar.activation(xT_hi[:, :, tt * P:(tt + 1) * P],
                                 rows_bank(g, tt)[:].rearrange("p (k t) -> p k t", k=KD), ACT.Copy).then_inc(xT_hi_done, 1)

        def rows_lo(dve, g, tt):
            dve.wait_ge(xT_hi_done, g * TT + tt + 1)
            cols = slice(tt * P, (tt + 1) * P)
            nc.vector.tensor_tensor(xT_lo[:, :, cols], rows_bank(g, tt)[:].rearrange("p (k t) -> p k t", k=KD),
                                    xT_hi[:, :, cols].bitcast(F32), ALU.subtract).then_inc(xT_done, 1)

        def rows_stats(dve, g, tt):
            if tt == 0:
                dve.wait_ge(ld_x, g * 16 + 16)
            nc.vector.bn_stats(bn[:, tt, :], x_tile[:, tt, :]).then_inc(stats_in, 1)

        def rows_moments():
            for tt in range(TT):
                last = nc.vector.bn_aggr(mean_var[:, tt, :], bn[:, tt, :])
            last.then_inc(stats, 1)

        def rows_rstd(gp, g):
            gp.wait_ge(stats, g + 1)
            nc.gpsimd.tensor_tensor(rstd[:], mean_var[:, :, 1], eps[:], ALU.add).then_inc(rstd_step, 1)
            gp.wait_ge(rstd_step, g * 2 + 1)
            nc.gpsimd.tensor_tensor(rstd[:], rstd[:], neg_half[:], ALU.pow).then_inc(rstd_step, 1)

        def rows_norm(dve, g, tts=range(TT)):
            dve.wait_ge(rstd_step, g * 2 + 2)
            for tt in tts:
                nc.vector.tensor_scalar(x_tile[:, tt, :], x_tile[:, tt, :], mean_var[:, tt, 0:1],
                                        rstd[:, tt:tt + 1], ALU.subtract, ALU.mult).then_inc(xn_ready, 1)

        def gate(gp, g, tt):
            gp.wait_ge(silu_done, g * TT + tt + 1)
            nc.gpsimd.tensor_tensor(g_tile[:, tt, :], g_tile[:, tt, :], s_tile[:, tt, :], ALU.mult).then_inc(s_free, 1)
            if tt == 0:
                gp.wait_ge(ld_res, g * 16 + 16)
            gp.wait_ge(s_free, g * TT + tt + 1 + TT)
            nc.gpsimd.tensor_tensor(g_tile[:, tt, :], g_tile[:, tt, :], x_res[:, tt, :], ALU.add).then_inc(rows_done, 1)

        def half(i):
            return slice(i * D // 2, (i + 1) * D // 2)

        def rows(tt):
            return slice(tt * P, (tt + 1) * P)

        def three(dst, pairs, start=True, stop=True):
            mms = [(a, b) for ah, al, bh, bl in pairs for a, b in ((ah, bh), (ah, bl), (al, bh))]
            for n, (a, b) in enumerate(mms):
                last = nc.tensor.matmul(dst, a, b, start=(start and n == 0), stop=(stop and n == len(mms) - 1))
            return last

        seg_ones = h[:, 0:P]
        row_cnt = h[:, P:2 * P]
        on = h[:, 2 * P:3 * P]
        ws_nat = s_tile
        c2_nat = x_res[:, 0, 0:IT * RANK].rearrange("p (i r) -> p i r", r=RANK)
        c2_rep = counts[:].bitcast(F32).rearrange("p a t n -> p (a t n)")[:, 0:IT * P]
        c2_rep_q = c2_rep.rearrange("p (i q r) -> p i q r", q=4, r=Q)
        up = [banks[0], banks[1]]
        acc = [banks[2 + tt] for tt in range(TT)]
        sel = banks[6]
        mask_bank = banks[5]
        first = banks[7][:].bitcast(BF16)[:, 0:S]
        NSEL = PIECES * TT
        MB = D // SEG

        logits = qkv[R:R + E, 2, :]
        pj = [banks[0], banks[1]]
        y = [banks[2], banks[3]]
        sc = [banks[4], banks[5]]
        tr = [banks[6], banks[7]]
        NROUTE = 19

        EARLY = [banks[i] for i in (2, 3, 4, 5, 7)]
        LATE = [banks[i] for i in (2, 3, 7)]
        W1 = [("w1", i) for i in range(IT)]
        C2 = [("c2", i) for i in range(0, IT, 4)]
        WS = [("ws", k) for k in range(KD)]
        items = W1[:1] + [("c1", 0)] + W1[1:2]
        BEFORE_ROWS = len(items)
        items += W1[2:4]
        BEFORE_WS = len(items)
        items += WS
        WS_END = len(items)
        items += C2[:1] + W1[4:6]
        BEFORE_S = len(items)
        items += W1[6:8] + C2[1:2] + W1[8:10] + C2[2:3] + W1[10:12] + C2[3:] + W1[12:]
        bank_of = [EARLY[n % 5] for n in range(len(items))]
        frees = [n - 5 for n in range(len(items))]
        NW = len(items)
        w_at = {item: n for n, item in enumerate(items)}
        AFTER_S = [range(BEFORE_S + 3 * tt, min(BEFORE_S + 3 * tt + 3, NW)) for tt in range(TT)]
        places = [g_tile[:, i, :] for i in range(4)] + [x_res[:, i, :] for i in range(1, 4)]
        NP = len(places)
        items += [("a", 0)]
        bank_of += [banks[6]]
        frees += [-1]
        L1_AT = len(items)
        items += [("base", k) for k in range(KD)] + [("b", k) for k in range(KE)]
        bank_of += [LATE[n % 3] for n in range(len(items) - L1_AT)]
        frees += [n - 3 if n >= 3 else -1 for n in range(len(items) - L1_AT)]
        for n, m in enumerate(frees):
            if n >= L1_AT and m >= 0:
                frees[n] = L1_AT + m

        def item_in(pe, n):
            kind, i = items[n]
            dst = bank_of[n]
            if frees[n] >= 0:
                pe.wait_ge(w_lo, frees[n] + 1)
            if kind == "c1":
                pe.wait_ge(ld_c1, 16)
                for k in range(KD):
                    last = nc.tensor.transpose(dst[:, k * RANK:(k + 1) * RANK], c1_nat[:, rows(k)], ident[0:RANK, 0:RANK])
            elif kind == "c2":
                pe.wait_ge(c2_wide, 1)
                for j in range(i, min(i + 4, IT)):
                    last = nc.tensor.transpose(dst[:, rows(j - i)], c2_rep[:, rows(j)], ident[:])
            elif kind == "ws":
                pe.wait_ge(ws0_masked, TT)
                for t in range(TT):
                    last = nc.tensor.transpose(dst[:, rows(t)], ws_nat[:, t, rows(i)], ident[:])
            elif kind == "w1":
                pe.wait_ge(ld_w[i % NP], 16 * (i // NP + 1))
                for k in range(KD):
                    last = nc.tensor.transpose(dst[:, rows(k)], places[i % NP][:, rows(k)], ident[:])
            elif kind == "a":
                pe.wait_ge(ld_l1_small, 16 * 4)
                for k in range(KD):
                    last = nc.tensor.transpose(dst[:, k * (R + E):(k + 1) * (R + E)], a_nat[0:R + E, rows(k)],
                                               ident[0:R + E, 0:R + E])
            elif kind == "base":
                pe.wait_ge(ld_base, 2 * 16)
                for t in range(TT):
                    last = nc.tensor.transpose(dst[:, rows(t)], base_nat[:, t, rows(i)], ident[:])
            else:
                pe.wait_ge(ld_b, TT * 16)
                for t in range(TT):
                    last = nc.tensor.transpose(dst[:, rows(t)],
                                               b_nat[:, t, EPT * i:EPT * (i + 1), :].rearrange("p e r -> p (e r)"), ident[:])
            last.then_inc(w_tr, 1)

        def item_parts(n):
            kind, i = items[n]
            src = bank_of[n]
            by_k = src[:].rearrange("p (k n) -> p k n", k=KD)
            if kind == "c1":
                got = src[:, 0:KD * RANK].rearrange("p (k r) -> p k r", k=KD)
                return [(got, c1_stack[:, :, q * Q:q * Q + RANK], c1_stack[:, :, q * Q:q * Q + RANK]) for q in range(4)]
            if kind == "ws":
                return [(src[:], ws_hi[:, i, :], ws_lo[:, i, :])]
            if kind == "w1":
                return [(by_k, w1T_hi[:, :, rows(i)], w1T_lo[:, :, rows(i)])]
            if kind == "a":
                return [(src[:, 0:KD * (R + E)].rearrange("p (k r) -> p k r", k=KD), a_hi[:], a_lo[:])]
            if kind == "base":
                return [(src[:], base_hi[:, i, :], base_lo[:, i, :])]
            return [(src[:], b_hi[:, i, :], b_lo[:, i, :])]

        def item_hi(act, n):
            kind, i = items[n]
            act.wait_ge(w_tr, n + 1)
            if kind == "c1":
                act.wait_ge(consts_dve, 12)
            if kind == "c2":
                cols = slice(i * P, min(i + 4, IT) * P)
                last = nc.scalar.activation(c2_stack[:, cols], bank_of[n][:, 0:cols.stop - cols.start], ACT.Copy)
            else:
                for got, hi, _ in item_parts(n):
                    last = nc.scalar.activation(hi, got, ACT.Copy)
            last.then_inc(w_hi, 1)

        def item_lo(dve, n):
            kind, i = items[n]
            dve.wait_ge(w_hi, n + 1)
            if kind == "c2":
                cols = slice(i * P, min(i + 4, IT) * P)
                part = c2_stack[2 * Q:3 * Q, cols]
                last = nc.vector.tensor_tensor(part, bank_of[n][2 * Q:3 * Q, 0:cols.stop - cols.start],
                                               part.bitcast(F32), ALU.subtract)
            else:
                for got, hi, lo in item_parts(n)[-1:]:
                    last = nc.vector.tensor_tensor(lo, got, hi.bitcast(F32), ALU.subtract)
            last.then_inc(w_lo, 1)

        LATE_GROUPS = [range(L1_AT + 3 * j, L1_AT + 3 * j + 3) for j in range(4)]

        block = ctx.enter_context(nc.Block())

        @block.sync
        def _(sp):
            def stage(n):
                m = n - NP
                if 0 <= m < IT:
                    sp.wait_ge(w_tr, w_at["w1", m] + 1)
                elif m >= IT:
                    sp.wait_ge(w2_lo, m - IT + 1)
                w, i = (w1, n) if n < IT else (w2, n - IT)
                sp.dma_start(places[n % NP], w[i * P:(i + 1) * P, :]).then_inc(ld_w[n % NP], 16)

            stage(0)
            sp.dma_start(c1_nat[:], c1_w).then_inc(ld_c1, 16)
            sp.dma_start(x_tile[:, 0:2, :], x_rows[0][:, 0:2, :]).then_inc(ld_x_first, 16)
            sp.dma_start(x_tile[:, 2:TT, :], x_rows[0][:, 2:TT, :]).then_inc(ld_x, 16)
            sp.dma_start(mask_nat[:], mask.rearrange("(t p) k -> p t k", p=P)).then_inc(ld_mask, 16)
            stage(1)
            sp.dma_start(ws_nat[:], w_s0.rearrange("(t p) k -> p t k", p=P)).then_inc(ld_ws0, 16)
            for n in range(2, 4):
                stage(n)
            sp.dma_start(c2_nat, c2_w.rearrange("(i p) r -> p i r", p=P)).then_inc(ld_c2, 16)
            sp.dma_start(bias_a[:], b_s0.rearrange("(a n) -> a n", a=1).to_broadcast([P, D])).then_inc(ld_bias, 16)
            for n in range(4, IT):
                stage(n)
            for n in range(IT, 2 * IT):
                stage(n)
            sp.dma_start(a_nat[R:R + E, :], router_w).then_inc(ld_l1_small, 16)
            sp.dma_start(a_nat[0:R, :], lora_a).then_inc(ld_l1_small, 16)
            sp.dma_start(bias_b[:], base_b.rearrange("(a n) -> a n", a=1).to_broadcast([P, D])).then_inc(ld_l1_small, 16)
            with nc.allow_non_contiguous_dma(reason="three short columns"):
                sp.dma_start(bqkv_col[:], bqkv.rearrange("(j p) -> p j", p=P)).then_inc(ld_l1_small, 16)

            def chunk(c, source, last):
                sp.wait_ge(xT_tr, c * TT + TT)
                sp.dma_start(x_tile[:], source).then_inc(ld_x, 16)
                sp.wait_ge(w2_lo, IT)
                sp.wait_ge(c2_wide, 1)
                sp.dma_start(x_res[:], x_rows[c]).then_inc(ld_res, 16)
                if last:
                    sp.wait_ge(t_done, CH)
                    sp.dma_start(wqkv_nat[:], wqkv.rearrange("(k p) n -> p k n", p=P)).then_inc(ld_wqkv, 16)
                if last:
                    sp.wait_ge(s_biased, CH * TT)
                    sp.dma_start(bias_a[:], bo.rearrange("(a n) -> a n", a=1).to_broadcast([P, D])).then_inc(ld_bo, 16)
                    sp.wait_ge(up_done, CH * IT)
                    sp.dma_start(base_nat[:], base_w.rearrange("(t p) k -> p t k", p=P)).then_inc(ld_base, 16)
                    sp.dma_start(wo_nat[:], wo).then_inc(ld_base, 16)
                    for t in range(TT):
                        sp.dma_start(b_nat[:, t], lora_b[:, rows(t), :].rearrange("e p r -> p e r")).then_inc(ld_b, 16)
                for tt in range(TT):
                    sp.wait_ge(rows_done, c * TT + tt + 1)
                    sp.dma_start(mid_rows[c][:, tt, :], g_tile[:, tt, :]).then_inc(st_rows, 16)
                sp.wait_ge(st_rows, c * TT * 16 + TT * 16)
                sp.sem_inc(g_free, 1)

            sp.sem_inc(g_free, 1)
            with sp.Fori(0, CH - 1) as c:
                chunk(c, x_rows[c + 1], False)
            chunk(CH - 1, mid_rows[0], True)

            def chunk(c, source):
                g = c + CH
                sp.dma_start(x_res[:], mid_rows[c]).then_inc(ld_res, 16)
                if source is not None:
                    sp.wait_ge(xT_tr, g * TT + TT)
                    sp.dma_start(x_tile[:], source).then_inc(ld_x, 16)
                for tt in range(TT if source is not None else TT - 1):
                    sp.wait_ge(rows_done, g * TT + tt + 1)
                    sp.dma_start(out_rows[c][:, tt, :], g_tile[:, tt, :]).then_inc(st_out, 16)
                if source is not None:
                    sp.wait_ge(st_out, c * TT * 16 + TT * 16)
                    sp.sem_inc(g_free, 1)
                else:
                    for i in range(2):
                        sp.wait_ge(end_done, i + 1)
                        sp.dma_start(out_rows[c][:, TT - 1, half(i)], g_tile[:, TT - 1, half(i)]).then_inc(st_out, 16)
                    sp.wait_ge(st_out, CH * TT * 16 + 16)

            with sp.Fori(0, CH - 1) as c:
                chunk(c, mid_rows[c + 1])
            chunk(CH - 1, None)

        @block.gpsimd
        def _(gp):
            gp.memset(ident[:], 0.0).then_inc(consts_gp, 1)
            gp.memset(ident_bf[:], 0.0).then_inc(consts_gp, 1)
            gp.memset(neg_half[:], -0.5).then_inc(consts_gp, 1)
            gp.memset(eps[:], EPS).then_inc(consts_gp, 1)
            gp.wait_ge(consts_gp, 4)
            for m in (ident, ident_bf):
                gp.affine_select(out=m[:], in_=m[:], compare_op=ALU.not_equal, fill=1.0, base=0,
                                 pattern=[[-1, P]], channel_multiplier=1).then_inc(consts_gp, 1)
            gp.sem_inc(s_free, TT)
            rows_rstd(gp, 0)
            gp.wait_ge(mask_on, 1)
            gp.wait_ge(ld_ws0, 16)
            for t in range(TT):
                part = ws_nat[:, t, :].rearrange("p (n s) -> p n s", s=SEG)
                nc.gpsimd.tensor_tensor(part, part, on[:, t * MB:(t + 1) * MB][:, :, None].to_broadcast([P, MB, SEG]),
                                        ALU.mult).then_inc(ws0_masked, 1)
            gp.wait_ge(ld_bias, 16)
            nc.gpsimd.tensor_scalar(bias_a[:], bias_a[:], 0.5, 1.0, ALU.mult, ALU.mult).then_inc(half_bias, 1)
            for i in range(IT):
                n = IT + i
                gp.wait_ge(ld_w[n % NP], 16 * (n // NP + 1))
                nc.gpsimd.tensor_copy(w2_hi_t[:, i, :], places[n % NP]).then_inc(w2_hi, 1)
                gp.wait_ge(w2_hi, i + 1)
                nc.gpsimd.tensor_tensor(w2_lo_t[:, i, :], places[n % NP], w2_hi_t[:, i, :].bitcast(F32),
                                        ALU.subtract).then_inc(w2_lo, 1)
            gp.wait_ge(half_bias, 1)

            def head(c):
                for tt in range(TT):
                    gp.wait_ge(s0_read, c * TT + tt + 1)
                    nc.gpsimd.tensor_tensor(s_tile[:, tt, :], s_tile[:, tt, :], bias_a[:], ALU.add).then_inc(s_biased, 1)

            def body(c, last):
                rows_rstd(gp, c + 1)
                if last:
                    gp.wait_ge(up_done, CH * IT)
                    gp.memset(pick_f[:], 0.0).then_inc(pick_ready, 1)
                    for q in range(2):
                        gp.wait_ge(pick_ready, q + 1)
                        sq = pick_f[:].rearrange("e k (h r) -> e k h r", r=R)
                        gp.affine_select(out=sq, in_=sq, compare_op=ALU.not_equal, fill=1.0, base=-q * Q,
                                         pattern=[[-EPT, KE], [-1, EPT], [0, R]], channel_multiplier=1).then_inc(pick_ready, 1)
                    gp.wait_ge(pick_ready, 3)
                    nc.gpsimd.tensor_copy(pick[:], pick_f[:]).then_inc(pick_ready, 1)
                gp.wait_ge(s_biased, c * TT + TT)
                for tt in range(TT):
                    gate(gp, c, tt)

            head(0)
            with gp.Fori(0, CH - 1) as c:
                body(c, False)
                head(c + 1)
            body(CH - 1, True)

            gp.wait_ge(ld_bo, 16)
            nc.gpsimd.tensor_scalar(bias_a[:], bias_a[:], 0.5, 1.0, ALU.mult, ALU.mult).then_inc(wo_split, 1)
            gp.wait_ge(w_direct_hi, 2)
            nc.gpsimd.tensor_tensor(wo_lo[:], wo_nat[:], wo_hi[:].bitcast(F32), ALU.subtract).then_inc(wo_split, 1)

            def chunk(c, last):
                for kt in range(KE):
                    gp.wait_ge(prod_hi_done, c * KE + kt + 1)
                    nc.gpsimd.tensor_tensor(prod_lo[:, kt, :], prod[:, kt % 3, :], prod_hi[:, kt, :].bitcast(F32),
                                            ALU.subtract).then_inc(prod_split, 1)
                if not last:
                    rows_rstd(gp, c + CH + 1)
                for tt in range(TT - 1 if last else TT):
                    gate(gp, c + CH, tt)

            with gp.Fori(0, CH - 1) as c:
                chunk(c, False)
            chunk(CH - 1, True)

        @block.scalar
        def _(act):
            def t_round(c):
                act.wait_ge(t_done, c + 1)
                nc.scalar.activation(t_stack[:], sel[:], ACT.Copy).then_inc(t_hi, 1)

            def s_read(c, tt):
                act.wait_ge(s0_done, c * TT + tt + 1)
                act.wait_ge(s_free, c * TT + tt + 1)
                nc.scalar.activation(s_tile[:, tt, :], up[tt % 2][:], ACT.Copy, scale=0.5).then_inc(s0_read, 1)

            def head(c):
                t_round(c)
                for tt in range(TT):
                    s_read(c, tt)

            def body(c, last):
                for it in range(IT):
                    act.wait_ge(up_done, c * IT + it + 1)
                    if it:
                        act.wait_ge(h_split, c * IT + it)
                    nc.scalar.activation(h[:], up[it % 2][:], ACT.Relu).then_inc(relu_done, 1)
                    if last and it == IT - 4:
                        act.wait_ge(ld_wqkv, 16)
                        nc.scalar.activation(wqkv_hi[:], wqkv_nat[:], ACT.Copy).then_inc(w_direct_hi, 1)
                    if last and it == IT - 1:
                        item_hi(act, NW)
                    act.wait_ge(h_masked, c * IT + it + 1)
                    if it >= 2:
                        act.wait_ge(down_done, c * IT + it - 1)
                    nc.scalar.activation(h_hi[:, it % 2, :], h[:], ACT.Copy).then_inc(h_hi_done, 1)
                for tt in range(TT):
                    rows_hi(act, c + 1, tt)
                act.wait_ge(down_done, c * IT + IT)
                act.wait_ge(w2_lo, IT)
                act.wait_ge(g_free, c + 1)
                for tt in range(TT):
                    nc.scalar.activation(g_tile[:, tt, :], acc[tt][:], ACT.Tanh, scale=0.5).then_inc(tanh_done, 1)

            for n in range(BEFORE_ROWS):
                item_hi(act, n)
            for tt in range(TT):
                rows_hi(act, 0, tt)
            for n in range(BEFORE_ROWS, WS_END):
                item_hi(act, n)
            act.wait_ge(consts_dve, 12)
            act.wait_ge(ld_c2, 16)
            for q in range(4):
                last = nc.scalar.activation(c2_rep_q[:, :, q, 0:RANK], c2_nat, ACT.Copy)
            last.then_inc(c2_wide, 1)
            for n in range(WS_END, BEFORE_S):
                item_hi(act, n)
            t_round(0)
            for tt in range(TT):
                s_read(0, tt)
                for n in AFTER_S[tt]:
                    item_hi(act, n)
            with act.Fori(0, CH - 1) as c:
                body(c, False)
                head(c + 1)
            body(CH - 1, True)

            def probs_exp(c, tt):
                act.wait_ge(neg_max, c * TT + tt + 1)
                act.wait_ge(silu_done, (c + CH - 1) * TT + tt + 1)
                nc.scalar.activation(probs[:, tt, :], sc[tt % 2][:], ACT.Exp, bias=s_neg[:, tt:tt + 1], scale=QK_SCALE,
                                     accum_out=p_sum[:, tt:tt + 1]).then_inc(exp_done, 1)

            def prods_hi(c, kt):
                if kt == 4:
                    act.wait_ge(wo_split, 2)
                act.wait_ge(prod_done, c * KE + kt + 1)
                nc.scalar.activation(prod_hi[:, kt, :], prod[:, kt % 3, :], ACT.Copy).then_inc(prod_hi_done, 1)

            def probs_hi(c, kt):
                act.wait_ge(p_tr, c * TT + kt + 1)
                nc.scalar.activation(pT_hi[:, kt, :], tr[kt % 2][:], ACT.Copy).then_inc(p_hi_done, 1)

            def gate_tanh(c, tt):
                act.wait_ge(y_read, (c + 1) * TT + tt + 1)
                nc.scalar.activation(probs[:, tt, :], g_tile[:, tt, :], ACT.Tanh, scale=0.5).then_inc(tanh_done, 1)

            def chunk(c, is_first, last):
                act.wait_ge(proj_done, c * 4 + 1)
                nc.scalar.activation(logits, pj[0][R:R + E, :], ACT.Copy).then_inc(logits_out, 1)
                for j in range(EPT):
                    last_read = nc.scalar.activation(res[j * R:(j + 1) * R, :], pj[0][0:R, :], ACT.Copy)
                last_read.then_inc(proj_read, 1)
                act.wait_ge(route_step, c * NROUTE + 2)
                nc.scalar.activation(gate_p[:], gate_p[:], ACT.Exp).then_inc(route_exp, 1)
                for j, src in enumerate((pj[1], sc[0], sc[1])):
                    if j == 2:
                        act.wait_ge(comb_tr, c + 1)
                        nc.scalar.activation(combT[:], tr[0][0:2 * Q, :], ACT.Copy).then_inc(comb_hi, 1)
                    act.wait_ge(proj_done, c * 4 + j + 2)
                    nc.scalar.activation(qkv[:, j, :], src[:], ACT.Identity, bias=bqkv_col[:, j:j + 1]).then_inc(proj_read, 1)
                    if j < 2:
                        act.wait_ge(proj_read, c * 4 + j + 2)
                        nc.scalar.activation(qk_hi[:, j, :], qkv[:, j, :], ACT.Copy).then_inc(qk_hi_done, 1)
                    if is_first:
                        for n in LATE_GROUPS[j]:
                            item_hi(act, n)
                if is_first:
                    for n in LATE_GROUPS[3]:
                        item_hi(act, n)
                probs_exp(c, 0)
                if is_first:
                    nc.scalar.activation(wo_hi[:], wo_nat[:], ACT.Copy).then_inc(w_direct_hi, 1)
                act.wait_ge(v_tr, c + 1)
                nc.scalar.activation(v_hi[:], tr[1][:].rearrange("p (t d) -> p t d", t=TT), ACT.Copy).then_inc(v_hi_done, 1)
                prods_hi(c, 0)
                prods_hi(c, 1)
                probs_exp(c, 1)
                prods_hi(c, 2)
                prods_hi(c, 3)
                probs_exp(c, 2)
                probs_exp(c, 3)
                prods_hi(c, 4)
                prods_hi(c, 5)
                probs_hi(c, 0)
                probs_hi(c, 1)
                probs_hi(c, 2)
                probs_hi(c, 3)
                prods_hi(c, 6)
                prods_hi(c, 7)
                act.wait_ge(pv_done, c + 1)
                nc.scalar.activation(at_hi[:], sc[0][:], ACT.Copy).then_inc(a_hi_done, 1)
                for tt in range(3):
                    gate_tanh(c, tt)
                if not last:
                    for tt in range(TT):
                        rows_hi(act, c + CH + 1, tt)
                    gate_tanh(c, 3)
                else:
                    for i in range(2):
                        act.wait_ge(end_g, i + 1)
                        nc.scalar.activation(probs[:, TT - 1, half(i)], g_tile[:, TT - 1, half(i)], ACT.Tanh,
                                             scale=0.5).then_inc(end_tanh, 1)

            chunk(0, True, False)
            with act.Fori(1, CH - 1) as c:
                chunk(c, False, False)
            chunk(CH - 1, False, True)

        @block.vector
        def _(dve):
            nc.vector.memset(restart[:], 2.0).then_inc(consts_dve, 1)
            nc.vector.memset(restart_e[:], 2.0).then_inc(consts_dve, 1)
            nc.vector.memset(c1_stack[:].bitcast(F32), 0.0).then_inc(consts_dve, 1)
            nc.vector.memset(c2_rep, 0.0).then_inc(consts_dve, 1)
            nc.vector.memset(seg_ones, 0.0).then_inc(consts_dve, 1)
            nc.vector.memset(comb[:], 0.0).then_inc(consts_dve, 1)
            dve.wait_ge(consts_dve, 6)
            nc.vector.memset(restart[:].rearrange("p (s n) -> p s n", n=SEG)[:, :, 0:1], 0.0).then_inc(consts_dve, 1)
            nc.vector.memset(restart_e[:].rearrange("p (s n) -> p s n", n=E)[:, :, 0:1], 0.0).then_inc(consts_dve, 1)
            for q in range(4):
                nc.vector.memset(h[q * Q:(q + 1) * Q, q * Q:(q + 1) * Q], 1.0).then_inc(consts_dve, 1)
            dve.sem_inc(y_read, TT)
            dve.sem_inc(o_read, TT)
            for n in range(2):
                item_lo(dve, n)
            dve.wait_ge(ld_x_first, 16)
            for tt in range(2):
                nc.vector.bn_stats(bn[:, tt, :], x_tile[:, tt, :]).then_inc(stats_in, 1)
            dve.wait_ge(ld_x, 16)
            for tt in range(2, TT):
                nc.vector.bn_stats(bn[:, tt, :], x_tile[:, tt, :]).then_inc(stats_in, 1)
            dve.wait_ge(stats_in, TT)
            rows_moments()
            dve.wait_ge(ld_mask, 16)
            with nc.allow_low_precision(reason="counts of ones"):
                nc.vector.reduce_sum(row_cnt[:, 0:TT * MB].rearrange("p (t n) -> p t n", t=TT),
                                     mask_nat[:].rearrange("p t (n s) -> p t n s", s=SEG), AX.X).then_inc(mask_sum, 1)
            rows_norm(dve, 0, range(0, 2))
            dve.wait_ge(mask_cnt, 1)
            nc.vector.tensor_scalar(on[:, 0:TT * MB], mask_bank[:, 0:TT * MB], 0.0, None, ALU.is_gt).then_inc(mask_on, 1)
            rows_norm(dve, 0, range(2, TT))
            for n in range(2, BEFORE_ROWS):
                item_lo(dve, n)
            for tt in range(TT):
                rows_lo(dve, 0, tt)
            for n in range(BEFORE_ROWS, BEFORE_WS):
                item_lo(dve, n)

            def t_rest(c):
                dve.wait_ge(t_hi, c + 1)
                nc.vector.tensor_tensor(t_stack[Q:2 * Q, :], sel[Q:2 * Q, :], t_stack[Q:2 * Q, :].bitcast(F32),
                                        ALU.subtract).then_inc(t_split, 1)

            def select(c, p, tt):
                select_largest(c, p, tt)
                select_count(c, p, tt)

            def select_largest(c, p, tt):
                n = p * TT + tt
                segs = PW[p] // SEG
                got = sel[:, 0:PW[p]].rearrange("p (s n) -> p s n", n=SEG)
                dve.wait_ge(sel_done, c * NSEL + n + 1)
                nc.vector.reduce_max(seg_top[:, 0:segs], got, AX.X).then_inc(seg_max, 1)
                dve.wait_ge(seg_max, c * NSEL + n + 1)
                nc.vector.tensor_tensor(eq[:, 0:PW[p]].rearrange("p (s n) -> p s n", n=SEG), got,
                                        seg_top[:, 0:segs, None].to_broadcast([P, segs, SEG]),
                                        ALU.is_equal).then_inc(sel_eq, 1)

            def select_count(c, p, tt):
                n = p * TT + tt
                dve.wait_ge(sel_eq, c * NSEL + n + 1)
                if tt == 0 and p >= 2:
                    dve.wait_ge(first_tr, c * IT + 4 * (p - 1))
                nc.vector.tensor_tensor_scan(counts[:, p % 2, tt, 0:PW[p]], restart[:, 0:PW[p]], eq[:, 0:PW[p]], 0.0,
                                             ALU.mult, ALU.add).then_inc(sel_count, 1)

            def head(c):
                t_rest(c)
                for tt in range(TT - 1):
                    select(c, 0, tt)

            def body(c, last):
                select(c, 0, TT - 1)
                for it in range(IT):
                    if 0 < it < 4 * (PIECES - 1):
                        select(c, it // 4 + 1, it % 4)
                    if last and it == IT - 1:
                        item_lo(dve, NW)
                    dve.wait_ge(relu_done, c * IT + it + 1)
                    dve.wait_ge(first_tr, c * IT + it + 1)
                    nc.vector.scalar_tensor_tensor(h[:], first, 1.0, h[:], ALU.is_equal, ALU.mult).then_inc(h_masked, 1)
                    if IT - 8 <= it < IT - 4:
                        rows_stats(dve, c + 1, it - (IT - 8))
                    if it == IT - 4:
                        dve.wait_ge(stats_in, (c + 1) * TT + TT)
                    if it == 0:
                        select_largest(c, 1, 0)
                    dve.wait_ge(h_hi_done, c * IT + it + 1)
                    nc.vector.tensor_tensor(h_lo[:, it % 2, :], h[:], h_hi[:, it % 2, :].bitcast(F32),
                                            ALU.subtract).then_inc(h_split, 1)
                    if it == 0:
                        select_count(c, 1, 0)
                    if it == IT - 4:
                        rows_moments()
                    if last and it == IT - 3:
                        dve.wait_ge(w_direct_hi, 1)
                        nc.vector.tensor_tensor(wqkv_lo[:], wqkv_nat[:], wqkv_hi[:].bitcast(F32),
                                                ALU.subtract).then_inc(w_direct_lo, 1)
                    if it == IT - 2:
                        rows_norm(dve, c + 1)
                for tt in range(TT):
                    rows_lo(dve, c + 1, tt)
                for tt in range(TT):
                    dve.wait_ge(tanh_done, c * TT + tt + 1)
                    nc.vector.scalar_tensor_tensor(g_tile[:, tt, :], g_tile[:, tt, :], 1.0, acc[tt][:],
                                                   ALU.add, ALU.mult).then_inc(silu_done, 1)

            for n in range(BEFORE_WS, BEFORE_S):
                item_lo(dve, n)
            t_rest(0)
            for tt in range(TT):
                if tt:
                    select(0, 0, tt - 1)
                for n in AFTER_S[tt]:
                    item_lo(dve, n)
            with dve.Fori(0, CH - 1) as c:
                body(c, False)
                head(c + 1)
            body(CH - 1, True)

            def wide(a):
                return a[:, :, None].to_broadcast([P, TT, E])

            def route(c, is_first):
                steps = [0]

                def step(ins, wait=True):
                    steps[0] += 1
                    ins.then_inc(route_step, 1)
                    if is_first and steps[0] in (7, 10, 13):
                        item_lo(dve, L1_AT + (steps[0] - 7) // 3)
                    if wait:
                        dve.wait_ge(route_step, c * NROUTE + steps[0])

                v = nc.vector
                tops = top_cnt[:].rearrange("p t e -> p (t e)")
                got = tr[0][:, 0:TT * E].rearrange("p (t e) -> p t e", t=TT)
                dve.wait_ge(route_in, c + 1)
                step(v.reduce_max(row_a[:], got, AX.X))
                step(v.tensor_tensor(gate_p[:], got, wide(row_a), ALU.subtract))
                dve.wait_ge(route_exp, c + 1)
                step(v.reduce_sum(row_a[:], gate_p[:], AX.X))
                step(v.reciprocal(row_a[:], row_a[:]))
                step(v.tensor_tensor(gate_p[:], gate_p[:], wide(row_a), ALU.mult))
                step(v.reduce_max(top_p[:, 0, :], gate_p[:], AX.X))
                step(v.tensor_tensor(is_top[:], gate_p[:], wide(top_p[:, 0, :]), ALU.is_equal))
                step(v.tensor_tensor_scan(tops, restart_e[:], is_top[:].rearrange("p t e -> p (t e)"), 0.0,
                                          ALU.mult, ALU.add))
                step(v.scalar_tensor_tensor(top_w[:, 0], top_cnt[:], 1.0, gate_p[:], ALU.is_equal, ALU.mult))
                step(v.tensor_tensor(gate_p[:], gate_p[:], top_w[:, 0], ALU.subtract))
                step(v.reduce_max(top_p[:, 1, :], gate_p[:], AX.X))
                step(v.tensor_tensor(is_top[:], gate_p[:], wide(top_p[:, 1, :]), ALU.is_equal), False)
                step(v.scalar_tensor_tensor(row_a[:], top_p[:, 0, :], 1e-6, top_p[:, 1, :], ALU.add, ALU.add))
                step(v.tensor_tensor_scan(tops, restart_e[:], is_top[:].rearrange("p t e -> p (t e)"), 0.0,
                                          ALU.mult, ALU.add), False)
                step(v.reciprocal(row_a[:], row_a[:]))
                step(v.scalar_tensor_tensor(top_w[:, 1], top_cnt[:], 1.0, gate_p[:], ALU.is_equal, ALU.mult))
                step(v.tensor_tensor(top_w[:, 0], top_w[:, 0], top_w[:, 1], ALU.add))
                for q in range(2):
                    step(v.scalar_tensor_tensor(comb[:, :, q * Q:q * Q + E], top_w[:, 0], SCALING, wide(row_a),
                                                ALU.mult, ALU.mult), q == 1)
                assert steps[0] == NROUTE

            def score_peak(c, tt):
                dve.wait_ge(score_done, c * TT + tt + 1)
                nc.vector.reduce_max(s_max[:, tt:tt + 1], sc[tt % 2][:], AX.X).then_inc(score_max, 1)
                dve.wait_ge(score_max, c * TT + tt + 1)
                nc.vector.tensor_scalar(s_neg[:, tt:tt + 1], s_max[:, tt:tt + 1], -QK_SCALE, None, ALU.mult).then_inc(neg_max, 1)

            def prods(c, kt):
                dve.wait_ge(spread_done, c * KE + kt + 1)
                if kt >= 3:
                    dve.wait_ge(prod_split, c * KE + kt - 2)
                nc.vector.tensor_tensor(prod[:, kt % 3, :], pj[kt % 2][:], res[:], ALU.mult).then_inc(prod_done, 1)

            def probs_lo(c, kt):
                dve.wait_ge(p_hi_done, c * TT + kt + 1)
                nc.vector.tensor_tensor(pT_lo[:, kt, :], tr[kt % 2][:], pT_hi[:, kt, :].bitcast(F32),
                                        ALU.subtract).then_inc(p_split, 1)

            def two_prods(c, kt):
                prods(c, kt)
                prods(c, kt + 1)

            def y_out(c, tt):
                dve.wait_ge(y_done, c * TT + tt + 1)
                if tt == 0:
                    dve.wait_ge(g_free, c + CH + 1)
                nc.vector.tensor_tensor(g_tile[:, tt, :], y[tt % 2][:], bias_b[:], ALU.add).then_inc(y_read, 1)

            def s_out(c, tt):
                if tt == 0:
                    dve.wait_ge(wo_split, 2)
                dve.wait_ge(o_done, c * TT + tt + 1)
                dve.wait_ge(s_free, (c + CH) * TT + tt + 1)
                nc.vector.scalar_tensor_tensor(s_tile[:, tt, :], sc[(tt + 1) % 2][:], p_inv[:, tt:tt + 1], bias_a[:],
                                               ALU.mult, ALU.add).then_inc(o_read, 1)

            def silu(c, tt):
                dve.wait_ge(tanh_done, (c + CH) * TT + tt + 1)
                nc.vector.scalar_tensor_tensor(g_tile[:, tt, :], probs[:, tt, :], 1.0, g_tile[:, tt, :],
                                               ALU.add, ALU.mult).then_inc(silu_done, 1)

            def end_tile(c):
                tt = TT - 1
                s_out(c, tt)
                dve.wait_ge(o_read, c * TT + 2 * TT)
                dve.wait_ge(ld_res, 2 * CH * 16)
                for i in range(2):
                    g, s, t = g_tile[:, tt, half(i)], s_tile[:, tt, half(i)], probs[:, tt, half(i)]
                    dve.wait_ge(end_y_done, i + 1)
                    nc.vector.tensor_tensor(g, y[1 - i][:, half(i)], bias_b[:, half(i)], ALU.add).then_inc(end_g, 1)
                    dve.wait_ge(end_g, i + 1)
                    nc.vector.tensor_tensor(s, s, g, ALU.mult).then_inc(end_gs, 1)
                    dve.wait_ge(end_gs, i + 1)
                    dve.wait_ge(end_tanh, i + 1)
                    nc.vector.scalar_tensor_tensor(g, t, 1.0, s, ALU.add, ALU.mult).then_inc(end_silu, 1)
                    dve.wait_ge(end_silu, i + 1)
                    nc.vector.tensor_tensor(g, g, x_res[:, tt, half(i)], ALU.add).then_inc(end_done, 1)

            def chunk(c, is_first, last):
                route(c, is_first)
                for j in range(2):
                    dve.wait_ge(qk_hi_done, c * 2 + j + 1)
                    nc.vector.tensor_tensor(qk_lo[:, j, :], qkv[:, j, :], qk_hi[:, j, :].bitcast(F32),
                                            ALU.subtract).then_inc(qk_split, 1)
                    if is_first:
                        for n in LATE_GROUPS[1 + j]:
                            item_lo(dve, n)
                if is_first:
                    for n in LATE_GROUPS[3]:
                        item_lo(dve, n)
                dve.wait_ge(comb_hi, c + 1)
                nc.vector.tensor_tensor(combT[Q:2 * Q, :], tr[0][Q:2 * Q, :], combT[Q:2 * Q, :].bitcast(F32),
                                        ALU.subtract).then_inc(comb_split, 1)
                score_peak(c, 0)
                two_prods(c, 0)
                dve.wait_ge(v_hi_done, c + 1)
                nc.vector.tensor_tensor(v_lo[:], tr[1][:].rearrange("p (t d) -> p t d", t=TT), v_hi[:].bitcast(F32),
                                        ALU.subtract).then_inc(v_split, 1)
                score_peak(c, 1)
                two_prods(c, 2)
                score_peak(c, 2)
                score_peak(c, 3)
                two_prods(c, 4)
                probs_lo(c, 0)
                probs_lo(c, 1)
                probs_lo(c, 2)
                probs_lo(c, 3)
                two_prods(c, 6)
                dve.wait_ge(exp_done, c * TT + TT)
                nc.vector.reciprocal(p_inv[:], p_sum[:]).then_inc(inv_step, 1)
                dve.wait_ge(inv_step, c * 2 + 1)
                nc.vector.tensor_scalar(p_inv[:], p_inv[:], 0.5, None, ALU.mult).then_inc(inv_step, 1)
                dve.wait_ge(a_hi_done, c + 1)
                nc.vector.tensor_tensor(at_lo[:], sc[0][:], at_hi[:].bitcast(F32), ALU.subtract).then_inc(a_split, 1)
                dve.wait_ge(inv_step, c * 2 + 2)
                for tt in range(TT):
                    if tt == TT - 1 and not last:
                        for t in range(TT):
                            rows_lo(dve, c + CH + 1, t)
                    if tt == TT - 1 and last:
                        end_tile(c)
                        break
                    y_out(c, tt)
                    s_out(c, tt)
                    silu(c, tt)
                    if tt == 0 and not last:
                        for t in range(TT):
                            rows_stats(dve, c + CH + 1, t)
                        dve.wait_ge(stats_in, (c + CH + 1) * TT + TT)
                    if tt == 1 and not last:
                        rows_moments()
                        rows_norm(dve, c + CH + 1)

            chunk(0, True, False)
            with dve.Fori(1, CH - 1) as c:
                chunk(c, False, False)
            chunk(CH - 1, False, True)

        @block.tensor
        def _(pe):
            def rank_product():
                for k in range(KD):
                    for x in (xT_hi, xT_lo):
                        last = nc.tensor.matmul(sel[:], c1_stack[:, k, :], x[:, k, :], start=(k == 0 and x is xT_hi),
                                                stop=(k == KD - 1 and x is xT_lo))
                last.then_inc(t_done, 1)

            def s_product(c, tt):
                if tt >= 2:
                    pe.wait_ge(s0_read, c * TT + tt - 1)
                three(up[tt % 2][:], [(xT_hi[:, k, rows(tt)], xT_lo[:, k, rows(tt)], ws_hi[:, k, :], ws_lo[:, k, :])
                                      for k in range(KD)]).then_inc(s0_done, 1)

            def select(c, p, tt):
                if p == 0 and tt == 0:
                    pe.wait_ge(t_split, c + 1)
                else:
                    pe.wait_ge(sel_eq, c * NSEL + p * TT + tt)
                if tt == 0:
                    pe.wait_ge(w_lo, w_at["c2", TT * p] + 1)
                nc.tensor.matmul(sel[:, 0:PW[p]], t_stack[:, rows(tt)],
                                 c2_stack[:, p * BANK:p * BANK + PW[p]], start=True, stop=True).then_inc(sel_done, 1)

            def up_product(c, it):
                if it < 2:
                    pe.wait_ge(s0_read, c * TT + TT - 1 + it)
                else:
                    pe.wait_ge(relu_done, c * IT + it - 1)
                pe.wait_ge(w_lo, w_at["w1", it] + 1)
                three(up[it % 2][:], [(w1T_hi[:, k, rows(it)], w1T_lo[:, k, rows(it)], xT_hi[:, k, :], xT_lo[:, k, :])
                                      for k in range(KD)]).then_inc(up_done, 1)

            def transpose_counts(c, it):
                pe.wait_ge(sel_count, c * NSEL + (it // 4 + 1) * TT)
                if it:
                    pe.wait_ge(h_masked, c * IT + it)
                for tt in range(TT):
                    last = nc.tensor.transpose(first[:, rows(tt)], counts[:, it // 4 % 2, tt, rows(it % 4)], ident_bf[:])
                last.then_inc(first_tr, 1)

            def down_product(it, tts):
                pe.wait_ge(w2_lo, it + 1)
                for tt in tts:
                    last = three(acc[tt][:], [(h_hi[:, it % 2, rows(tt)], h_lo[:, it % 2, rows(tt)],
                                               w2_hi_t[:, it, :], w2_lo_t[:, it, :])], start=(it == 0), stop=(it == IT - 1))
                return last

            def head(c):
                pe.wait_ge(xT_done, c * TT + TT)
                rank_product()
                s_product(c, 0)
                s_product(c, 1)
                select(c, 0, 0)
                s_product(c, 2)
                select(c, 0, 1)
                s_product(c, 3)
                select(c, 0, 2)

            def body(c, last):
                up_product(c, 0)
                select(c, 0, 3)
                for it in range(1, IT + 1):
                    if it < IT:
                        up_product(c, it)
                        if (it - 1) // 4 + 1 < PIECES:
                            select(c, (it - 1) // 4 + 1, (it - 1) % 4)
                        elif last and it == IT - 1:
                            pe.wait_ge(sel_eq, c * NSEL + NSEL)
                            item_in(pe, NW)
                    else:
                        pe.wait_ge(relu_done, c * IT + IT - 1)
                        transpose_rows(pe, c + 1, 0)
                    transpose_counts(c, it - 1)
                    if it >= 2:
                        pe.wait_ge(h_split, c * IT + it - 1)
                        down_product(it - 2, range(TT)).then_inc(down_done, 1)
                pe.wait_ge(relu_done, c * IT + IT)
                transpose_rows(pe, c + 1, 1)
                pe.wait_ge(xT_done, (c + 1) * TT + 1)
                transpose_rows(pe, c + 1, 2)
                pe.wait_ge(h_split, c * IT + IT)
                down_product(IT - 1, range(0, 2))
                pe.wait_ge(xT_done, (c + 1) * TT + 2)
                transpose_rows(pe, c + 1, 3)
                down_product(IT - 1, range(2, TT)).then_inc(down_done, 1)

            pe.wait_ge(consts_gp, 6)
            for n in range(BEFORE_ROWS):
                item_in(pe, n)
            pe.wait_ge(mask_sum, 1)
            nc.tensor.matmul(mask_bank[:, 0:TT * MB], seg_ones, row_cnt[:, 0:TT * MB],
                             start=True, stop=True).then_inc(mask_cnt, 1)
            for tt in range(TT):
                if tt == TT - 1:
                    pe.wait_ge(xT_done, 1)
                transpose_rows(pe, 0, tt)
            pe.wait_ge(mask_on, 1)
            for n in range(BEFORE_ROWS, WS_END):
                item_in(pe, n)
            pe.wait_ge(xT_done, TT)
            rank_product()
            for n in range(WS_END, BEFORE_S):
                item_in(pe, n)
            pe.wait_ge(w_lo, WS_END)
            for tt in range(TT):
                s_product(0, tt)
                if tt:
                    select(0, 0, tt - 1)
                for n in AFTER_S[tt]:
                    item_in(pe, n)
            with pe.Fori(0, CH - 1) as c:
                body(c, False)
                head(c + 1)
            body(CH - 1, True)

            def scores(c, tt):
                if tt >= 2:
                    pe.wait_ge(exp_done, c * TT + tt - 1)
                three(sc[tt % 2][:], [(qk_hi[:, 0, rows(tt)], qk_lo[:, 0, rows(tt)], qk_hi[:, 1, :], qk_lo[:, 1, :])])\
                    .then_inc(score_done, 1)

            def spread(c, kt):
                if kt < 2:
                    pe.wait_ge(proj_read, c * 4 + kt + 1)
                else:
                    pe.wait_ge(prod_done, c * KE + kt - 1)
                nc.tensor.matmul(pj[kt % 2][:], pick[:, kt, :], combT[:], start=True, stop=True).then_inc(spread_done, 1)

            def base(c, tt, k0=0, k1=KD):
                if k0 == 0:
                    pe.wait_ge(y_read, c * TT + TT + tt - 1)
                three(y[tt % 2][:], [(xT_hi[:, k, rows(tt)], xT_lo[:, k, rows(tt)], base_hi[:, k, :], base_lo[:, k, :])
                                     for k in range(k0, k1)], start=(k0 == 0), stop=False)

            def lora(c, tt, k0, k1):
                pe.wait_ge(prod_split, c * KE + k1)
                last = three(y[tt % 2][:], [(prod_hi[:, k, rows(tt)], prod_lo[:, k, rows(tt)], b_hi[:, k, :], b_lo[:, k, :])
                                            for k in range(k0, k1)], start=False, stop=(k1 == KE))
                if k1 == KE:
                    last.then_inc(y_done, 1)

            def end_half(c, i):
                tt, cols = TT - 1, half(i)
                pe.wait_ge(y_read, c * TT + TT + tt - 1 + i)
                three(y[1 - i][:, cols],
                      [(xT_hi[:, k, rows(tt)], xT_lo[:, k, rows(tt)], base_hi[:, k, cols], base_lo[:, k, cols])
                       for k in range(KD)]
                      + [(prod_hi[:, k, rows(tt)], prod_lo[:, k, rows(tt)], b_hi[:, k, cols], b_lo[:, k, cols])
                         for k in range(KE)]).then_inc(end_y_done, 1)

            def probs_transpose(c, kt):
                if kt == 0:
                    pe.wait_ge(exp_done, c * TT + TT)
                elif kt == 1:
                    pe.wait_ge(v_split, c + 1)
                else:
                    pe.wait_ge(p_split, c * TT + kt - 1)
                for tt in range(TT):
                    last = nc.tensor.transpose(tr[kt % 2][:, rows(tt)], probs[:, tt, rows(kt)], ident[:])
                last.then_inc(p_tr, 1)

            def project(c, tt):
                if tt == 0:
                    pe.wait_ge(wo_split, 2)
                if tt >= 2:
                    pe.wait_ge(o_read, c * TT + TT + tt - 1)
                three(sc[(tt + 1) % 2][:], [(at_hi[:, rows(tt)], at_lo[:, rows(tt)], wo_hi[:], wo_lo[:])]).then_inc(o_done, 1)

            def chunk(c, is_first, last_chunk):
                g = c + CH
                pe.wait_ge(xT_done, g * TT + TT)
                three(pj[0][0:R + E, :], [(a_hi[:, k, :], a_lo[:, k, :], xT_hi[:, k, :], xT_lo[:, k, :])
                                          for k in range(KD)]).then_inc(proj_done, 1)
                if is_first:
                    pe.wait_ge(w_direct_lo, 1)
                for j, dst in enumerate((pj[1], sc[0], sc[1])):
                    if j == 1:
                        pe.wait_ge(o_read, c * TT + TT)
                    d = slice(j * DH, (j + 1) * DH)
                    parts = [(wqkv_hi[:, k, d], wqkv_lo[:, k, d], xT_hi[:, k, :], xT_lo[:, k, :]) for k in range(KD)]
                    if j == 0:
                        three(dst[:], parts[0:1], stop=False)
                        pe.wait_ge(logits_out, c + 1)
                        three(dst[:], parts[1:2], start=False, stop=False)
                        for tt in range(TT):
                            routed = nc.tensor.transpose(tr[0][:, tt * E:(tt + 1) * E], logits[:, rows(tt)],
                                                         ident[R:R + E, R:R + E])
                        routed.then_inc(route_in, 1)
                        three(dst[:], parts[2:], start=False).then_inc(proj_done, 1)
                    elif j == 1:
                        three(dst[:], parts).then_inc(proj_done, 1)
                    else:
                        three(dst[:], parts[0:2], stop=False)
                        pe.wait_ge(route_step, c * NROUTE + NROUTE)
                        three(dst[:], parts[2:3], start=False, stop=False)
                        for tt in range(TT):
                            combined = nc.tensor.transpose(tr[0][0:2 * Q, rows(tt)], comb[:, tt, :], ident[:])
                        combined.then_inc(comb_tr, 1)
                        three(dst[:], parts[3:], start=False).then_inc(proj_done, 1)
                    if is_first:
                        if j == 0:
                            pe.wait_ge(silu_done, CH * TT)
                            pe.wait_ge(pick_ready, 4)
                        for n in LATE_GROUPS[j]:
                            item_in(pe, n)
                pe.wait_ge(qk_split, c * 2 + 2)
                scores(c, 0)
                if is_first:
                    for n in LATE_GROUPS[3]:
                        item_in(pe, n)
                if is_first:
                    pe.wait_ge(w_lo, len(items))
                base(c, 0, 0, 1)
                pe.wait_ge(proj_read, c * 4 + 4)
                for tt in range(TT):
                    last = nc.tensor.transpose(tr[1][:, rows(tt)], qkv[:, 2, rows(tt)], ident[:])
                last.then_inc(v_tr, 1)
                pe.wait_ge(comb_split, c + 1)
                spread(c, 0)
                spread(c, 1)
                scores(c, 1)
                base(c, 0, 1, KD)
                spread(c, 2)
                spread(c, 3)
                scores(c, 2)
                scores(c, 3)
                base(c, 1)
                spread(c, 4)
                spread(c, 5)
                probs_transpose(c, 0)
                probs_transpose(c, 1)
                lora(c, 0, 0, 4)
                probs_transpose(c, 2)
                probs_transpose(c, 3)
                spread(c, 6)
                spread(c, 7)
                lora(c, 1, 0, 4)
                pe.wait_ge(p_split, c * TT + TT)
                three(sc[0][:], [(v_hi[:, k, :], v_lo[:, k, :], pT_hi[:, k, :], pT_lo[:, k, :])
                                 for k in range(TT)]).then_inc(pv_done, 1)
                lora(c, 0, 4, 8)
                pe.wait_ge(a_split, c + 1)
                project(c, 0)
                lora(c, 1, 4, 8)
                project(c, 1)
                base(c, 2)
                lora(c, 2, 0, 8)
                project(c, 2)
                if last_chunk:
                    end_half(c, 0)
                    project(c, 3)
                    end_half(c, 1)
                else:
                    base(c, 3)
                    transpose_rows(pe, g + 1, 0)
                    transpose_rows(pe, g + 1, 1)
                    lora(c, 3, 0, 4)
                    for tt in (2, 3):
                        pe.wait_ge(xT_done, (g + 1) * TT + tt - 1)
                        transpose_rows(pe, g + 1, tt)
                    lora(c, 3, 4, 8)
                    project(c, 3)

            chunk(0, True, False)
            with pe.Fori(1, CH - 1) as c:
                chunk(c, False, False)
            chunk(CH - 1, False, True)


_INS = ["L0_attn_data", "L0_attn_mask", "L0_attn_weight", "L0_attn_bias", "L0_ffn_c1_w", "L0_ffn_c2_w", "L0_ffn_w1",
        "L0_ffn_w2t", "L1_attn_Wqkv", "L1_attn_bqkv", "L1_attn_Wo", "L1_attn_bo", "L1_ffn_base_w", "L1_ffn_base_b",
        "L1_ffn_A", "L1_ffn_B", "L1_ffn_router_w"]


def kernel(**inputs):
    import concourse.bacc as bacc
    from concourse.bass_utils import run_bass_kernel_spmd

    nc = bacc.Bacc("TRN2", target_bir_lowering=False, num_devices=1, dynamic_dma_scratch_size=1024)
    arrays, args = {}, []
    for name in _INS:
        a = np.ascontiguousarray(inputs[name])
        arrays[f"in_{name}"] = a
        args.append(nc.dram_tensor(f"in_{name}", a.shape, mybir.dt.from_np(a.dtype), kind="ExternalInput").ap())
    shape = arrays["in_L0_attn_data"].shape
    args.append(nc.dram_tensor("out", shape, F32, kind="ExternalOutput").ap())
    block_mask_ffn_then_attention_lora_kernel(nc, *args)
    r = run_bass_kernel_spmd(nc, [arrays], core_ids=[0])
    return r.results[0]["out"]
```
